# Optimizing a Trainium2 kernel written in Bass

```python
import numpy as np
import jax
import jax.numpy as jnp

def _softmax(x, axis=-1):
    return jax.nn.softmax(x, axis=axis)

def _gelu(x):
    return jax.nn.gelu(x, approximate=True)

def _silu(x):
    return jax.nn.silu(x)

def _sigmoid(x):
    return jax.nn.sigmoid(x)

def _layernorm(x, axis=-1, eps=1e-05):
    m = jnp.mean(x, axis=axis, keepdims=True)
    v = jnp.var(x, axis=axis, keepdims=True)
    return (x - m) / jnp.sqrt(v + eps)

def _scatter_add(tgt, idx, src, axis=0):
    return tgt.at[idx].add(src)

def _segment_sum(src, seg, n):
    return jax.ops.segment_sum(src, seg, n)
kernel_name = 'mk_decoder_postln_d2_seqx_r8_2e2f58'

def setup_inputs(seed: int=0):
    np.random.seed(seed)
    _w = jnp.asarray

    def _rec_inputs():
        import jax
        import jax.numpy as jnp
        _rk = jax.random.key(seed)
        x = 7.22e-05 + 1 * jax.random.normal(jax.random.fold_in(_rk, 1), (16, 128, 128), jnp.float32)
        _lenS = 128 - jax.random.randint(jax.random.fold_in(_rk, 7), (16,), 0, max(1, 128 // 4) + 1, jnp.int32)
        _lenS2 = 120 - jax.random.randint(jax.random.fold_in(_rk, 8), (16,), 0, max(1, 120 // 4) + 1, jnp.int32)
        _ctx_1024P = jax.random.normal(jax.random.fold_in(_rk, 11), (16, 16, 128), jnp.float32)
        _ctx_1024c = jax.random.dirichlet(jax.random.fold_in(_rk, 511), 0.3 * jnp.ones((16,), jnp.float32), (16, 120))
        _ctx_1024t = jnp.einsum('bsk,bkd->bsd', _ctx_1024c, _ctx_1024P)
        _ctx_1024t = _ctx_1024t * jax.lax.rsqrt(jnp.mean(jnp.square(_ctx_1024t)) + 1e-12) * 0.953939
        ctx_1024 = 4.13588e-05 + 0.999923 * (_ctx_1024t + 0.3 * jax.random.normal(jax.random.fold_in(_rk, 611), (16, 120, 128), jnp.float32))
        _validS = jnp.arange(128)[None, :] < _lenS[:, None]
        _validS2 = jnp.arange(120)[None, :] < _lenS2[:, None]
        _causal = jnp.tril(jnp.ones((128, 128), dtype=bool))
        mask_Bx1xSxS2_ik1 = jnp.where(jnp.broadcast_to(_validS2[:, None, None, :], (16, 1, 128, 120)), 1, 0).astype(jnp.int32)
        return (x, ctx_1024, mask_Bx1xSxS2_ik1)
    x, ctx_1024, mask_Bx1xSxS2_ik1 = _rec_inputs()

    def _L0_attn_setup():
        import jax, jax.numpy as jnp
        from jax import lax
        import numpy as np
        D_MODEL, D_STATE, D_CONV, EXPAND = (128, 16, 4, 2)
        D_INNER = EXPAND * D_MODEL
        BATCH, SEQLEN = (2, 256)

        def _ssm_scan(x_conv, dt, A, B_ssm):
            Bb, L, Di = x_conv.shape
            h0 = jnp.zeros((Bb, Di, A.shape[1]), x_conv.dtype)

            def step(h, inp):
                x_t, dt_t, B_t = inp
                dA = jnp.exp(dt_t[:, :, None] * A)
                h = h * dA + dt_t[:, :, None] * B_t[:, None, :] * x_t[:, :, None]
                return (h, h.sum(axis=2))
            xs = (x_conv.transpose(1, 0, 2), dt.transpose(1, 0, 2), B_ssm.transpose(1, 0, 2))
            _, ys = lax.scan(step, h0, xs)
            return ys.transpose(1, 0, 2)
        key = jax.random.key(seed)
        ks = jax.random.split(key, 8)
        sc = lambda k, shape, s: jax.random.normal(k, shape, jnp.float32) * s
        return {'x': jax.random.normal(ks[0], (BATCH, SEQLEN, D_MODEL), jnp.float32), 'W_in': sc(ks[1], (D_MODEL, 2 * D_INNER), 0.02), 'conv_w': sc(ks[2], (D_INNER, D_CONV), 0.1), 'conv_b': jnp.zeros((D_INNER,), jnp.float32), 'W_x': sc(ks[3], (D_INNER, 2 * D_STATE), 0.02), 'W_dt': sc(ks[4], (D_STATE, D_INNER), 0.1), 'b_dt': jnp.zeros((D_INNER,), jnp.float32), 'A_log': jnp.log(jax.random.uniform(ks[5], (D_INNER, D_STATE), jnp.float32, 0.0001, 1.0)), 'D': jnp.ones((D_INNER,), jnp.float32), 'W_out': sc(ks[6], (D_INNER, D_MODEL), 0.02)}
    _L0_attn_all = _L0_attn_setup()
    _L0_attn_in = {k: v for k, v in _L0_attn_all.items() if k in ('W_in', 'conv_w', 'conv_b', 'W_x', 'W_dt', 'b_dt', 'A_log', 'D', 'W_out')}
    del _L0_attn_all

    def _L0_xattn_setup():
        import jax, jax.numpy as jnp
        import numpy as np
        D_MODEL = 128
        N_HEAD = 16
        B, S = (4, 256)

        def _split_heads(x):
            b, l, d = x.shape
            return x.reshape(b, l, N_HEAD, d // N_HEAD).transpose(0, 2, 1, 3)
        key = jax.random.key(seed)
        ks = jax.random.split(key, 13)
        s = 1.0 / np.sqrt(D_MODEL)
        inp = {'query': jax.random.normal(ks[0], (B, S, D_MODEL), jnp.float32), 'key_': jax.random.normal(ks[1], (B, S, D_MODEL), jnp.float32), 'value': jax.random.normal(ks[2], (B, S, D_MODEL), jnp.float32), 'mask': jax.random.randint(ks[3], (B, 1, S, S), 0, 2, jnp.int32), 'Wq': jax.random.normal(ks[4], (D_MODEL, D_MODEL), jnp.float32) * s, 'bq': jax.random.normal(ks[5], (D_MODEL,), jnp.float32) * 0.02, 'Wk': jax.random.normal(ks[6], (D_MODEL, D_MODEL), jnp.float32) * s, 'bk': jax.random.normal(ks[7], (D_MODEL,), jnp.float32) * 0.02, 'Wv': jax.random.normal(ks[8], (D_MODEL, D_MODEL), jnp.float32) * s, 'bv': jax.random.normal(ks[9], (D_MODEL,), jnp.float32) * 0.02, 'Wo': jax.random.normal(ks[10], (D_MODEL, D_MODEL), jnp.float32) * s, 'bo': jax.random.normal(ks[11], (D_MODEL,), jnp.float32) * 0.02}
        return inp
    _L0_xattn_all = _L0_xattn_setup()
    _L0_xattn_in = {k: v for k, v in _L0_xattn_all.items() if k in ('Wq', 'bq', 'Wk', 'bk', 'Wv', 'bv', 'Wo', 'bo')}
    del _L0_xattn_all

    def _L0_ffn_setup():
        import jax, jax.numpy as jnp
        import numpy as np
        T, Z, D_DIM = (8, 256, 128)
        N_EXP, P_SLOT, H = (64, 32, 128)
        LN_EPS = 1e-05
        key = jax.random.key(seed)
        k = jax.random.split(key, 5)
        s = 0.02
        return {'x': jax.random.normal(k[0], (T, Z, D_DIM), dtype=jnp.float32), 'phi_w': jax.random.normal(k[1], (N_EXP * P_SLOT, D_DIM), dtype=jnp.float32) * s, 'phi_b': jax.random.normal(k[2], (N_EXP * P_SLOT,), dtype=jnp.float32) * s, 'expert_w': jax.random.normal(k[3], (N_EXP, D_DIM, H), dtype=jnp.float32) * s, 'expert_b': jax.random.normal(k[4], (N_EXP, H), dtype=jnp.float32) * s}
    _L0_ffn_all = _L0_ffn_setup()
    _L0_ffn_in = {k: v for k, v in _L0_ffn_all.items() if k in ('phi_w', 'phi_b', 'expert_w', 'expert_b')}
    del _L0_ffn_all

    def _L1_attn_setup():
        import jax, jax.numpy as jnp
        import numpy as np
        B, T, C, NH = (8, 128, 128, 16)
        HD = C // NH
        EPS = 1e-05

        def _decay_mask(nh, t, dtype):
            gamma = 1.0 - 2.0 ** (-5.0 - jnp.arange(nh, dtype=jnp.float32))
            idx = jnp.arange(t)
            diff = idx[:, None] - idx[None, :]
            mask = diff >= 0
            pow_ = gamma[:, None, None] ** jnp.where(mask, diff, 0).astype(jnp.float32)
            return (jnp.where(mask[None], pow_, 0.0).astype(dtype), gamma.astype(dtype))

        def _reference_tuple_inner(x, past_kv, W_qkv, gn_weight, gn_bias):
            b, t, c = x.shape
            nh = gn_weight.shape[0]
            hd = c // nh
            qkv = x @ W_qkv
            q, k, v = jnp.split(qkv, 3, axis=2)
            split_heads = lambda u: u.reshape(b, t, nh, hd).transpose(0, 2, 1, 3)
            q, k, v = (split_heads(q), split_heads(k), split_heads(v))
            decay, gamma = _decay_mask(nh, t, x.dtype)
            ret = jnp.einsum('bhtd,bhsd->bhts', q, k) * decay
            inner = jnp.einsum('bhts,bhsd->bhtd', ret, v)
            inner_decay = float(nh * hd)
            cross = jnp.einsum('bhtd,hde->bhte', q, past_kv) * inner_decay
            r = inner + cross
            current_kv = gamma[:, None, None] * past_kv + jnp.einsum('bhtd,bhte->bhde', k, v)
            current_kv = current_kv.mean(axis=0)
            y = r.transpose(0, 1, 3, 2)
            mu = y.mean(axis=(1, 2, 3), keepdims=True)
            var = y.var(axis=(1, 2, 3), keepdims=True)
            yn = (y - mu) * jax.lax.rsqrt(var + EPS)
            yn = yn * gn_weight[None, :, None, None] + gn_bias[None, :, None, None]
            out = yn.transpose(0, 3, 1, 2).reshape(b, t, c)
            return (out, current_kv)
        key = jax.random.key(seed)
        k1, k2, k3 = jax.random.split(key, 3)
        x = jax.random.normal(k1, (B, T, C), dtype=jnp.float32)
        past_kv = jax.random.normal(k2, (NH, HD, HD), dtype=jnp.float32) * 0.1
        W_qkv = jax.random.normal(k3, (C, 3 * C), dtype=jnp.float32) * 0.02
        gn_weight = jnp.ones((NH,), dtype=jnp.float32)
        gn_bias = jnp.zeros((NH,), dtype=jnp.float32)
        return {'x': x, 'past_kv': past_kv, 'W_qkv': W_qkv, 'gn_weight': gn_weight, 'gn_bias': gn_bias}
    _L1_attn_all = _L1_attn_setup()
    _L1_attn_in = {k: v for k, v in _L1_attn_all.items() if k in ('past_kv', 'W_qkv', 'gn_weight', 'gn_bias')}
    del _L1_attn_all

    def _L1_xattn_setup():
        import jax, jax.numpy as jnp
        import numpy as np
        DIM = 128
        NUM_HEADS = 16
        HEAD_DIM = DIM // NUM_HEADS
        SCALE = HEAD_DIM ** (-0.5)
        key = jax.random.key(seed)
        ks = jax.random.split(key, 11)
        B, SQ, SKV = (2, 256, 256)
        s = DIM ** (-0.5)
        return {'q': jax.random.normal(ks[0], (B, SQ, DIM), jnp.float32), 'k': jax.random.normal(ks[1], (B, SKV, DIM), jnp.float32), 'v': jax.random.normal(ks[2], (B, SKV, DIM), jnp.float32), 'Wq': jax.random.normal(ks[3], (DIM, DIM), jnp.float32) * s, 'bq': jnp.zeros((DIM,), jnp.float32), 'Wk': jax.random.normal(ks[4], (DIM, DIM), jnp.float32) * s, 'bk': jnp.zeros((DIM,), jnp.float32), 'Wv': jax.random.normal(ks[5], (DIM, DIM), jnp.float32) * s, 'bv': jnp.zeros((DIM,), jnp.float32), 'Wo': jax.random.normal(ks[6], (DIM, DIM), jnp.float32) * s, 'bo': jnp.zeros((DIM,), jnp.float32)}
    _L1_xattn_all = _L1_xattn_setup()
    _L1_xattn_in = {k: v for k, v in _L1_xattn_all.items() if k in ('Wq', 'bq', 'Wk', 'bk', 'Wv', 'bv', 'Wo', 'bo')}
    del _L1_xattn_all

    def _L1_ffn_setup():
        import jax, jax.numpy as jnp
        import numpy as np
        BITS = 8
        LORA_RANK = 16
        LORA_ALPHA = 32
        SCALING = LORA_ALPHA / LORA_RANK

        def fake_quant_weight(w, bits=BITS):
            qmax = 2.0 ** (bits - 1) - 1
            scale = jnp.max(jnp.abs(w)) / qmax
            wq = jnp.clip(jnp.round(w / scale), -qmax - 1, qmax) * scale
            return w + jax.lax.stop_gradient(wq - w)

        def qat_lora_linear(x, W, b, A, B):
            Wq = fake_quant_weight(W)
            base = jnp.einsum('bsi,oi->bso', x, Wq) + b
            lora = jnp.einsum('bsr,or->bso', jnp.einsum('bsi,ri->bsr', x, A), B)
            return base + SCALING * lora
        key = jax.random.key(seed)
        ks = jax.random.split(key, 9)
        d, f = (128, 512)
        s_in = 1.0 / np.sqrt(d)
        s_ff = 1.0 / np.sqrt(f)
        return {'hidden_states': jax.random.normal(ks[0], (4, 256, d), jnp.float32), 'W_fc': jax.random.normal(ks[1], (f, d), jnp.float32) * s_in, 'b_fc': jnp.zeros((f,), jnp.float32), 'A_fc': jax.random.normal(ks[2], (LORA_RANK, d), jnp.float32) * s_in, 'B_fc': jnp.zeros((f, LORA_RANK), jnp.float32), 'W_proj': jax.random.normal(ks[3], (d, f), jnp.float32) * s_ff, 'b_proj': jnp.zeros((d,), jnp.float32), 'A_proj': jax.random.normal(ks[4], (LORA_RANK, f), jnp.float32) * s_ff, 'B_proj': jnp.zeros((d, LORA_RANK), jnp.float32)}
    _L1_ffn_all = _L1_ffn_setup()
    _L1_ffn_in = {k: v for k, v in _L1_ffn_all.items() if k in ('W_fc', 'b_fc', 'A_fc', 'B_fc', 'W_proj', 'b_proj', 'A_proj', 'B_proj')}
    del _L1_ffn_all
    return {'x': x, 'ctx_1024': ctx_1024, 'mask_Bx1xSxS2_ik1': mask_Bx1xSxS2_ik1, 'L0_attn_W_in': _L0_attn_in['W_in'], 'L0_attn_conv_w': _L0_attn_in['conv_w'], 'L0_attn_conv_b': _L0_attn_in['conv_b'], 'L0_attn_W_x': _L0_attn_in['W_x'], 'L0_attn_W_dt': _L0_attn_in['W_dt'], 'L0_attn_b_dt': _L0_attn_in['b_dt'], 'L0_attn_A_log': _L0_attn_in['A_log'], 'L0_attn_D': _L0_attn_in['D'], 'L0_attn_W_out': _L0_attn_in['W_out'], 'L0_xattn_Wq': _L0_xattn_in['Wq'], 'L0_xattn_bq': _L0_xattn_in['bq'], 'L0_xattn_Wk': _L0_xattn_in['Wk'], 'L0_xattn_bk': _L0_xattn_in['bk'], 'L0_xattn_Wv': _L0_xattn_in['Wv'], 'L0_xattn_bv': _L0_xattn_in['bv'], 'L0_xattn_Wo': _L0_xattn_in['Wo'], 'L0_xattn_bo': _L0_xattn_in['bo'], 'L0_ffn_phi_w': _L0_ffn_in['phi_w'], 'L0_ffn_phi_b': _L0_ffn_in['phi_b'], 'L0_ffn_expert_w': _L0_ffn_in['expert_w'], 'L0_ffn_expert_b': _L0_ffn_in['expert_b'], 'L1_attn_past_kv': _L1_attn_in['past_kv'], 'L1_attn_W_qkv': _L1_attn_in['W_qkv'], 'L1_attn_gn_weight': _L1_attn_in['gn_weight'], 'L1_attn_gn_bias': _L1_attn_in['gn_bias'], 'L1_xattn_Wq': _L1_xattn_in['Wq'], 'L1_xattn_bq': _L1_xattn_in['bq'], 'L1_xattn_Wk': _L1_xattn_in['Wk'], 'L1_xattn_bk': _L1_xattn_in['bk'], 'L1_xattn_Wv': _L1_xattn_in['Wv'], 'L1_xattn_bv': _L1_xattn_in['bv'], 'L1_xattn_Wo': _L1_xattn_in['Wo'], 'L1_xattn_bo': _L1_xattn_in['bo'], 'L1_ffn_W_fc': _L1_ffn_in['W_fc'], 'L1_ffn_b_fc': _L1_ffn_in['b_fc'], 'L1_ffn_A_fc': _L1_ffn_in['A_fc'], 'L1_ffn_B_fc': _L1_ffn_in['B_fc'], 'L1_ffn_W_proj': _L1_ffn_in['W_proj'], 'L1_ffn_b_proj': _L1_ffn_in['b_proj'], 'L1_ffn_A_proj': _L1_ffn_in['A_proj'], 'L1_ffn_B_proj': _L1_ffn_in['B_proj']}

def reference(x, ctx_1024, mask_Bx1xSxS2_ik1, L0_attn_W_in, L0_attn_conv_w, L0_attn_conv_b, L0_attn_W_x, L0_attn_W_dt, L0_attn_b_dt, L0_attn_A_log, L0_attn_D, L0_attn_W_out, L0_xattn_Wq, L0_xattn_bq, L0_xattn_Wk, L0_xattn_bk, L0_xattn_Wv, L0_xattn_bv, L0_xattn_Wo, L0_xattn_bo, L0_ffn_phi_w, L0_ffn_phi_b, L0_ffn_expert_w, L0_ffn_expert_b, L1_attn_past_kv, L1_attn_W_qkv, L1_attn_gn_weight, L1_attn_gn_bias, L1_xattn_Wq, L1_xattn_bq, L1_xattn_Wk, L1_xattn_bk, L1_xattn_Wv, L1_xattn_bv, L1_xattn_Wo, L1_xattn_bo, L1_ffn_W_fc, L1_ffn_b_fc, L1_ffn_A_fc, L1_ffn_B_fc, L1_ffn_W_proj, L1_ffn_b_proj, L1_ffn_A_proj, L1_ffn_B_proj):
    import jax
    import jax.numpy as jnp

    def _L0_attn_ref(x, W_in, conv_w, conv_b, W_x, W_dt, b_dt, A_log, D, W_out):
        import jax, jax.numpy as jnp
        from jax import lax
        import numpy as np
        D_MODEL, D_STATE, D_CONV, EXPAND = (128, 16, 4, 2)
        D_INNER = EXPAND * D_MODEL
        BATCH, SEQLEN = (2, 256)

        def _ssm_scan(x_conv, dt, A, B_ssm):
            Bb, L, Di = x_conv.shape
            h0 = jnp.zeros((Bb, Di, A.shape[1]), x_conv.dtype)

            def step(h, inp):
                x_t, dt_t, B_t = inp
                dA = jnp.exp(dt_t[:, :, None] * A)
                h = h * dA + dt_t[:, :, None] * B_t[:, None, :] * x_t[:, :, None]
                return (h, h.sum(axis=2))
            xs = (x_conv.transpose(1, 0, 2), dt.transpose(1, 0, 2), B_ssm.transpose(1, 0, 2))
            _, ys = lax.scan(step, h0, xs)
            return ys.transpose(1, 0, 2)
        Bb, L, _ = x.shape
        xz = x @ W_in
        x_proj, z = jnp.split(xz, 2, axis=-1)
        xc = lax.conv_general_dilated(x_proj.transpose(0, 2, 1), conv_w[:, None, :], window_strides=(1,), padding=[(D_CONV - 1, 0)], feature_group_count=D_INNER, dimension_numbers=('NCH', 'OIH', 'NCH'))
        x_conv = jax.nn.silu(xc.transpose(0, 2, 1) + conv_b)
        x_ssm = x_conv @ W_x
        dt_in, B_ssm = jnp.split(x_ssm, 2, axis=-1)
        dt = jax.nn.softplus(dt_in @ W_dt + b_dt)
        A = -jnp.exp(A_log)
        y = _ssm_scan(x_conv, dt, A, B_ssm)
        y = y + x_conv * D[None, None, :]
        y = y * jax.nn.silu(z)
        return y @ W_out

    def _L0_xattn_ref(query, key_, value, mask, Wq, bq, Wk, bk, Wv, bv, Wo, bo):
        import jax, jax.numpy as jnp
        import numpy as np
        D_MODEL = 128
        N_HEAD = 16
        B, S = (4, 256)

        def _split_heads(x):
            b, l, d = x.shape
            return x.reshape(b, l, N_HEAD, d // N_HEAD).transpose(0, 2, 1, 3)
        q = _split_heads(query @ Wq + bq)
        k = _split_heads(key_ @ Wk + bk)
        v = _split_heads(value @ Wv + bv)
        dh = q.shape[-1]
        score = jnp.einsum('bhqd,bhkd->bhqk', q, k) / jnp.sqrt(jnp.float32(dh))
        score = jnp.where(mask == 0, jnp.float32(-1000000000.0), score)
        attn = jax.nn.softmax(score, axis=-1)
        out = jnp.einsum('bhqk,bhkd->bhqd', attn, v)
        b, h, l, d = out.shape
        out = out.transpose(0, 2, 1, 3).reshape(b, l, h * d)
        return out @ Wo + bo

    def _L0_ffn_ref(x, phi_w, phi_b, expert_w, expert_b):
        import jax, jax.numpy as jnp
        import numpy as np
        T, Z, D_DIM = (8, 256, 128)
        N_EXP, P_SLOT, H = (64, 32, 128)
        LN_EPS = 1e-05
        t, z, d = x.shape
        n = expert_w.shape[0]
        p = phi_w.shape[0] // n
        logits = (jnp.einsum('tzd,ed->tze', x, phi_w) + phi_b).reshape(t, z, n, p)
        D = jax.nn.softmax(logits, axis=3)
        C = jax.nn.softmax(logits, axis=2)
        X_tilde = jnp.einsum('tznp,tzd->npd', D, x)
        X_tilde = jnp.clip(X_tilde, -33000.0, 65000.0)
        mu = jnp.mean(X_tilde, axis=-1, keepdims=True)
        var = jnp.mean(jnp.square(X_tilde - mu), axis=-1, keepdims=True)
        X_tilde = (X_tilde - mu) * jax.lax.rsqrt(var + LN_EPS)
        X_tilde = jnp.tanh(X_tilde)
        Y_tilde = jnp.einsum('npd,ndH->npH', X_tilde, expert_w) + expert_b[:, None, :]
        Y = jnp.einsum('tznp,npH->tzH', C, Y_tilde)
        return Y

    def _L1_attn_ref(x, past_kv, W_qkv, gn_weight, gn_bias):
        import jax, jax.numpy as jnp
        import numpy as np
        B, T, C, NH = (8, 128, 128, 16)
        HD = C // NH
        EPS = 1e-05

        def _decay_mask(nh, t, dtype):
            gamma = 1.0 - 2.0 ** (-5.0 - jnp.arange(nh, dtype=jnp.float32))
            idx = jnp.arange(t)
            diff = idx[:, None] - idx[None, :]
            mask = diff >= 0
            pow_ = gamma[:, None, None] ** jnp.where(mask, diff, 0).astype(jnp.float32)
            return (jnp.where(mask[None], pow_, 0.0).astype(dtype), gamma.astype(dtype))

        def _reference_tuple_inner(x, past_kv, W_qkv, gn_weight, gn_bias):
            b, t, c = x.shape
            nh = gn_weight.shape[0]
            hd = c // nh
            qkv = x @ W_qkv
            q, k, v = jnp.split(qkv, 3, axis=2)
            split_heads = lambda u: u.reshape(b, t, nh, hd).transpose(0, 2, 1, 3)
            q, k, v = (split_heads(q), split_heads(k), split_heads(v))
            decay, gamma = _decay_mask(nh, t, x.dtype)
            ret = jnp.einsum('bhtd,bhsd->bhts', q, k) * decay
            inner = jnp.einsum('bhts,bhsd->bhtd', ret, v)
            inner_decay = float(nh * hd)
            cross = jnp.einsum('bhtd,hde->bhte', q, past_kv) * inner_decay
            r = inner + cross
            current_kv = gamma[:, None, None] * past_kv + jnp.einsum('bhtd,bhte->bhde', k, v)
            current_kv = current_kv.mean(axis=0)
            y = r.transpose(0, 1, 3, 2)
            mu = y.mean(axis=(1, 2, 3), keepdims=True)
            var = y.var(axis=(1, 2, 3), keepdims=True)
            yn = (y - mu) * jax.lax.rsqrt(var + EPS)
            yn = yn * gn_weight[None, :, None, None] + gn_bias[None, :, None, None]
            out = yn.transpose(0, 3, 1, 2).reshape(b, t, c)
            return (out, current_kv)
        return _reference_tuple_inner(x, past_kv, W_qkv, gn_weight, gn_bias)[0]

    def _L1_xattn_ref(q, k, v, Wq, bq, Wk, bk, Wv, bv, Wo, bo):
        import jax, jax.numpy as jnp
        import numpy as np
        DIM = 128
        NUM_HEADS = 16
        HEAD_DIM = DIM // NUM_HEADS
        SCALE = HEAD_DIM ** (-0.5)
        B, SQ, _ = q.shape
        SKV = k.shape[1]
        qh = (q @ Wq.T + bq).reshape(B, SQ, NUM_HEADS, HEAD_DIM).transpose(0, 2, 1, 3)
        kh = (k @ Wk.T + bk).reshape(B, SKV, NUM_HEADS, HEAD_DIM).transpose(0, 2, 1, 3)
        vh = (v @ Wv.T + bv).reshape(B, SKV, NUM_HEADS, HEAD_DIM).transpose(0, 2, 1, 3)
        attn = jax.nn.softmax(jnp.einsum('bhqd,bhkd->bhqk', qh, kh) * SCALE, axis=-1)
        out = jnp.einsum('bhqk,bhkd->bhqd', attn, vh)
        out = out.transpose(0, 2, 1, 3).reshape(B, SQ, DIM)
        return out @ Wo.T + bo

    def _L1_ffn_ref(hidden_states, W_fc, b_fc, A_fc, B_fc, W_proj, b_proj, A_proj, B_proj):
        import jax, jax.numpy as jnp
        import numpy as np
        BITS = 8
        LORA_RANK = 16
        LORA_ALPHA = 32
        SCALING = LORA_ALPHA / LORA_RANK

        def fake_quant_weight(w, bits=BITS):
            qmax = 2.0 ** (bits - 1) - 1
            scale = jnp.max(jnp.abs(w)) / qmax
            wq = jnp.clip(jnp.round(w / scale), -qmax - 1, qmax) * scale
            return w + jax.lax.stop_gradient(wq - w)

        def qat_lora_linear(x, W, b, A, B):
            Wq = fake_quant_weight(W)
            base = jnp.einsum('bsi,oi->bso', x, Wq) + b
            lora = jnp.einsum('bsr,or->bso', jnp.einsum('bsi,ri->bsr', x, A), B)
            return base + SCALING * lora
        h = qat_lora_linear(hidden_states, W_fc, b_fc, A_fc, B_fc)
        h = jax.nn.gelu(h, approximate=False)
        h = qat_lora_linear(h, W_proj, b_proj, A_proj, B_proj)
        return h
    x = _layernorm(x + _L0_attn_ref(x, L0_attn_W_in, L0_attn_conv_w, L0_attn_conv_b, L0_attn_W_x, L0_attn_W_dt, L0_attn_b_dt, L0_attn_A_log, L0_attn_D, L0_attn_W_out), axis=-1)
    x = _layernorm(x + _L0_xattn_ref(x, ctx_1024, ctx_1024, mask_Bx1xSxS2_ik1, L0_xattn_Wq, L0_xattn_bq, L0_xattn_Wk, L0_xattn_bk, L0_xattn_Wv, L0_xattn_bv, L0_xattn_Wo, L0_xattn_bo), axis=-1)
    x = _layernorm(x + _L0_ffn_ref(x, L0_ffn_phi_w, L0_ffn_phi_b, L0_ffn_expert_w, L0_ffn_expert_b), axis=-1)
    x = _layernorm(x + _L1_attn_ref(x, L1_attn_past_kv, L1_attn_W_qkv, L1_attn_gn_weight, L1_attn_gn_bias), axis=-1)
    x = _layernorm(x + _L1_xattn_ref(x, ctx_1024, ctx_1024, L1_xattn_Wq, L1_xattn_bq, L1_xattn_Wk, L1_xattn_bk, L1_xattn_Wv, L1_xattn_bv, L1_xattn_Wo, L1_xattn_bo), axis=-1)
    x = _layernorm(x + _L1_ffn_ref(x, L1_ffn_W_fc, L1_ffn_b_fc, L1_ffn_A_fc, L1_ffn_B_fc, L1_ffn_W_proj, L1_ffn_b_proj, L1_ffn_A_proj, L1_ffn_B_proj), axis=-1)
    return x

_drawn_inputs = setup_inputs


def setup_inputs(seed=0):
    import zlib

    import numpy as np

    out = dict(_drawn_inputs(seed))
    spreads = {'L0_attn_conv_b': (0.0, 0.8),
     'L0_attn_b_dt': (0.0, 0.8),
     'L0_attn_D': (1.0, 0.6),
     'L1_attn_gn_weight': (1.0, 0.2),
     'L1_attn_gn_bias': (0.0, 0.1),
     'L1_xattn_bq': (0.0, 0.399),
     'L1_xattn_bk': (0.0, 2.0),
     'L1_xattn_bv': (0.0, 0.1),
     'L1_xattn_bo': (0.0, 0.1),
     'L1_ffn_b_fc': (0.0, 0.1),
     'L1_ffn_B_fc': (0.0, 0.1),
     'L1_ffn_b_proj': (0.0, 0.1),
     'L1_ffn_B_proj': (0.0, 0.1)}
    factors = {'L0_attn_W_in': 8.0,
     'L0_attn_conv_w': 8.0,
     'L0_attn_W_x': 8.0,
     'L0_attn_W_dt': 8.0,
     'L0_attn_A_log': 8.0,
     'L0_attn_W_out': 8.0,
     'L0_xattn_bq': 5.305,
     'L0_xattn_bk': 64.0,
     'L0_ffn_phi_b': 31.662,
     'L0_ffn_phi_w': 2.768}
    for name, (base, spread) in spreads.items():
        noise = np.random.default_rng([zlib.crc32(name.encode()), seed]).standard_normal(out[name].shape)
        drawn = base * np.exp(spread * noise) if base else spread * noise
        out[name] = jnp.asarray(drawn.astype(out[name].dtype))
    for name, factor in factors.items():
        out[name] = (out[name] * factor).astype(out[name].dtype)
    return out
```

```python
from contextlib import ExitStack

import numpy as np
import concourse.bass as bass
from concourse import mybir
from concourse.bass import ds

F32 = mybir.dt.float32
BF16 = mybir.dt.bfloat16
I32 = mybir.dt.int32
ALU = mybir.AluOpType
ACT = mybir.ActivationFunctionType
AX = mybir.AxisListType

NT, P, D = 16, 128, 128
NH, HD = 16, 8
SK = 120
G, GT = 4, 4
GW = GT * P
NS, DI, NC = 16, 256, 2
KC = 4
NE, PS = 64, 32
E = NE * PS
EC_N = E // P
FF, R = 512, 16
FC = FF // P
LN_EPS = 1e-5
MASKED = -float(2 ** 30)
QMAX = 127.0
ROUND = 12582912.0

LN_MAMBA, LN_XA0, LN_MOE, LN_RET, LN_XA1, LN_FFN, LN_END = 0, 4, 20, 36, 52, 68, 72
OUT_DMAS = G


def build(nc, a, out):
    ctx = ExitStack()
    with ctx:
        def sb(name, shape, dt=F32):
            return ctx.enter_context(nc.sbuf_tensor(name, shape, dt))

        def sem(name):
            return ctx.enter_context(nc.semaphore(name))

        bank = ctx.enter_context(nc.psum_tensor("bank", [P, 8, 512], F32))
        arena = sb("arena", [P, NT * E])
        X = sb("X", [P, NT, D])
        slots = sb("slots", [P, 2, E])
        slotsT = sb("slotsT", [P, 2, EC_N, P])
        phiT = sb("phiT", [P, E])
        phib = sb("phib", [P, E], BF16)
        Yt = sb("Yt", [P, EC_N, D])
        ident = sb("ident", [P, P])
        identb = sb("identb", [P, P], BF16)
        onesb = sb("onesb", [P, P], BF16)
        mean_w = sb("mean_w", [P, P])
        hmask = sb("hmask", [P, NH])
        selcol = sb("selcol", [P, NS])
        mhalf = sb("mhalf", [P, 16])
        xs = sb("xs", [P, 2, D])
        xr = sb("xr", [P, 2, D])
        xT = sb("xT", [P, 2, 256])
        lny = sb("lny", [P, 2, GT, D])
        lnst = sb("lnst", [P, 2, GT, 6])
        lnmv = sb("lnmv", [P, 2, GT, 2])
        lnve = sb("lnve", [P, 2, GT])
        lnrs = sb("lnrs", [P, 2, GT])
        wa = sb("wa", [P, 2, 4, D])
        ab = sb("ab", [P, 2, 3])
        abr = sb("abr", [P, 2, D])
        sel9 = sb("sel9", [P, 4 * (HD + 1)])
        sel8 = sb("sel8", [P, 4 * HD])
        rC = sb("rC", [P, NT, PS])
        mxn = sb("mxn", [P, 2, NE])
        mxp = sb("mxp", [P, 2, PS])
        rD = sb("rD", [P, 2, NE])
        sm = sb("sm", [P, 96])

        off = [0]

        def carve(cols, dt=F32):
            v = arena[:, off[0]:off[0] + cols]
            off[0] += cols
            assert off[0] <= NT * E
            return v if dt == F32 else v.bitcast(dt)

        xconv = carve(NC * NT * P).rearrange("p (c n) -> p c n", c=NC)
        sz = carve(NC * NT * P).rearrange("p (c n) -> p c n", c=NC)
        dt_all = carve(NC * NT * P).rearrange("p (c n) -> p c n", c=NC)
        dtx_all = carve(NC * NT * P).rearrange("p (c n) -> p c n", c=NC)
        dA = carve(2 * 4 * GW).rearrange("p (b n) -> p b n", b=2)
        dBx = carve(2 * 4 * GW).rearrange("p (b n) -> p b n", b=2)
        Bs = carve(NT * P // 2, BF16)
        sel = carve(NS * P // 2, BF16).rearrange("p (n m) -> p n m", n=NS)
        w_in = carve(2 * DI)
        cwb = carve(DI * KC).rearrange("p (d k) -> p d k", k=KC)
        wk = carve(KC * DI).rearrange("p (k d) -> p k d", k=KC)
        wx = carve(NC * P).rearrange("p (c n) -> p c n", c=NC)
        wdt = carve(DI)
        wout = carve(NC * D).rearrange("p (c n) -> p c n", c=NC)
        alog = carve(NC * NS).rearrange("p (c n) -> p c n", c=NC)
        Am = carve(NC * NS).rearrange("p (c n) -> p c n", c=NC)
        convb, bdt, Dv = carve(NC), carve(NC), carve(NC)
        xTp = carve(2 * GT * (P + KC - 1)).rearrange("p (b j n) -> p b j n", b=2, j=GT)
        top_a2 = off[0]
        xs4 = carve(2 * GW).rearrange("p (b j n) -> p b j n", b=2, j=GT)
        off[0] = top_a2
        bres = carve(GW)
        dtin = carve(GW)
        sp_l = dA[:, 0, :].rearrange("p (c n) -> p c n", c=4)[:, 0:2, :]
        sp_r = dA[:, 1, :].rearrange("p (c n) -> p c n", c=4)[:, 0:2, :]
        yTm = slotsT[:, 0, 0:2 * GT, :].rearrange("p (c j) n -> p c (j n)", c=NC)

        off[0] = 0
        ctxb = carve(2 * P).rearrange("p (b n) -> p b n", b=2)
        maskb = carve(2 * SK).rearrange("p (b n) -> p b n", b=2).bitcast(I32)
        mbias = carve(SK, BF16).rearrange("p (b n) -> p b n", b=2)
        mflag = carve(2 * SK).rearrange("p (b n) -> p b n", b=2)
        allm = carve(2).rearrange("p (b n) -> p b n", b=2)
        escale = carve(2).rearrange("p (b n) -> p b n", b=2)
        qT = carve(2 * P).rearrange("p (b n) -> p b n", b=2)
        kT = carve(2 * SK).rearrange("p (b n) -> p b n", b=2)
        kexp = carve(2 * NH * SK).rearrange("p (b h n) -> p b h n", b=2, h=NH)
        vaug = carve(2 * NH * 32).rearrange("p (b h n) -> p b h n", b=2, h=NH)
        poT = carve(2 * 4 * P).rearrange("p (b r n) -> p b r n", b=2, r=4)
        nmx = carve(2 * NH).rearrange("p (b h n) -> p b h n", b=2, n=1)
        sc = carve(2 * NH * SK).rearrange("p (b h n) -> p b h n", b=2, h=NH)
        pT = carve(2 * NH * P).rearrange("p (b h n) -> p b h n", b=2, h=NH)
        rden = carve(2 * NH).rearrange("p (b h n) -> p b h n", b=2, n=1)
        on = carve(2 * D).rearrange("p (b n) -> p b n", b=2)
        oT = carve(2 * D).rearrange("p (b n) -> p b n", b=2)
        wraw = carve(4 * D).rearrange("p (i n) -> p i n", i=4)
        top_attn = off[0]

        EC = arena[:, :].rearrange("p (t e) -> p t e", t=NT)
        xtl = slotsT[:, 0, :, :]
        xtlT = slotsT[:, 1, :, :]
        phir = slotsT[:, 0, :, :]
        lgc = slotsT[:, :, :, :].rearrange("p b c n -> p b (c n)")
        fold = Yt[:, 0:12, :].rearrange("p c n -> p (c n)")
        moe_y = slots[:, 0, :].rearrange("p (c n) -> p c n", c=EC_N)
        ew = slots[:, 1, :].rearrange("p (b e n) -> p b e n", b=4, e=4)

        off[0] = 0
        decay = carve(NH * P).rearrange("p (h n) -> p h n", h=NH)
        qexp = carve(2 * NH * P).rearrange("p (b h n) -> p b h n", b=2, h=NH)
        rd = carve(2 * NH * P).rearrange("p (b h n) -> p b h n", b=2, h=NH)
        qkT = carve(2 * 2 * D).rearrange("p (b n) -> p b n", b=2)
        vpad = carve(2 * NH * 32).rearrange("p (b h n) -> p b h n", b=2, h=NH)
        rpo = carve(2 * 4 * P).rearrange("p (b r n) -> p b r n", b=2, r=4)
        crs = carve(2 * D).rearrange("p (b n) -> p b n", b=2)
        gr = carve(2 * D).rearrange("p (b n) -> p b n", b=2)
        gst = carve(2 * 6).rearrange("p (b n) -> p b n", b=2)
        gmv = carve(2 * 2).rearrange("p (b n) -> p b n", b=2)
        gsc = carve(2 * 4).rearrange("p (b n) -> p b n", b=2)
        gt1 = carve(2 * D).rearrange("p (b n) -> p b n", b=2)
        gt2 = carve(2 * D).rearrange("p (b n) -> p b n", b=2)
        wqkv = carve(3 * D)
        kvl = carve(HD)
        kvbd = carve(D)
        gnw, gnb = carve(NH), carve(NH)

        assert max(off[0], top_attn) <= 17920
        off[0] = 17920
        wf1 = carve(FC * D).rearrange("p (c n) -> p c n", c=FC)
        wf2 = carve(FF)
        tq1 = carve(FF)
        tq2 = carve(FF)
        bfcr = carve(FC)
        bpr = carve(D)
        afc = carve(D)
        bfc = carve(FC * R).rearrange("p (c r) -> p c r", c=FC)
        apj = carve(FF)
        bpj = carve(R)
        bT = carve(FF + D)
        w1T = carve(FF)
        w2T = carve(FC * D).rearrange("p (c n) -> p c n", c=FC)
        amx = carve(8)
        fs4 = carve(2 * GW).rearrange("p (b j n) -> p b j n", b=2, j=GT)
        fr4 = carve(2 * GW).rearrange("p (b j n) -> p b j n", b=2, j=GT)
        fxT = carve(2 * GW).rearrange("p (b n) -> p b n", b=2)
        hT = carve(2 * FC * GW).rearrange("p (b c n) -> p b c n", b=2, c=FC)

        ld_const, ld_x, ld_mamba, ld_attn, ld_moe = (sem(f"ld_{n}") for n in ("const", "x", "mamba", "attn", "moe"))
        ld_eb, ld_ret, ld_xa1, ld_ffn = (sem(f"ld_{n}") for n in ("eb", "ret", "xa1", "ffn"))
        ld_xs4 = [sem("ld_xs4_0"), sem("ld_xs4_1")]
        ld_ctx = [sem("ld_ctx0"), sem("ld_ctx1")]
        ld_mask = [sem("ld_mask0"), sem("ld_mask1")]
        ld_ew = [sem(f"ld_ew{i}") for i in range(4)]
        stored = sem("stored")
        set_v, set_p, set_w = sem("set_v"), sem("set_p"), sem("set_w")
        lny_s, lnst_s, lnmv_s, lnve_s, lnrs_s, x_ready = (sem(n) for n in ("ln_y", "ln_stats", "ln_mv", "ln_ve", "ln_rstd", "x_ready"))
        m_tr, m_xT, m_mm, m_silu, m_silz = (sem(f"m_{n}") for n in ("tr", "xT", "mm", "silu", "silz"))
        m_wx, m_dtin, m_bs, m_dtp, m_abs, m_ln1, m_relu, m_dt, m_dtx = (sem(f"m_{n}") for n in ("wx", "dtin", "bs", "dtp", "abs", "ln", "relu", "dt", "dtx"))
        m_dA, m_dz, m_B, m_dBx, m_h, m_sum, m_y, m_o, m_A = (sem(f"m_{n}") for n in ("dA", "dz", "B", "dBx", "h", "sum", "y", "o", "A"))
        m_e, m_split = sem("m_e"), sem("m_split")
        a_xs, a_xr, a_tr, a_xT, a_qkv, a_qk, a_v, a_kexp, a_mb, a_esc = (sem(f"a_{n}") for n in ("xs", "xr", "tr", "xT", "qkv", "qk", "v", "kexp", "mb", "esc"))
        a_s, a_max, a_sub, a_exp, a_pt, a_ptc, a_pv, a_po, a_sel = (sem(f"a_{n}") for n in ("s", "max", "sub", "exp", "pt", "ptc", "pv", "po", "sel"))
        a_rden, a_on, a_ot, a_otc, a_out, a_flag, a_bvo, a_bias = (sem(f"a_{n}") for n in ("rden", "on", "ot", "otc", "out", "flag", "bvo", "bias"))
        e_xs, e_tr, e_xT, e_log, e_lgc, e_mxp, e_mxn, e_subD, e_subC, e_expD, e_expC = (sem(f"e_{n}") for n in ("xs", "tr", "xT", "log", "lgc", "mxp", "mxn", "subD", "subC", "expD", "expC"))
        e_sum, e_sumC, e_rD, e_rC, e_Dn, e_xt, e_pb, e_phi, e_fold1, e_fold2 = (sem(f"e_{n}") for n in ("sum", "sumC", "rD", "rC", "Dn", "xt", "pb", "phi", "fold1", "fold2"))
        y_clip, y_mv, y_ve, y_n, y_tanh, y_tr, y_trc, y_mm, y_out = (sem(f"y_{n}") for n in ("clip", "mv", "ve", "n", "tanh", "tr", "trc", "mm", "out"))
        c_n, c_tr, c_ca, c_cv, c_y = (sem(f"c_{n}") for n in ("n", "tr", "ca", "cv", "y"))
        r_xs, r_xr, r_tr, r_xT, r_qkv, r_cr, r_qk, r_crc, r_v, r_qe, r_s, r_rd, r_pv, r_po, r_sel = (sem(f"r_{n}") for n in ("xs", "xr", "tr", "xT", "qkv", "cr", "qk", "crc", "v", "qe", "s", "rd", "pv", "po", "sel"))
        r_r, r_st, r_mv, r_m1, r_d, r_v2, r_m2, r_ve, r_rs, r_t1, r_t2 = (sem(f"r_{n}") for n in ("r", "st", "mv", "m1", "d", "v2", "m2", "ve", "rs", "t1", "t2"))
        f_w, f_wp, f_wt, f_wc, f_xs, f_tr, f_xT, f_h, f_g, f_o = (sem(f"f_{n}") for n in ("w", "wp", "wt", "wc", "xs", "tr", "xT", "h", "g", "o"))

        passed_dve, passed_act, passed_pool = sem("passed_dve"), sem("passed_act"), sem("passed_pool")
        block = ctx.enter_context(nc.Block())

        def tile(buf, t, k=1):
            v = buf[:, ds(t, k), :]
            return v.rearrange("p a n -> p (a n)") if k == 1 else v

        def pairs(eng, n, step, last_peeled=False):
            step(0, 0)
            step(0, 1)
            end = n // 2 - (1 if last_peeled else 0)
            if end > 1:
                with eng.Fori(1, end) as j:
                    step(j, 0)
                    step(j, 1)
            if last_peeled:
                step(n // 2 - 1, 0)
                step(n // 2 - 1, 1)

        def steps(eng, step):
            for t in range(-2, 2):
                step(t // 2, t % 2)
            with eng.Fori(1, NT // 2 - 2) as j:
                step(j, 0)
                step(j, 1)
            for t in range(NT - 4, NT + 1):
                step(t // 2, t % 2)

        def ok(t):
            return not isinstance(t, int) or 0 <= t < NT

        def bc(ap, n):
            return ap.to_broadcast([ap.shape[0], ap.shape[1], n])

        def mid(ap, n):
            return ap.unsqueeze(1).to_broadcast([ap.shape[0], n, ap.shape[1]])

        def num(x):
            return isinstance(x, int)

        @block.sync
        def _(sp):
            for dst, name in ((ident, "c_ident"), (hmask, "c_hmask"), (selcol, "c_selcol"), (sel9, "c_sel9"), (sel8, "c_sel8")):
                sp.dma_start(dst[:, :], a[name]).then_inc(ld_const, 16)
            xt = a["x"].rearrange("t p d -> p t d")
            sp.dma_start(xs4[:, 0, :, :], xt[:, 0:GT, :]).then_inc(ld_xs4[0], 16)
            sp.dma_start(xs4[:, 1, :, :], xt[:, GT:2 * GT, :]).then_inc(ld_xs4[1], 16)
            sp.dma_start(w_in, a["L0_attn_W_in"]).then_inc(ld_mamba, 16)
            sp.dma_start(cwb.rearrange("p d k -> p (d k)"),
                         a["L0_attn_conv_w"].rearrange("d k -> (d k)").partition_broadcast(P)).then_inc(ld_mamba, 16)
            for dst, name in ((convb, "L0_attn_conv_b"), (bdt, "L0_attn_b_dt"), (Dv, "L0_attn_D")):
                sp.dma_start(dst, a[name].rearrange("(c p) -> p c", p=P), allow_slow_non_contiguous=True).then_inc(ld_mamba, 16)
            sp.dma_start(alog, a["L0_attn_A_log"].rearrange("(c p) n -> p c n", p=P)).then_inc(ld_mamba, 16)
            sp.dma_start(wout, a["L0_attn_W_out"].rearrange("(c p) n -> p c n", p=P)).then_inc(ld_mamba, 16)
            sp.dma_start(wdt[0:R, :], a["L0_attn_W_dt"]).then_inc(ld_mamba, 16)
            sp.wait_ge(set_w, 1)
            wxr = a["L0_attn_W_x"].rearrange("(c p) n -> p c n", p=P)
            for q in range(4):
                sp.dma_start(wx[:, :, 32 * q:32 * q + NS],
                             wxr[:, :, (0 if q == 0 else NS):(NS if q == 0 else 2 * NS)]).then_inc(ld_mamba, 16)
            sp.dma_start(X[:, :, :], xt).then_inc(ld_x, 16)
            for g in range(2, G):
                sp.wait_ge(m_tr, g - 1)
                sp.dma_start(xs4[:, g % 2, :, :], xt[:, GT * g:GT * g + GT, :]).then_inc(ld_xs4[g % 2], 16)
            for i, n in enumerate(("Wq", "Wk", "Wv", "Wo")):
                sp.dma_start(wa[:, 0, i, :], a["L0_xattn_" + n]).then_inc(ld_attn, 16)
            for lay in range(2):
                for i, n in enumerate(("bq", "bk", "bv")):
                    sp.dma_start(ab[:, lay, i:i + 1], a[f"L{lay}_xattn_{n}"].rearrange("(p o) -> p o", o=1)).then_inc(ld_attn, 16)
                sp.dma_start(abr[:, lay, :], a[f"L{lay}_xattn_bo"].partition_broadcast(P)).then_inc(ld_attn, 16)
            sp.wait_ge(x_ready, LN_XA0)
            sp.dma_start(phir, a["L0_ffn_phi_w"].rearrange("(c p) d -> p c d", p=P)).then_inc(ld_moe, 16)
            sp.wait_ge(set_w, 2)
            pb_row = a["L0_ffn_phi_b"].rearrange("(o n) -> o n", o=1)
            for row in (0, 64, 96):
                sp.dma_start(slots[row:row + 1, 0, :], pb_row).then_inc(ld_moe, 16)

            def attn_loads(lay):
                def step(j, par):
                    t, u = 2 * j + par, NT * lay + 2 * j + par
                    if not (num(u) and u < 2):
                        sp.wait_ge(a_tr, u - 1)
                    sp.dma_start(ctxb[0:SK, par, :], tile(a["ctx_1024"].rearrange("t s d -> s t d"), t)).then_inc(ld_ctx[par], 16)
                    if lay == 0:
                        if not (num(t) and t < 2):
                            sp.wait_ge(a_mb, t - 1)
                        sp.dma_start(maskb[:, par, :], tile(a["mask_Bx1xSxS2_ik1"].rearrange("t o q k -> q t (o k)"), t)).then_inc(ld_mask[par], 16)
                pairs(sp, NT, step)

            attn_loads(0)
            sp.wait_ge(e_xt, NT)
            ebv = a["L0_ffn_expert_b"].rearrange("(c n) h -> n c h", n=4)
            for n in range(4):
                sp.dma_start(moe_y[32 * n:32 * n + 32, :, :], ebv[n].partition_broadcast(PS)).then_inc(ld_eb, 16)
            ewv = a["L0_ffn_expert_w"].rearrange("(c n) d h -> c d n h", n=4)
            for c in range(EC_N):
                if c >= 4:
                    sp.wait_ge(y_mm, c - 3)
                sp.dma_start(ew[:, c % 4, :, :], ewv[c]).then_inc(ld_ew[c % 4], 16)
            sp.wait_ge(x_ready, LN_RET)
            sp.dma_start(decay, a["c_decay"]).then_inc(ld_ret, 16)
            sp.dma_start(wqkv, a["L1_attn_W_qkv"]).then_inc(ld_ret, 16)
            sp.dma_start(kvl, a["L1_attn_past_kv"].rearrange("h d e -> (h d) e")).then_inc(ld_ret, 16)
            sp.dma_start(gnw, a["L1_attn_gn_weight"].partition_broadcast(P)).then_inc(ld_ret, 16)
            sp.dma_start(gnb, a["L1_attn_gn_bias"].partition_broadcast(P)).then_inc(ld_ret, 16)
            sp.dma_start(wf1, a["L1_ffn_W_fc"].rearrange("(c p) d -> p c d", p=P)).then_inc(ld_ffn, 16)
            sp.dma_start(wf2, a["L1_ffn_W_proj"]).then_inc(ld_ffn, 16)
            sp.dma_start(bfcr, a["L1_ffn_b_fc"].rearrange("(c p) -> p c", p=P), allow_slow_non_contiguous=True).then_inc(ld_ffn, 16)
            sp.dma_start(bpr, a["L1_ffn_b_proj"].partition_broadcast(P)).then_inc(ld_ffn, 16)
            sp.dma_start(afc[0:R, :], a["L1_ffn_A_fc"]).then_inc(ld_ffn, 16)
            sp.dma_start(bfc, a["L1_ffn_B_fc"].rearrange("(c p) r -> p c r", p=P)).then_inc(ld_ffn, 16)
            sp.dma_start(apj[0:R, :], a["L1_ffn_A_proj"]).then_inc(ld_ffn, 16)
            sp.dma_start(bpj, a["L1_ffn_B_proj"]).then_inc(ld_ffn, 16)
            sp.wait_ge(x_ready, LN_XA1)
            for i, n in enumerate(("Wq", "Wk", "Wv", "Wo")):
                sp.dma_start(wraw[:, i, :], a["L1_xattn_" + n]).then_inc(ld_xa1, 16)
            attn_loads(1)
            ot = out.rearrange("t p d -> p t d")
            for g in range(G):
                sp.wait_ge(x_ready, LN_FFN + g + 1)
                sp.dma_start(ot[:, GT * g:GT * g + GT, :], X[:, GT * g:GT * g + GT, :]).then_inc(stored, 16)
            sp.wait_ge(stored, 16 * OUT_DMAS)

        @block.gpsimd
        def _(pool):
            def ln_rstd(e, par, k):
                pool.wait_ge(lnmv_s, e + 1)
                pool.sem_inc(passed_pool, 1)
                pool.tensor_scalar(lnve[:, par, 0:k], lnmv[:, par, 0:k, 1], LN_EPS, None, ALU.add).then_inc(lnve_s, 1)
                pool.wait_ge(lnve_s, e + 1)
                pool.tensor_tensor(lnrs[:, par, 0:k], lnve[:, par, 0:k], mhalf[:, 0:k], ALU.pow).then_inc(lnrs_s, 1)

            pool.memset(mhalf[:, :], -0.5)
            pool.memset(mean_w[:, :], 1.0 / P)
            pool.memset(onesb[:, :], 1.0).then_inc(set_p, 1)
            pool.wait_ge(set_p, 1)

            def scan_reset(g, k):
                kk = 8 * g + k
                pool.wait_ge(m_dA, kk + 1)
                v = dA[:, k % 2, :].rearrange("p (s n) -> p s n", n=P)[:, :, 0:1]
                pool.memset(v, 0.0).then_inc(m_dz, 1)

            def mamba_group(g, par):
                for k in range(8):
                    scan_reset(g, k)
                    if k == 1 and not (num(g) and g == 0):
                        ln_rstd(g - 1, 1 - par, GT)
            pairs(pool, G, lambda j, par: mamba_group(2 * j + par, par))
            ln_rstd(G - 1, (G - 1) % 2, GT)

            def attention(lay, ln0):
                def stage(t, par):
                    u = NT * lay + t
                    if not (num(u) and u < 2):
                        pool.wait_ge(a_tr, u - 1)
                    pool.tensor_copy(xs[:, par, :], tile(X, t)).then_inc(a_xs, 1)

                pool.wait_ge(x_ready, ln0)
                stage(0, 0)
                pool.wait_ge(a_bias, lay + 1)

                def step(j, par):
                    t = 2 * j + par
                    u = NT * lay + t
                    if ok(t + 3):
                        stage(t + 3, 1 - par)
                    if ok(t):
                        if not (num(t) and t < 2):
                            pool.wait_ge(lny_s, ln0 + t - 1)
                        pool.tensor_tensor(xr[:, par, :], tile(X, t), abr[:, lay, :], ALU.add).then_inc(a_xr, 1)
                    if ok(t + 2):
                        pool.wait_ge(a_qk, u + 3)
                        if not (num(u) and u < 0):
                            pool.wait_ge(a_s, 2 * u + 2)
                        pool.tensor_tensor(kexp[:, par, :, :], mid(kT[:, par, :], NH), bc(hmask[:, :].unsqueeze(2), SK),
                                           ALU.mult).then_inc(a_kexp, 1)
                    if ok(t - 1):
                        ln_rstd(ln0 + t - 1, 1 - par, 1)
                steps(pool, step)

            pool.wait_ge(ld_const, 80)
            attention(0, LN_XA0)

            pool.wait_ge(x_ready, LN_MOE)

            def moe_stage(t, par):
                if not (num(t) and t < 2):
                    pool.wait_ge(e_tr, t - 1)
                pool.tensor_copy(xs[:, par, :], tile(X, t)).then_inc(e_xs, 1)

            moe_stage(0, 0)

            def step(j, par):
                t = 2 * j + par
                if ok(t + 3):
                    moe_stage(t + 3, 1 - par)
                if ok(t):
                    pool.wait_ge(e_expC, t + 1)
                    if not (num(t) and t == 0):
                        pool.wait_ge(e_sumC, t)
                    c = tile(EC, t)
                    pool.tensor_tensor(fold[:, 0:E // 2], c[:, 0:E // 2], c[:, E // 2:E], ALU.add).then_inc(e_fold1, 1)
                    pool.wait_ge(e_fold1, t + 1)
                    pool.tensor_tensor(fold[:, E // 2:3 * E // 4], fold[:, 0:E // 4], fold[:, E // 4:E // 2], ALU.add).then_inc(e_fold2, 1)
                    pool.wait_ge(e_rD, t + 1)
                    v = slots[:, par, :].rearrange("p (n s) -> p n s", s=PS)
                    pool.tensor_tensor(v, v, bc(rD[:, par, :].unsqueeze(2), PS), ALU.mult).then_inc(e_Dn, 1)
                if ok(t + 1):
                    pool.wait_ge(e_mxp, t + 2)
                    pool.tensor_tensor(tile(EC, t + 1).rearrange("p (n s) -> p n s", s=PS), lgc[:, 1 - par, :].rearrange("p (n s) -> p n s", s=PS),
                                       mid(mxp[:, 1 - par, :], NE), ALU.subtract).then_inc(e_subC, 1)
            steps(pool, step)

            pool.wait_ge(y_mv, 2)
            pool.tensor_scalar(sm[:, 64:80], sm[:, 32:64].rearrange("p (c n) -> p c n", n=2)[:, :, 1], LN_EPS, None, ALU.add).then_inc(y_ve, 1)
            pool.wait_ge(y_ve, 1)
            pool.tensor_tensor(sm[:, 80:96], sm[:, 64:80], mhalf[:, :], ALU.pow).then_inc(y_ve, 1)

            pool.wait_ge(y_out, 1)

            def step(j, par):
                t = 2 * j + par
                if ok(t + 2):
                    if not (num(t) and t < 0):
                        pool.wait_ge(c_tr, 4 * t + 4)
                    pool.tensor_tensor(slots[:, par, :].rearrange("p (n s) -> p n s", s=PS),
                                       tile(EC, t + 2).rearrange("p (n s) -> p n s", s=PS),
                                       mid(tile(rC, t + 2), NE), ALU.mult).then_inc(c_n, 1)
                if ok(t):
                    ln_rstd(LN_MOE + t, par, 1)
            steps(pool, step)

            pool.wait_ge(x_ready, LN_RET)
            pool.wait_ge(ld_ret, 16 * 5)

            def stage(t, par):
                if not (num(t) and t < 2):
                    pool.wait_ge(r_tr, t - 1)
                pool.tensor_copy(xs[:, par, :], tile(X, t)).then_inc(r_xs, 1)

            stage(0, 0)

            def step(j, par):
                t = 2 * j + par
                if ok(t + 3):
                    stage(t + 3, 1 - par)
                if ok(t):
                    if not (num(t) and t < 2):
                        pool.wait_ge(lny_s, LN_RET + t - 1)
                    pool.tensor_tensor(xr[:, par, :].rearrange("p (h e) -> p h e", e=HD), tile(X, t).rearrange("p (h e) -> p h e", e=HD),
                                       bc(gnb.unsqueeze(2), HD), ALU.add).then_inc(r_xr, 1)
                if ok(t + 2):
                    pool.wait_ge(r_qk, t + 3)
                    if not (num(t) and t < 0):
                        pool.wait_ge(r_s, 2 * t + 2)
                    pool.tensor_tensor(qexp[:, par, :, :], mid(qkT[:, par, 0:P], NH), bc(hmask[:, :].unsqueeze(2), P),
                                       ALU.mult).then_inc(r_qe, 1)
                if ok(t - 1):
                    pool.wait_ge(r_ve, t)
                    pool.tensor_tensor(gsc[:, 1 - par, 3:4], gsc[:, 1 - par, 2:3], mhalf[:, 0:1], ALU.pow).then_inc(r_rs, 1)
                    ln_rstd(LN_RET + t - 1, 1 - par, 1)
            steps(pool, step)

            attention(1, LN_XA1)

            pool.wait_ge(f_w, 1)
            pool.partition_all_reduce(amx[:, 2:4], amx[:, 0:2], P, bass.bass_isa.ReduceOp.max).then_inc(f_w, 1)
            pool.wait_ge(x_ready, LN_FFN)

            def step(j, par):
                g = 2 * j + par
                if not (num(g) and g < 2):
                    pool.wait_ge(f_tr, g - 1)
                    pool.wait_ge(lny_s, LN_FFN + g - 1)
                pool.tensor_copy(fs4[:, par, :, :], tile(X, GT * g, GT)).then_inc(f_xs, 1)
                pool.tensor_tensor(fr4[:, par, :, :], tile(X, GT * g, GT), mid(bpr, GT), ALU.add).then_inc(f_xs, 1)
                if not (num(g) and g == 0):
                    ln_rstd(LN_FFN + g - 1, 1 - par, GT)
            pairs(pool, G, step)
            ln_rstd(LN_FFN + G - 1, 1, GT)

        @block.scalar
        def _(act):
            A = act.activation
            def conv_silu(g, par):
                act.wait_ge(m_tr, g + 1)
                if g >= 2:
                    act.wait_ge(m_mm, 4 * (g - 1))
                act.copy(xTp[:, par, :, KC - 1:], bank[:, 0, :].rearrange("p (j n) -> p j n", j=GT)).then_inc(m_xT, 1)
                for c in range(NC):
                    act.wait_ge(m_mm, 4 * g + c + 1)
                    A(xconv[:, c, GW * g:GW * g + GW], bank[:, 1 + c, :], ACT.Silu, bias=convb[:, c:c + 1]).then_inc(m_silu, 1)
                for c in range(NC):
                    act.wait_ge(m_mm, 4 * g + 2 + c + 1)
                    A(sz[:, c, GW * g:GW * g + GW], bank[:, 3 + c, :], ACT.Silu).then_inc(m_silz, 1)
            act.wait_ge(ld_mamba, 16 * 12)
            act.wait_ge(set_v, 1)
            for g in range(G):
                conv_silu(g, g % 2)
            act.preload_act_table_set("natural_log_exp_and_others")
            A(Am, alog, ACT.Exp).then_inc(m_A, 1)

            def steps_soft(g):
                act.wait_ge(m_wx, g + 1)
                if g >= 1:
                    act.wait_ge(m_dtp, 2 * g)
                act.copy(dtin[0:R, :], bank[0:R, 7, :]).then_inc(m_dtin, 1)
                if g >= 1:
                    act.wait_ge(m_dt, g)
                for c in range(NC):
                    act.wait_ge(m_dtp, 2 * g + c + 1)
                    A(sp_l[:, c, :], bank[:, 5 + c, :], ACT.Abs, bias=bdt[:, c:c + 1]).then_inc(m_abs, 1)
                act.wait_ge(m_abs, 2 * g + 2)
                A(sp_l, sp_l, ACT.Exp, scale=-1.0).then_inc(m_e, 1)
                act.wait_ge(m_e, g + 1)
                A(sp_l, sp_l, ACT.Ln, bias=1.0).then_inc(m_ln1, 1)
            for g in range(G):
                steps_soft(g)

            act.wait_ge(m_A, 2)
            act.wait_ge(m_dtx, G)

            def decays(g):
                for k in range(8):
                    kk, c, q = 8 * g + k, k // 4, k % 4
                    if not (num(kk) and kk < 2):
                        act.wait_ge(m_h, kk - 1)
                        act.sem_inc(passed_act, 1)
                    for i in range(4):
                        s = 4 * q + i
                        ins = A(dA[:, k % 2, GW * i:GW * i + GW], dt_all[:, c, ds(GW * g, GW)], ACT.Exp, scale=Am[:, c, s:s + 1])
                    ins.then_inc(m_dA, 1)
            decays(0)
            with act.Fori(1, G) as g:
                decays(g)

            def attention(lay, ln0):
                def probs(u, par, hf):
                    act.wait_ge(a_sub, 2 * u + hf + 1)
                    v = sc[:, par, 8 * hf:8 * hf + 8, :]
                    if lay == 0:
                        if hf == 0:
                            act.wait_ge(a_esc, u + 1)
                        A(v, v, ACT.Exp, scale=escale[:, par, :]).then_inc(a_exp, 1)
                    else:
                        A(v, v, ACT.Exp, scale=HD ** -0.5).then_inc(a_exp, 1)

                def probsT(u, par, r):
                    act.wait_ge(a_pt, 4 * u + r + 1)
                    if r == 0 and not (num(u) and u < 2):
                        act.wait_ge(a_pv, u - 1)
                    act.copy(pT[0:SK, par, 4 * r:4 * r + 4, :], bank[0:SK, 6 + r % 2, :].rearrange("p (h n) -> p h n", h=4)).then_inc(a_ptc, 1)

                def step(j, par):
                    t = 2 * j + par
                    u = NT * lay + t
                    if ok(t + 2):
                        act.wait_ge(a_tr, u + 3)
                        if not (num(u) and u < 0):
                            act.wait_ge(a_qkv, u + 1)
                        act.copy(xT[:, par, 0:P + SK], bank[:, 1, 0:P + SK]).then_inc(a_xT, 1)
                    if ok(t + 1):
                        probs(u + 1, 1 - par, 0)
                    if ok(t - 1):
                        act.wait_ge(a_ot, u)
                        if not (num(u) and u < 3):
                            act.wait_ge(a_out, u - 2)
                        act.copy(oT[:, 1 - par, :], bank[:, 1, 0:D]).then_inc(a_otc, 1)
                    if ok(t + 2):
                        act.wait_ge(a_qkv, u + 3)
                        if not (num(u) and u < 0):
                            act.wait_ge(a_s, 2 * u + 2)
                            act.wait_ge(a_kexp, u + 1)
                        A(qT[:, par, :], bank[:, 0, 0:P], ACT.Identity, bias=ab[:, lay, 0:1])
                        A(kT[:, par, :], bank[:, 0, P:P + SK], ACT.Identity, bias=ab[:, lay, 1:2]).then_inc(a_qk, 1)
                    if ok(t):
                        probsT(u, par, 0)
                        probsT(u, par, 1)
                    if ok(t + 1):
                        probs(u + 1, 1 - par, 1)
                    if ok(t):
                        probsT(u, par, 2)
                        probsT(u, par, 3)
                        act.wait_ge(a_pv, u + 1)
                        if not (num(u) and u < 2):
                            act.wait_ge(a_sel, u - 1)
                        act.copy(poT[:, par, :, :], bank[:, 6, :].rearrange("p (r n) -> p r n", r=4)).then_inc(a_po, 1)
                steps(act, step)

            act.wait_ge(ld_attn, 16 * 12)
            attention(0, LN_XA0)

            for b in range(4):
                act.wait_ge(set_w, 3 + b)
                act.copy(phiT[:, 512 * b:512 * b + 512], bank[:, b, :]).then_inc(e_phi, 1)

            def step(j, par):
                t = 2 * j + par
                if ok(t + 2):
                    act.wait_ge(e_tr, t + 3)
                    if not (num(t) and t < 0):
                        act.wait_ge(e_log, 4 * t + 4)
                    act.copy(xT[:, par, 0:P], bank[:, 0, 0:P]).then_inc(e_xT, 1)
                if ok(t + 1):
                    act.wait_ge(e_subD, t + 2)
                    A(slots[:, 1 - par, :], slots[:, 1 - par, :], ACT.Exp).then_inc(e_expD, 1)
                if ok(t + 2):
                    if not (num(t) and t < 0):
                        act.wait_ge(e_subD, t + 1)
                        act.wait_ge(e_subC, t + 1)
                    for b in range(4):
                        act.wait_ge(e_log, 4 * (t + 2) + b + 1)
                        act.copy(lgc[:, par, 512 * b:512 * b + 512], bank[:, b, :]).then_inc(e_lgc, 1)
                if ok(t + 1):
                    act.wait_ge(e_subC, t + 2)
                    act.sem_inc(passed_act, 1)
                    A(tile(EC, t + 1), tile(EC, t + 1), ACT.Exp).then_inc(e_expC, 1)
            steps(act, step)

            act.wait_ge(y_n, 1)
            A(xtl, xtl, ACT.Tanh).then_inc(y_tanh, 1)
            for b in range(4):
                act.wait_ge(y_tr, b + 1)
                act.copy(xtlT[:, 4 * b:4 * b + 4, :], bank[:, b, :].rearrange("p (c n) -> p c n", c=4)).then_inc(y_trc, 1)

            act.wait_ge(y_out, 1)

            def step(j, par):
                t = 2 * j + par
                if ok(t + 1):
                    for b in range(2):
                        act.wait_ge(c_tr, 4 * (t + 1) + b + 1)
                        if b == 0 and not (num(t) and t < 1):
                            act.wait_ge(c_y, t)
                        act.copy(slotsT[:, 1 - par, 4 * b:4 * b + 4, :], bank[:, b, :].rearrange("p (c n) -> p c n", c=4)).then_inc(c_ca, 1)
            steps(act, step)

            act.wait_ge(x_ready, LN_RET)

            def step(j, par):
                t = 2 * j + par
                if ok(t + 2):
                    act.wait_ge(r_tr, t + 3)
                    if not (num(t) and t < 0):
                        act.wait_ge(r_qkv, t + 1)
                    act.copy(xT[:, par, 0:P], bank[:, 1, 0:P]).then_inc(r_xT, 1)
                    act.wait_ge(r_qkv, t + 3)
                    if not (num(t) and t < 0):
                        act.wait_ge(r_s, 2 * t + 2)
                        act.wait_ge(r_qe, t + 1)
                        act.wait_ge(r_cr, t + 1)
                    act.copy(qkT[:, par, :], bank[:, 0, 0:2 * P]).then_inc(r_qk, 1)
                if ok(t + 1):
                    act.wait_ge(r_cr, t + 2)
                    if not (num(t) and t < 1):
                        act.wait_ge(r_r, t)
                    act.copy(crs[:, 1 - par, :], bank[:, 0, 3 * P:4 * P]).then_inc(r_crc, 1)
                if ok(t):
                    act.wait_ge(r_pv, t + 1)
                    if not (num(t) and t < 2):
                        act.wait_ge(r_sel, t - 1)
                    act.copy(rpo[:, par, :, :], bank[:, 6, :].rearrange("p (r n) -> p r n", r=4)).then_inc(r_po, 1)
            steps(act, step)

            act.wait_ge(set_w, 7)
            act.copy(wa[:, 1, :, :], bank[:, 0, :].rearrange("p (i n) -> p i n", i=4)).then_inc(set_w, 1)
            act.preload_act_table_set("exp_and_others")
            attention(1, LN_XA1)

            act.wait_ge(f_wt, 1)
            act.copy(bT[0:R, 0:FF], bank[0:R, 0, :]).then_inc(f_wc, 1)
            act.wait_ge(f_wt, 2)
            act.copy(bT[0:R, FF:FF + D], bank[0:R, 1, 0:D]).then_inc(f_wc, 1)
            act.wait_ge(f_wt, 3)
            act.copy(w1T, bank[:, 2, :]).then_inc(f_wc, 1)
            act.wait_ge(f_wt, 4)
            act.copy(w2T, bank[:, 3, :].rearrange("p (c n) -> p c n", c=FC)).then_inc(f_wc, 1)

            def step(j, par):
                g = 2 * j + par
                act.wait_ge(f_tr, g + 1)
                if not (num(g) and g < 2):
                    act.wait_ge(f_h, 4 * (g - 1))
                act.copy(fxT[:, par, :], bank[:, 0, :]).then_inc(f_xT, 1)
                for c in range(FC):
                    act.wait_ge(f_h, 4 * g + c + 1)
                    if c == 0 and not (num(g) and g < 2):
                        act.wait_ge(f_o, g - 1)
                    A(hT[:, par, c, :], bank[:, 2 + c, :], ACT.Gelu, bias=bfcr[:, c:c + 1]).then_inc(f_g, 1)
            pairs(act, G, step)

        @block.vector
        def _(dve):
            TT, TS, STT, RED = dve.tensor_tensor, dve.tensor_scalar, dve.scalar_tensor_tensor, dve.tensor_reduce

            def ln_stats(e, par, acc, res, k):
                y = lny[:, par, 0:k, :] if k > 1 else lny[:, par, 0, :]
                TT(y, acc, res, ALU.add).then_inc(lny_s, 1)
                dve.wait_ge(lny_s, e + 1)
                for i in range(k):
                    ins = dve.bn_stats(lnst[:, par, i, :], lny[:, par, i, :])
                ins.then_inc(lnst_s, 1)
                dve.wait_ge(lnst_s, e + 1)
                dve.sem_inc(passed_dve, 1)
                for i in range(k):
                    ins = dve.bn_aggr(lnmv[:, par, i, :], lnst[:, par, i, :])
                ins.then_inc(lnmv_s, 1)

            def ln_norm(e, par, t, k):
                dve.wait_ge(lnrs_s, e + 1)
                for i in range(k):
                    ins = TS(tile(X, t + i), lny[:, par, i, :], lnmv[:, par, i, 0:1], lnrs[:, par, i:i + 1], ALU.subtract, ALU.mult)
                ins.then_inc(x_ready, 1)

            dve.memset(wx, 0.0).then_inc(set_w, 1)
            dve.memset(xTp[:, :, :, 0:KC - 1], 0.0)
            dve.wait_ge(ld_const, 80)
            dve.tensor_copy(identb[:, :], ident[:, :])
            dve.tensor_copy(sel, bc(selcol[:, :].unsqueeze(2), P))
            dve.wait_ge(ld_mamba, 16 * 12)
            for k in range(KC):
                ins = TT(wk[:, k, :], w_in[:, 0:DI], cwb[:, :, k], ALU.mult)
            ins.then_inc(set_v, 1)
            dve.wait_ge(m_A, 1)
            TS(Am, Am, -1.0, None, ALU.mult).then_inc(m_A, 1)

            for g in range(G):
                gw = slice(GW * g, GW * g + GW)
                n = 3 * g
                dve.wait_ge(m_dtin, g + 1)
                dve.tensor_copy(Bs[:, gw], bank[:, 7, :]).then_inc(m_split, 1)
                dve.wait_ge(m_split, n + 1)
                TT(bres, bank[:, 7, :], Bs[:, gw], ALU.subtract).then_inc(m_split, 1)
                dve.wait_ge(m_split, n + 2)
                dve.tensor_copy(Bs[64:128, gw], bres[64:128, :]).then_inc(m_split, 1)
                dve.wait_ge(m_split, n + 3)
                TT(Bs[96:128, gw], bres[96:128, :], Bs[96:128, gw], ALU.subtract).then_inc(m_bs, 1)
                dve.wait_ge(m_abs, 2 * g + 2)
                for c in range(NC):
                    ins = TS(sp_r[:, c, :], bank[:, 5 + c, :], bdt[:, c:c + 1], 0.0, ALU.add, ALU.max)
                ins.then_inc(m_relu, 1)
                dve.wait_ge(m_relu, g + 1)
                dve.wait_ge(m_ln1, g + 1)
                TT(dt_all[:, :, gw], sp_r, sp_l, ALU.add).then_inc(m_dt, 1)
                dve.wait_ge(m_dt, g + 1)
                TT(dtx_all[:, :, gw], dt_all[:, :, gw], xconv[:, :, gw], ALU.mult).then_inc(m_dtx, 1)
            dve.wait_ge(m_dtx, G)

            def quad(g, k):
                kk, c = 8 * g + k, k // 4
                dve.wait_ge(m_B, kk + 1)
                if not (num(kk) and kk < 2):
                    dve.wait_ge(m_sum, kk - 1)
                TT(dBx[:, k % 2, :].rearrange("p (s n) -> p s n", s=4), bank[:, 0:4, :],
                   mid(dtx_all[:, c, ds(GW * g, GW)], 4), ALU.mult).then_inc(m_dBx, 1)
                dve.wait_ge(m_dz, kk + 1)
                dve.wait_ge(m_dBx, kk + 1)
                dve.tensor_tensor_scan(dBx[:, k % 2, :], dA[:, k % 2, :], dBx[:, k % 2, :], 0.0, ALU.mult, ALU.add).then_inc(m_h, 1)

            def gate(g, c):
                dve.wait_ge(m_sum, 8 * g + 4 * c + 4)
                if not (num(g) and g == 0):
                    dve.wait_ge(m_o, g)
                n = 4 * g + 2 * c
                STT(yTm[:, c, :], xconv[:, c, ds(GW * g, GW)], Dv[:, c:c + 1], bank[:, 4 + c, :], ALU.mult, ALU.add).then_inc(m_y, 1)
                dve.wait_ge(m_y, n + 1)
                TT(yTm[:, c, :], yTm[:, c, :], sz[:, c, ds(GW * g, GW)], ALU.mult).then_inc(m_y, 1)

            def group(g, par):
                for k in range(8):
                    quad(g, k)
                    if k == 1 and not (num(g) and g == 0):
                        ln_norm(g - 1, 1 - par, GT * (g - 1), GT)
                    if k == 4:
                        gate(g, 0)
                gate(g, 1)
                dve.wait_ge(m_o, g + 1)
                ln_stats(g, par, bank[:, 7, :].rearrange("p (j n) -> p j n", j=GT), tile(X, GT * g, GT), GT)
            dve.wait_ge(ld_x, 16)
            pairs(dve, G, lambda j, par: group(2 * j + par, par))
            ln_norm(G - 1, 1, GT * (G - 1), GT)

            def attention(lay, ln0):
                def mask_bias(j, par, t):
                    dve.wait_ge(ld_mask[par], 16 * (j + 1))
                    if not (num(t) and t < 2):
                        dve.wait_ge(a_s, 2 * (t - 1))
                        dve.wait_ge(a_exp, 2 * (t - 1))
                    TS(mflag[:, par, :], maskb[:, par, :], 0.0, None, ALU.is_equal).then_inc(a_flag, 1)
                    dve.wait_ge(a_flag, 2 * t + 1)
                    TS(mbias[:, par, :], mflag[:, par, :], MASKED, None, ALU.mult).then_inc(a_mb, 1)
                    RED(allm[:, par, :], mflag[:, par, :], AX.X, ALU.min).then_inc(a_flag, 1)
                    dve.wait_ge(a_flag, 2 * t + 2)
                    TS(escale[:, par, :], allm[:, par, :], -(HD ** -0.5), HD ** -0.5, ALU.mult, ALU.add).then_inc(a_esc, 1)

                def shift(u, par, hf):
                    dve.wait_ge(a_s, 2 * u + hf + 1)
                    if hf == 0 and not (num(u) and u < 2):
                        dve.wait_ge(a_pt, 4 * (u - 1))
                    s = bank[:, 2 + 2 * hf:4 + 2 * hf, 0:4 * SK].rearrange("p b (h n) -> p b h n", h=4)
                    m = nmx[:, par, 8 * hf:8 * hf + 8, :].rearrange("p (b h) n -> p b h n", b=2)
                    RED(m.rearrange("p b h n -> p b (h n)"), s, AX.X, ALU.max).then_inc(a_max, 1)
                    dve.wait_ge(a_max, 2 * u + hf + 1)
                    TT(sc[:, par, 8 * hf:8 * hf + 8, :].rearrange("p (b h) n -> p b h n", b=2), s,
                       m.to_broadcast([P, 2, 4, SK]), ALU.subtract).then_inc(a_sub, 1)

                dve.wait_ge(a_bvo, lay + 1)
                TT(abr[:, lay, :], abr[:, lay, :], bank[:, 7, 0:D], ALU.add).then_inc(a_bias, 1)
                dve.memset(vaug[:, :, :, HD + 1:32], 0.0)
                dve.memset(vaug[:, :, :, HD:HD + 1], 1.0)

                def step(j, par):
                    t = 2 * j + par
                    u = NT * lay + t
                    if ok(t + 1):
                        shift(u + 1, 1 - par, 0)
                    if ok(t - 1):
                        dve.wait_ge(a_sel, u)
                        o = bank[:, 1, 0:NH * (HD + 1)].rearrange("p (h n) -> p h n", h=NH)
                        dve.reciprocal(rden[:, 1 - par, :, :], o[:, :, HD:HD + 1]).then_inc(a_rden, 1)
                        dve.wait_ge(a_rden, u)
                        if not (num(u) and u < 3):
                            dve.wait_ge(a_ot, u - 2)
                        TT(on[:, 1 - par, :].rearrange("p (h n) -> p h n", h=NH), o[:, :, 0:HD], bc(rden[:, 1 - par, :, :], HD), ALU.mult).then_inc(a_on, 1)
                    if ok(t + 1):
                        shift(u + 1, 1 - par, 1)
                    if ok(t - 2):
                        ln_norm(ln0 + t - 2, par, t - 2, 1)
                    if ok(t - 1):
                        dve.wait_ge(a_out, u)
                        dve.wait_ge(a_xr, u)
                        ln_stats(ln0 + t - 1, 1 - par, bank[:, 1, 0:D], xr[:, 1 - par, :], 1)
                    if ok(t + 2):
                        if lay == 0:
                            mask_bias(j + 1, par, t + 2)
                        dve.wait_ge(a_qk, u + 3)
                        if not (num(u) and u < 0):
                            dve.wait_ge(a_pv, u + 1)
                        dve.tensor_copy(vaug[0:SK, par, :, 0:HD], bank[0:SK, 0, 256:384].rearrange("p (h n) -> p h n", h=NH)).then_inc(a_v, 1)
                steps(dve, step)
                ln_norm(ln0 + NT - 1, 1, NT - 1, 1)

            dve.wait_ge(ld_attn, 16 * 12)
            dve.memset(slots[:, 0, :], 0.0).then_inc(set_w, 1)
            attention(0, LN_XA0)

            dve.wait_ge(ld_moe, 64)
            dve.tensor_copy(phib[:, :], slots[:, 0, :]).then_inc(e_pb, 1)
            dve.wait_ge(e_pb, 1)
            TT(slots[:, 1, :], slots[:, 0, :], phib[:, :], ALU.subtract).then_inc(e_pb, 1)
            dve.wait_ge(e_pb, 2)
            dve.tensor_copy(phib[64:128, :], slots[64:128, 1, :]).then_inc(e_pb, 1)
            dve.wait_ge(e_pb, 3)
            TT(phib[96:128, :], slots[96:128, 1, :], phib[96:128, :], ALU.subtract).then_inc(e_pb, 1)
            dve.wait_ge(e_pb, 4)

            def step(j, par):
                t = 2 * j + par
                if ok(t):
                    dve.wait_ge(e_expD, t + 1)
                    RED(mxn[:, par, :], slots[:, par, :].rearrange("p (n s) -> p n s", s=PS), AX.X, ALU.add).then_inc(e_sum, 1)
                    dve.wait_ge(e_sum, t + 1)
                    dve.reciprocal(rD[:, par, :], mxn[:, par, :]).then_inc(e_rD, 1)
                if ok(t + 1):
                    lg = lgc[:, 1 - par, :].rearrange("p (n s) -> p n s", s=PS)
                    dve.wait_ge(e_lgc, 4 * (t + 1) + 4)
                    if not (num(t) and t < 1):
                        dve.wait_ge(e_rC, t)
                        dve.wait_ge(e_rD, t)
                    RED(mxp[:, 1 - par, :], lg.rearrange("p n s -> p s n"), AX.X, ALU.max).then_inc(e_mxp, 1)
                    RED(mxn[:, 1 - par, :], lg, AX.X, ALU.max).then_inc(e_mxn, 1)
                    dve.wait_ge(e_mxn, t + 2)
                    if not (num(t) and t < 1):
                        dve.wait_ge(e_xt, t)
                    TT(slots[:, 1 - par, :].rearrange("p (n s) -> p n s", s=PS), lg, bc(mxn[:, 1 - par, :].unsqueeze(2), PS), ALU.subtract).then_inc(e_subD, 1)
                if ok(t):
                    dve.wait_ge(e_fold2, t + 1)
                    RED(mxp[:, par, :], fold[:, E // 2:3 * E // 4].rearrange("p (n s) -> p s n", s=PS), AX.X, ALU.add).then_inc(e_sumC, 1)
                    dve.wait_ge(e_sumC, t + 1)
                    dve.reciprocal(tile(rC, t), mxp[:, par, :]).then_inc(e_rC, 1)
            steps(dve, step)

            dve.wait_ge(e_xt, NT)
            TS(xtl, bank[:, 4:8, :].rearrange("p b (c n) -> p (b c) n", n=D), -33000.0, 65000.0, ALU.max, ALU.min).then_inc(y_clip, 1)
            dve.wait_ge(y_clip, 1)
            bst = lny[:, :, :, :].rearrange("p b j n -> p (b j n)")[:, 0:EC_N * 6].rearrange("p (c n) -> p c n", n=6)
            bmv = sm[:, 32:64].rearrange("p (c n) -> p c n", n=2)
            for c in range(EC_N):
                ins = dve.bn_stats(bst[:, c, :], xtl[:, c, :])
            ins.then_inc(y_mv, 1)
            dve.wait_ge(y_mv, 1)
            for c in range(EC_N):
                ins = dve.bn_aggr(bmv[:, c, :], bst[:, c, :])
            ins.then_inc(y_mv, 1)
            dve.wait_ge(y_ve, 2)
            for c in range(EC_N):
                ins = TS(xtl[:, c, :], xtl[:, c, :], bmv[:, c, 0:1], sm[:, 80 + c:81 + c], ALU.subtract, ALU.mult)
            ins.then_inc(y_n, 1)
            dve.wait_ge(y_mm, EC_N)
            dve.wait_ge(ld_eb, 64)
            TT(Yt[:, :, :], bank[:, 4:8, :].rearrange("p b (c n) -> p (b c) n", n=D), moe_y, ALU.add).then_inc(y_out, 1)

            def step(j, par):
                t = 2 * j + par
                if ok(t + 1):
                    for b in range(2, 4):
                        dve.wait_ge(c_tr, 4 * (t + 1) + b + 1)
                        if b == 2 and not (num(t) and t < 1):
                            dve.wait_ge(c_y, t)
                        dve.tensor_copy(slotsT[:, 1 - par, 4 * b:4 * b + 4, :], bank[:, b, :].rearrange("p (c n) -> p c n", c=4)).then_inc(c_cv, 1)
                if ok(t - 1):
                    ln_norm(LN_MOE + t - 1, 1 - par, t - 1, 1)
                if ok(t):
                    dve.wait_ge(c_y, t + 1)
                    ln_stats(LN_MOE + t, par, bank[:, 4 + par, 0:D], tile(X, t), 1)
            steps(dve, step)

            dve.wait_ge(ld_ret, 16 * 5)
            STT(kvbd.rearrange("p (h e) -> p h e", e=HD), mid(kvl, NH), float(NH * HD), bc(hmask[:, :].unsqueeze(2), HD), ALU.mult, ALU.mult).then_inc(set_v, 1)

            dve.memset(vpad[:, :, :, HD:32], 0.0)

            def decayed(t, par, hf):
                dve.wait_ge(r_s, 2 * t + hf + 1)
                if hf == 0 and not (num(t) and t < 2):
                    dve.wait_ge(r_pv, t - 1)
                TT(rd[:, par, 8 * hf:8 * hf + 8, :].rearrange("p (b h) n -> p b (h n)", b=2), bank[:, 2 + 2 * hf:4 + 2 * hf, :],
                   decay[:, 8 * hf:8 * hf + 8, :].rearrange("p (b h) n -> p b (h n)", b=2), ALU.mult).then_inc(r_rd, 1)

            def step(j, par):
                t = 2 * j + par
                q = 1 - par
                if ok(t + 1):
                    decayed(t + 1, q, 0)
                if ok(t - 1):
                    dve.wait_ge(r_sel, t)
                    dve.wait_ge(r_crc, t)
                    TT(gr[:, q, :], bank[:, 7, 0:D], crs[:, q, :], ALU.add).then_inc(r_r, 1)
                    dve.wait_ge(r_r, t)
                    dve.bn_stats(gst[:, q, :], gr[:, q, :]).then_inc(r_st, 1)
                    dve.wait_ge(r_st, t)
                    dve.sem_inc(passed_dve, 1)
                    dve.bn_aggr(gmv[:, q, :], gst[:, q, :]).then_inc(r_mv, 1)
                if ok(t + 1):
                    decayed(t + 1, q, 1)
                if ok(t - 2):
                    ln_norm(LN_RET + t - 2, par, t - 2, 1)
                if ok(t - 1):
                    dve.wait_ge(r_m1, t)
                    dve.tensor_copy(gsc[:, q, 0:1], bank[:, 7, P:P + 1]).then_inc(r_d, 1)
                    dve.wait_ge(r_d, 2 * t - 1)
                    TT(gsc[:, q, 1:2], gmv[:, q, 0:1], gsc[:, q, 0:1], ALU.subtract).then_inc(r_d, 1)
                    dve.wait_ge(r_d, 2 * t)
                    TS(gmv[:, q, 0:1], gsc[:, q, 1:2], gsc[:, q, 1:2], gmv[:, q, 1:2], ALU.mult, ALU.add).then_inc(r_v2, 1)
                    dve.wait_ge(r_m2, t)
                    TS(gsc[:, q, 2:3], bank[:, 7, P + 1:P + 2], LN_EPS, None, ALU.add).then_inc(r_ve, 1)
                    dve.wait_ge(r_rs, t)
                    TS(gt1[:, q, :], gr[:, q, :], gsc[:, q, 0:1], gsc[:, q, 3:4], ALU.subtract, ALU.mult).then_inc(r_t1, 1)
                    dve.wait_ge(r_t1, t)
                    TT(gt2[:, q, :].rearrange("p (h e) -> p h e", e=HD), gt1[:, q, :].rearrange("p (h e) -> p h e", e=HD),
                       bc(gnw.unsqueeze(2), HD), ALU.mult).then_inc(r_t2, 1)
                    dve.wait_ge(r_t2, t)
                    dve.wait_ge(r_xr, t)
                    ln_stats(LN_RET + t - 1, q, gt2[:, q, :], xr[:, q, :], 1)
                if ok(t + 2):
                    dve.wait_ge(r_qk, t + 3)
                    dve.wait_ge(r_crc, t + 2)
                    if not (num(t) and t < 0):
                        dve.wait_ge(r_pv, t + 1)
                    dve.tensor_copy(vpad[:, par, :, 0:HD], bank[:, 0, 2 * P:3 * P].rearrange("p (h n) -> p h n", h=NH)).then_inc(r_v, 1)
            steps(dve, step)
            ln_norm(LN_RET + NT - 1, 1, NT - 1, 1)

            attention(1, LN_XA1)

            dve.wait_ge(ld_ffn, 16 * 8)
            RED(amx[:, 0:1], wf1.rearrange("p c n -> p (c n)"), AX.X, ALU.max, apply_absolute_value=True)
            RED(amx[:, 1:2], wf2, AX.X, ALU.max, apply_absolute_value=True).then_inc(f_w, 1)
            dve.wait_ge(f_w, 2)
            TS(amx[:, 4:6], amx[:, 2:4], 1.0 / QMAX, None, ALU.mult).then_inc(f_wp, 1)
            dve.wait_ge(f_wp, 1)
            dve.reciprocal(amx[:, 6:8], amx[:, 4:6]).then_inc(f_wp, 1)
            dve.wait_ge(f_wp, 2)
            n = 2
            for i, (w, tq) in enumerate(((wf1.rearrange("p c n -> p (c n)"), tq1), (wf2, tq2))):
                TS(tq, w, amx[:, 6 + i:7 + i], ROUND, ALU.mult, ALU.add).then_inc(f_wp, 1)
                dve.wait_ge(f_wp, n + 1)
                TS(tq, tq, ROUND, QMAX, ALU.subtract, ALU.min).then_inc(f_wp, 1)
                dve.wait_ge(f_wp, n + 2)
                TS(tq, tq, -QMAX - 1.0, amx[:, 4 + i:5 + i], ALU.max, ALU.mult).then_inc(f_wp, 1)
                dve.wait_ge(f_wp, n + 3)
                TT(tq, tq, w, ALU.subtract).then_inc(f_wp, 1)
                dve.wait_ge(f_wp, n + 4)
                TT(w, w, tq, ALU.add).then_inc(f_wp, 1)
                n += 5
            TS(afc[0:R, :], afc[0:R, :], 2.0, None, ALU.mult)
            TS(apj[0:R, :], apj[0:R, :], 2.0, None, ALU.mult).then_inc(f_wp, 1)

            def step(j, par):
                g = 2 * j + par
                if not (num(g) and g == 0):
                    ln_norm(LN_FFN + g - 1, 1 - par, GT * (g - 1), GT)
                dve.wait_ge(f_o, g + 1)
                dve.wait_ge(f_xs, 2 * g + 2)
                ln_stats(LN_FFN + g, par, bank[:, 6 + par, :].rearrange("p (j n) -> p j n", j=GT), fr4[:, par, :, :], GT)
            pairs(dve, G, step)
            ln_norm(LN_FFN + G - 1, 1, GT * (G - 1), GT)

        @block.tensor
        def _(pe):
            MM = pe.matmul
            I = ident[:, :]
            pe.wait_ge(ld_const, 80)
            pe.wait_ge(set_v, 1)
            for g in range(G):
                par = g % 2
                pe.wait_ge(ld_xs4[par], 16 * (g // 2 + 1))
                if g >= 1:
                    pe.wait_ge(m_xT, g)
                for j in range(GT):
                    ins = pe.transpose(bank[:, 0, P * j:P * j + P], xs4[:, par, j, :], I)
                ins.then_inc(m_tr, 1)
                pe.wait_ge(m_xT, g + 1)
                for c in range(NC):
                    if g >= 1:
                        pe.wait_ge(m_silu, 2 * (g - 1) + c + 1)
                    for k in range(KC):
                        ins = MM(bank[:, 1 + c, :], wk[:, k, P * c:P * c + P], xTp[:, par, :, k:k + P], start=(k == 0), stop=(k == KC - 1))
                    ins.then_inc(m_mm, 1)
                for c in range(NC):
                    if g >= 1:
                        pe.wait_ge(m_silz, 2 * (g - 1) + c + 1)
                    MM(bank[:, 3 + c, :], w_in[:, DI + P * c:DI + P * c + P], xTp[:, par, :, KC - 1:], start=True, stop=True).then_inc(m_mm, 1)
            for g in range(G):
                gw = slice(GW * g, GW * g + GW)
                pe.wait_ge(m_silu, 2 * g + 2)
                if g >= 1:
                    pe.wait_ge(m_split, 3 * g - 1)
                for c in range(NC):
                    ins = MM(bank[:, 7, :], wx[:, c, :], xconv[:, c, gw], start=(c == 0), stop=(c == NC - 1))
                ins.then_inc(m_wx, 1)
                pe.wait_ge(m_dtin, g + 1)
                if g >= 1:
                    pe.wait_ge(m_relu, g)
                for c in range(NC):
                    MM(bank[:, 5 + c, :], wdt[0:R, P * c:P * c + P], dtin[0:R, :], start=True, stop=True).then_inc(m_dtp, 1)

            def spread(g, k):
                kk, q = 8 * g + k, k % 4
                if not (num(kk) and kk == 0):
                    pe.wait_ge(m_dBx, kk)
                for i in range(4):
                    ins = MM(bank[:, i, :], sel[:, 4 * q + i, :], Bs[:, ds(GW * g, GW)], start=True, stop=True)
                ins.then_inc(m_B, 1)

            def sum_states(g, k):
                kk, c, q = 8 * g + k, k // 4, k % 4
                pe.wait_ge(m_h, kk + 1)
                if q == 0 and not (num(g) and g == 0):
                    pe.wait_ge(m_y, 4 * (g - 1) + 2 * c + 1)
                for i in range(4):
                    ins = MM(bank[:, 4 + c, :], I, dBx[:, k % 2, GW * i:GW * i + GW],
                             start=(q == 0 and i == 0), stop=(q == 3 and i == 3))
                ins.then_inc(m_sum, 1)

            def scans(g):
                for k in range(8):
                    if k < 7:
                        spread(g, k + 1)
                    elif not (num(g) and g == G - 1):
                        spread(g + 1, 0)
                    sum_states(g, k)
                pe.wait_ge(m_y, 4 * g + 4)
                if not (num(g) and g == 0):
                    pe.wait_ge(lny_s, g)
                for j in range(GT):
                    for c in range(NC):
                        ins = MM(bank[:, 7, P * j:P * j + P], yTm[:, c, P * j:P * j + P], wout[:, c, :], start=(c == 0), stop=(c == NC - 1))
                ins.then_inc(m_o, 1)
            pe.wait_ge(m_bs, G)
            pe.wait_ge(m_dtx, G)
            spread(0, 0)
            scans(0)
            with pe.Fori(1, G - 1) as g:
                scans(g)
            scans(G - 1)

            def attention(lay, ln0):
                wq, wkk, wv, wo = (wa[:, lay, i, :] for i in range(4))
                MM(bank[:, 7, 0:D], ab[:, lay, 2:3].to_broadcast([P, P]), wo, start=True, stop=True).then_inc(a_bvo, 1)
                pe.wait_ge(a_bias, lay + 1)

                def scores(u, par, hf):
                    if hf == 0:
                        pe.wait_ge(a_kexp, u + 1)
                        if lay == 0:
                            pe.wait_ge(a_mb, u + 1)
                    if not (num(u) and u == 0):
                        pe.wait_ge(a_sub, 2 * (u - 1) + hf + 1)
                    for b in (2 * hf, 2 * hf + 1):
                        ins = MM(bank[:, 2 + b, 0:4 * SK], qT[:, par, :], kexp[:, par, 4 * b:4 * b + 4, :], start=True, stop=(lay == 1))
                        if lay == 0:
                            ins = MM(bank[:, 2 + b, 0:4 * SK].rearrange("p (h n) -> p h n", h=4), identb[:, :], mid(mbias[:, par, :], 4), start=False, stop=True)
                    ins.then_inc(a_s, 1)

                def step(j, par):
                    t = 2 * j + par
                    u = NT * lay + t
                    if ok(t + 2):
                        pe.wait_ge(a_xs, u + 3)
                        pe.wait_ge(ld_ctx[par], 16 * (8 * lay + j + 2))
                    if not (num(t) and t < 2):
                        pe.wait_ge(lny_s, ln0 + t - 1)
                    if ok(t + 2):
                        pe.transpose(bank[:, 1, 0:P], xs[:, par, :], I)
                        pe.transpose(bank[:, 1, P:P + SK], ctxb[0:SK, par, :], ident[0:SK, 0:SK]).then_inc(a_tr, 1)
                    if ok(t + 1):
                        scores(u + 1, 1 - par, 0)
                    if ok(t + 2):
                        pe.wait_ge(a_xT, u + 3)
                    if ok(t - 1):
                        pe.wait_ge(a_po, u)
                        for r in range(4):
                            ins = MM(bank[:, 1, 36 * r:36 * r + 36], poT[:, 1 - par, r, :], sel9[:, :], start=True, stop=True)
                        ins.then_inc(a_sel, 1)
                    if ok(t + 1):
                        scores(u + 1, 1 - par, 1)
                    if ok(t - 1):
                        pe.wait_ge(a_on, u)
                        pe.transpose(bank[:, 1, 0:D], on[:, 1 - par, :], I).then_inc(a_ot, 1)
                    if ok(t + 2):
                        if not (num(u) and u < -1):
                            pe.wait_ge(a_qk, u + 2)
                            pe.wait_ge(a_v, u + 2)
                        MM(bank[:, 0, 0:P], wq, xT[:, par, 0:P], start=True, stop=True)
                        MM(bank[:, 0, P:P + SK], wkk, xT[:, par, P:P + SK], start=True, stop=True)
                        MM(bank[0:SK, 0, 256:384], xT[:, par, P:P + SK], wv, start=True, stop=True).then_inc(a_qkv, 1)
                    if ok(t - 1):
                        pe.wait_ge(a_otc, u)
                        MM(bank[:, 1, 0:D], oT[:, 1 - par, :], wo, start=True, stop=True).then_inc(a_out, 1)
                    if ok(t):
                        for r in range(4):
                            if r % 2 == 0:
                                pe.wait_ge(a_exp, 2 * u + r // 2 + 1)
                            if r == 0 and not (num(u) and u == 0):
                                pe.wait_ge(a_po, u)
                            if r > 0 and not (num(u) and u == 0 and r == 1):
                                pe.wait_ge(a_ptc, 4 * u + r - 1)
                            for i in range(4):
                                ins = pe.transpose(bank[0:SK, 6 + r % 2, P * i:P * i + P], sc[:, par, 4 * r + i, :], I)
                            ins.then_inc(a_pt, 1)
                        pe.wait_ge(a_v, u + 1)
                        for r in range(4):
                            if r in (0, 3):
                                pe.wait_ge(a_ptc, 4 * u + (3 if r == 0 else 4))
                            for i in range(4):
                                ins = MM(bank[32 * i:32 * i + 32, 6, P * r:P * r + P], vaug[0:SK, par, 4 * r + i, :], pT[0:SK, par, 4 * r + i, :],
                                         start=True, stop=True, skip_group_check=True)
                        ins.then_inc(a_pv, 1)
                steps(pe, step)

            pe.wait_ge(ld_attn, 16 * 12)
            pe.wait_ge(x_ready, LN_XA0)
            attention(0, LN_XA0)

            pe.wait_ge(x_ready, LN_MOE)
            pe.wait_ge(ld_moe, 64)
            for b in range(4):
                for i in range(4):
                    ins = pe.transpose(bank[:, b, P * i:P * i + P], phir[:, 4 * b + i, :], I)
                ins.then_inc(set_w, 1)
            pe.wait_ge(e_phi, 4)
            pe.wait_ge(e_pb, 4)

            def step(j, par):
                t = 2 * j + par
                if ok(t + 2):
                    pe.wait_ge(e_xs, t + 3)
                    if not (num(t) and t < -1):
                        pe.wait_ge(e_lgc, 4 * (t + 1) + 1)
                    pe.transpose(bank[:, 0, 0:P], xs[:, par, :], I).then_inc(e_tr, 1)
                if ok(t - 1):
                    pe.wait_ge(e_Dn, t)
                    for c in range(EC_N):
                        ins = MM(bank[:, 4 + c // 4, P * (c % 4):P * (c % 4) + P], slots[:, 1 - par, P * c:P * c + P], tile(X, t - 1),
                                 start=(num(t) and t == 1 and c % 4 == 0), stop=(num(t) and t == NT), skip_group_check=True)
                    ins.then_inc(e_xt, 1)
                if ok(t + 2):
                    pe.wait_ge(e_xT, t + 3)
                    for b in range(4):
                        if b > 0 and not (num(t) and t < -1):
                            pe.wait_ge(e_lgc, 4 * (t + 1) + b + 1)
                        MM(bank[:, b, :], xT[:, par, 0:P], phiT[:, 512 * b:512 * b + 512], start=True, stop=False)
                        MM(bank[:, b, :], onesb[:, :], phib[:, 512 * b:512 * b + 512], start=False, stop=True).then_inc(e_log, 1)
            steps(pe, step)

            pe.wait_ge(y_tanh, 1)
            for b in range(4):
                for i in range(4):
                    ins = pe.transpose(bank[:, b, P * i:P * i + P], xtl[:, 4 * b + i, :], I)
                ins.then_inc(y_tr, 1)
            pe.wait_ge(y_trc, 4)
            for c in range(EC_N):
                pe.wait_ge(ld_ew[c % 4], 16 * (c // 4 + 1))
                for n in range(4):
                    ins = MM(bank[32 * n:32 * n + 32, 4 + c // 4, P * (c % 4):P * (c % 4) + P], xtlT[:, c, 32 * n:32 * n + 32], ew[:, c % 4, n, :],
                             start=True, stop=True, skip_group_check=True)
                ins.then_inc(y_mm, 1)

            pe.wait_ge(y_out, 1)

            def step(j, par):
                t = 2 * j + par
                if ok(t + 1):
                    pe.wait_ge(c_n, t + 2)
                    for b in range(4):
                        if not (num(t) and t < 0):
                            if b < 2:
                                pe.wait_ge(c_ca, 2 * t + b + 1)
                            else:
                                pe.wait_ge(c_cv, 2 * t + b - 2 + 1)
                        for i in range(4):
                            ins = pe.transpose(bank[:, b, P * i:P * i + P], slots[:, 1 - par, P * (4 * b + i):P * (4 * b + i) + P], I)
                        ins.then_inc(c_tr, 1)
                if ok(t):
                    if not (num(t) and t < 2):
                        pe.wait_ge(lny_s, LN_MOE + t - 1)
                    pe.wait_ge(c_ca, 2 * t + 2)
                    pe.wait_ge(c_cv, 2 * t + 2)
                    for c in range(EC_N):
                        ins = MM(bank[:, 4 + par, 0:D], slotsT[:, par, c, :], Yt[:, c, :], start=(c == 0), stop=(c == EC_N - 1))
                    ins.then_inc(c_y, 1)
            steps(pe, step)

            pe.wait_ge(x_ready, LN_RET)
            pe.wait_ge(ld_ret, 16 * 5)
            pe.wait_ge(set_v, 2)

            def scores(t, par, hf):
                if hf == 0:
                    pe.wait_ge(r_qe, t + 1)
                if not (num(t) and t == 0):
                    pe.wait_ge(r_rd, 2 * (t - 1) + hf + 1)
                for b in (2 * hf, 2 * hf + 1):
                    ins = MM(bank[:, 2 + b, :], qkT[:, par, P:2 * P], qexp[:, par, 4 * b:4 * b + 4, :], start=True, stop=True)
                ins.then_inc(r_s, 1)

            def step(j, par):
                t = 2 * j + par
                if ok(t + 2):
                    pe.wait_ge(r_xs, t + 3)
                    if not (num(t) and t < -1):
                        pe.wait_ge(r_xT, t + 2)
                    pe.transpose(bank[:, 1, 0:P], xs[:, par, :], I).then_inc(r_tr, 1)
                if ok(t + 1):
                    scores(t + 1, 1 - par, 0)
                if ok(t - 1):
                    pe.wait_ge(r_po, t)
                    if not (num(t) and t < 2):
                        pe.wait_ge(r_ve, t - 1)
                    for r in range(4):
                        ins = MM(bank[:, 7, 32 * r:32 * r + 32], rpo[:, 1 - par, r, :], sel8[:, :], start=True, stop=True)
                    ins.then_inc(r_sel, 1)
                if ok(t + 1):
                    scores(t + 1, 1 - par, 1)
                if ok(t - 1):
                    pe.wait_ge(r_mv, t)
                    MM(bank[:, 7, P:P + 1], mean_w[:, :], gmv[:, 1 - par, 0:1], start=True, stop=True).then_inc(r_m1, 1)
                if not (num(t) and (t < 0 or t == NT)):
                    pe.wait_ge(r_crc, t + 1)
                if ok(t + 1):
                    pe.wait_ge(r_v, t + 2)
                    MM(bank[:, 0, 3 * P:4 * P], qkT[:, 1 - par, 0:P], kvbd, start=True, stop=True).then_inc(r_cr, 1)
                if ok(t + 2):
                    pe.wait_ge(r_xT, t + 3)
                    MM(bank[:, 0, 0:P], wqkv[:, 0:D], xT[:, par, 0:P], start=True, stop=True)
                    MM(bank[:, 0, P:2 * P], wqkv[:, D:2 * D], xT[:, par, 0:P], start=True, stop=True)
                    MM(bank[:, 0, 2 * P:3 * P], xT[:, par, 0:P], wqkv[:, 2 * D:3 * D], start=True, stop=True).then_inc(r_qkv, 1)
                if ok(t - 1):
                    pe.wait_ge(r_v2, t)
                    MM(bank[:, 7, P + 1:P + 2], mean_w[:, :], gmv[:, 1 - par, 0:1], start=True, stop=True).then_inc(r_m2, 1)
                if ok(t):
                    pe.wait_ge(r_v, t + 1)
                    pe.wait_ge(r_rd, 2 * t + 2)
                    if not (num(t) and t == 0):
                        pe.wait_ge(r_po, t)
                    for r in range(4):
                        for i in range(4):
                            ins = MM(bank[32 * i:32 * i + 32, 6, P * r:P * r + P], vpad[:, par, 4 * r + i, :], rd[:, par, 4 * r + i, :],
                                     start=True, stop=True, skip_group_check=True)
                    ins.then_inc(r_pv, 1)
            steps(pe, step)

            pe.wait_ge(x_ready, LN_XA1)
            pe.wait_ge(ld_xa1, 64)
            for i in range(4):
                ins = pe.transpose(bank[:, 0, P * i:P * i + P], wraw[:, i, :], I)
            ins.then_inc(set_w, 1)
            pe.wait_ge(set_w, 8)
            attention(1, LN_XA1)

            pe.wait_ge(x_ready, LN_FFN)
            pe.wait_ge(f_wp, 13)
            for c in range(FC):
                ins = MM(bank[0:R, 0, P * c:P * c + P], bfc[:, c, :], I, start=True, stop=True)
            ins.then_inc(f_wt, 1)
            MM(bank[0:R, 1, 0:D], bpj, I, start=True, stop=True).then_inc(f_wt, 1)
            pe.wait_ge(f_wc, 2)
            for c in range(FC):
                MM(bank[:, 2, P * c:P * c + P], wf1[:, c, :], I, start=True, stop=False)
                ins = MM(bank[:, 2, P * c:P * c + P], afc[0:R, :], bT[0:R, P * c:P * c + P], start=False, stop=True)
            ins.then_inc(f_wt, 1)
            for c in range(FC):
                MM(bank[:, 3, P * c:P * c + P], wf2[:, P * c:P * c + P], I, start=True, stop=False)
                ins = MM(bank[:, 3, P * c:P * c + P], apj[0:R, P * c:P * c + P], bT[0:R, FF:FF + D], start=False, stop=True)
            ins.then_inc(f_wt, 1)
            pe.wait_ge(f_wc, 4)

            def up(g, par):
                pe.wait_ge(f_xs, 2 * g + 1)
                if not (num(g) and g == 0):
                    pe.wait_ge(f_xT, g)
                for j in range(GT):
                    ins = pe.transpose(bank[:, 0, P * j:P * j + P], fs4[:, par, j, :], I)
                ins.then_inc(f_tr, 1)
                pe.wait_ge(f_xT, g + 1)
                for c in range(FC):
                    if not (num(g) and g == 0):
                        pe.wait_ge(f_g, 4 * (g - 1) + c + 1)
                    MM(bank[:, 2 + c, :], w1T[:, P * c:P * c + P], fxT[:, par, :], start=True, stop=True).then_inc(f_h, 1)

            def down(g, par):
                pe.wait_ge(f_g, 4 * g + 4)
                if not (num(g) and g < 2):
                    pe.wait_ge(lny_s, LN_FFN + g - 1)
                for j in range(GT):
                    for c in range(FC):
                        ins = MM(bank[:, 6 + par, P * j:P * j + P], hT[:, par, c, P * j:P * j + P], w2T[:, c, :], start=(c == 0), stop=(c == FC - 1))
                ins.then_inc(f_o, 1)
            up(0, 0)

            def step(j, par):
                g = 2 * j + par
                if not (num(g) and g == G - 1):
                    up(g + 1, 1 - par)
                down(g, par)
            pairs(pe, G, step, last_peeled=True)


def shape_constants():
    p = np.arange(P)
    gamma = 1.0 - 2.0 ** (-5.0 - np.arange(NH, dtype=np.float64))
    diff = p[None, :] - p[:, None]
    decay = np.where(diff[:, None, :] >= 0, gamma[None, :, None] ** np.maximum(diff, 0)[:, None, :], 0.0)
    part = p[:, None]
    return {
        "c_ident": np.eye(P, dtype=np.float32),
        "c_hmask": (part // HD == np.arange(NH)[None, :]).astype(np.float32),
        "c_selcol": ((part >= 32) & (part % 32 == np.arange(NS)[None, :])).astype(np.float32),
        "c_sel9": ((p % 32 < HD + 1)[:, None] & ((HD + 1) * (p // 32) + p % 32)[:, None].__eq__(np.arange(4 * (HD + 1))[None, :])).astype(np.float32),
        "c_sel8": ((p % 32 < HD)[:, None] & (HD * (p // 32) + p % 32)[:, None].__eq__(np.arange(4 * HD)[None, :])).astype(np.float32),
        "c_decay": decay.astype(np.float32),
    }


def kernel(**inputs):
    import numpy as _np
    import concourse.bacc as _bacc
    from concourse import mybir as _mybir
    from concourse.bass_utils import run_bass_kernel_spmd as _run

    nc = _bacc.Bacc("TRN2", target_bir_lowering=False, num_devices=1)
    arrays, aps = {}, {}
    for name, value in {**inputs, **shape_constants()}.items():
        v = _np.ascontiguousarray(value)
        arrays[f"in_{name}"] = v
        aps[name] = nc.dram_tensor(f"in_{name}", v.shape, _mybir.dt.from_np(v.dtype), kind="ExternalInput").ap()
    out = nc.dram_tensor("out_0", (NT, P, D), F32, kind="ExternalOutput").ap()
    build(nc, aps, out)
    r = _run(nc, [arrays], core_ids=[0])
    return r.results[0]["out_0"]
```

```python
from contextlib import ExitStack

import numpy as np
import concourse.bass as bass
from concourse import mybir
from concourse.bass import ds

F32 = mybir.dt.float32
BF16 = mybir.dt.bfloat16
I32 = mybir.dt.int32
ALU = mybir.AluOpType
ACT = mybir.ActivationFunctionType
AX = mybir.AxisListType

NT, P, D = 16, 128, 128
NH, HD = 16, 8
SK = 120
G, GT = 4, 4
GW = GT * P
NS, DI, NC = 16, 256, 2
KC = 4
NE, PS = 64, 32
E = NE * PS
EC_N = E // P
FF, R = 512, 16
FC = FF // P
LN_EPS = 1e-5
MASKED = -float(2 ** 30)
QMAX = 127.0
ROUND = 12582912.0

LN_MAMBA, LN_XA0, LN_MOE, LN_RET, LN_XA1, LN_FFN, LN_END = 0, 4, 20, 36, 52, 68, 72
OUT_DMAS = G


def build(nc, a, out):
    ctx = ExitStack()
    with ctx:
        def sb(name, shape, dt=F32):
            return ctx.enter_context(nc.sbuf_tensor(name, shape, dt))

        def sem(name):
            return ctx.enter_context(nc.semaphore(name))

        bank = ctx.enter_context(nc.psum_tensor("bank", [P, 8, 512], F32))
        arena = sb("arena", [P, NT * E])
        X = sb("X", [P, NT, D])
        slots = sb("slots", [P, 2, E])
        slotsT = sb("slotsT", [P, 2, EC_N, P])
        phiT = sb("phiT", [P, E])
        phib = sb("phib", [P, E], BF16)
        spare = sb("spare", [P, E])
        ident = sb("ident", [P, P])
        identb = sb("identb", [P, P], BF16)
        onesb = sb("onesb", [P, P], BF16)
        mean_w = sb("mean_w", [P, P])
        hmask = sb("hmask", [P, NH])
        selcol = sb("selcol", [P, NS])
        mhalf = sb("mhalf", [P, 16])
        xs = sb("xs", [P, 2, D])
        xr = sb("xr", [P, 2, D])
        xT = sb("xT", [P, 2, 256])
        lny = sb("lny", [P, 2, GT, D])
        lnst = sb("lnst", [P, 2, GT, 6])
        lnmv = sb("lnmv", [P, 2, GT, 2])
        lnve = sb("lnve", [P, 2, GT])
        lnrs = sb("lnrs", [P, 2, GT])
        wa = sb("wa", [P, 2, 4, D])
        ab = sb("ab", [P, 2, 3])
        abr = sb("abr", [P, 2, D])
        sel9 = sb("sel9", [P, 4 * (HD + 1)])
        sel8 = sb("sel8", [P, 4 * HD])
        sel4 = sb("sel4", [P, P])
        rC = sb("rC", [P, NT, PS])
        mxn = sb("mxn", [P, 2, NE])
        mxp = sb("mxp", [P, 2, PS])
        rD = sb("rD", [P, 2, NE])
        sm = sb("sm", [P, 96 + 4])

        off = [0]

        def carve(cols, dt=F32):
            v = arena[:, off[0]:off[0] + cols]
            off[0] += cols
            assert off[0] <= NT * E
            return v if dt == F32 else v.bitcast(dt)

        xconv = carve(NC * NT * P).rearrange("p (c n) -> p c n", c=NC)
        sz = carve(NC * NT * P).rearrange("p (c n) -> p c n", c=NC)
        dt_all = carve(NC * NT * P).rearrange("p (c n) -> p c n", c=NC)
        dtx_all = carve(NC * NT * P).rearrange("p (c n) -> p c n", c=NC)
        dA = carve(2 * 4 * GW).rearrange("p (b n) -> p b n", b=2)
        dBx = carve(2 * 4 * GW).rearrange("p (b n) -> p b n", b=2)
        hb = [dBx[:, 0, :], dBx[:, 1, :], spare[:, :], slotsT[:, 1, :, :].rearrange("p c n -> p (c n)")]
        Bb = slots
        Bs = carve(NT * P // 2, BF16)
        sel = carve(NS * P // 2, BF16).rearrange("p (n m) -> p n m", n=NS)
        w_in = carve(2 * DI)
        cwb = carve(DI * KC).rearrange("p (d k) -> p d k", k=KC)
        wk = carve(KC * DI).rearrange("p (k d) -> p k d", k=KC)
        wx = carve(NC * P).rearrange("p (c n) -> p c n", c=NC)
        wdt = carve(DI)
        wout = carve(NC * D).rearrange("p (c n) -> p c n", c=NC)
        alog = carve(NC * NS).rearrange("p (c n) -> p c n", c=NC)
        Am = carve(NC * NS).rearrange("p (c n) -> p c n", c=NC)
        convb, bdt, Dv = carve(NC), carve(NC), carve(NC)
        xTp = carve(2 * GT * (P + KC - 1)).rearrange("p (b j n) -> p b j n", b=2, j=GT)
        xs4 = carve(2 * GW).rearrange("p (b j n) -> p b j n", b=2, j=GT)
        bres = spare[:, 0:GW]
        dtin = spare[:, GW:2 * GW]
        sp_l = dA[:, 0, :].rearrange("p (c n) -> p c n", c=4)[:, 0:2, :]
        sp_r = dA[:, 1, :].rearrange("p (c n) -> p c n", c=4)[:, 0:2, :]
        yTm = slotsT[:, 0, 0:2 * GT, :].rearrange("p (c j) n -> p c (j n)", c=NC)

        off[0] = 0
        ctxb = carve(2 * P).rearrange("p (b n) -> p b n", b=2)
        maskb = carve(2 * SK).rearrange("p (b n) -> p b n", b=2).bitcast(I32)
        mbias = carve(SK, BF16).rearrange("p (b n) -> p b n", b=2)
        mflag = carve(2 * SK).rearrange("p (b n) -> p b n", b=2)
        allm = carve(2).rearrange("p (b n) -> p b n", b=2)
        escale = carve(2).rearrange("p (b n) -> p b n", b=2)
        qT = carve(2 * P).rearrange("p (b n) -> p b n", b=2)
        kT = carve(2 * SK).rearrange("p (b n) -> p b n", b=2)
        kexp = carve(2 * NH * SK).rearrange("p (b h n) -> p b h n", b=2, h=NH)
        vaug = carve(2 * NH * 32).rearrange("p (b h n) -> p b h n", b=2, h=NH)
        poT = carve(2 * 4 * P).rearrange("p (b r n) -> p b r n", b=2, r=4)
        nmx = carve(2 * NH).rearrange("p (b h n) -> p b h n", b=2, n=1)
        sc = carve(2 * NH * SK).rearrange("p (b h n) -> p b h n", b=2, h=NH)
        pT = carve(2 * NH * P).rearrange("p (b h n) -> p b h n", b=2, h=NH)
        rden = carve(2 * NH).rearrange("p (b h n) -> p b h n", b=2, n=1)
        on = carve(2 * D).rearrange("p (b n) -> p b n", b=2)
        oT = carve(2 * D).rearrange("p (b n) -> p b n", b=2)
        wraw = carve(4 * D).rearrange("p (i n) -> p i n", i=4)
        top_attn = off[0]

        EC = arena[:, :].rearrange("p (t e) -> p t e", t=NT)
        xtl = slotsT[:, 0, :, :]
        xtlT = slotsT[:, 1, :, :]
        phir = slotsT[:, 0, :, :]
        lgc = slotsT[:, :, :, :].rearrange("p b c n -> p b (c n)")
        fold = spare[:, 0:E // 2]
        Yt = phiT[:, :].rearrange("p (c n) -> p c n", c=EC_N)
        ring = [b.rearrange("p (e n) -> p e n", e=16) for b in (slots[:, 0, :], slots[:, 1, :], spare[:, :])]
        bve, bnm, brs, bof = (sm[:, 32 + EC_N * i:32 + EC_N * (i + 1)] for i in range(4))

        def in_place(t):
            return isinstance(t, int) and t < 3

        off[0] = 0
        decay = carve(NH * P).rearrange("p (h n) -> p h n", h=NH)
        qexp = carve(2 * NH * P).rearrange("p (b h n) -> p b h n", b=2, h=NH)
        rd = carve(2 * NH * P).rearrange("p (b h n) -> p b h n", b=2, h=NH)
        qkT = carve(2 * 2 * D).rearrange("p (b n) -> p b n", b=2)
        vpad = carve(2 * NH * 32).rearrange("p (b h n) -> p b h n", b=2, h=NH)
        rpo = carve(2 * 4 * P).rearrange("p (b r n) -> p b r n", b=2, r=4)
        crs = carve(2 * D).rearrange("p (b n) -> p b n", b=2)
        gr = carve(2 * D).rearrange("p (b n) -> p b n", b=2)
        gst = carve(2 * 6).rearrange("p (b n) -> p b n", b=2)
        gmv = carve(2 * 2).rearrange("p (b n) -> p b n", b=2)
        gsc = carve(2 * 4).rearrange("p (b n) -> p b n", b=2)
        gt1 = carve(2 * D).rearrange("p (b n) -> p b n", b=2)
        gt2 = carve(2 * D).rearrange("p (b n) -> p b n", b=2)
        wqkv = carve(3 * D)
        kvl = carve(HD)
        kvbd = carve(D)
        gnw, gnb = carve(NH), carve(NH)

        assert max(off[0], top_attn) <= 17920
        off[0] = 17920
        wf1 = carve(FC * D).rearrange("p (c n) -> p c n", c=FC)
        wf2 = carve(FF)
        tq1 = carve(FF)
        tq2 = carve(FF)
        bfcr = carve(FC)
        bpr = carve(D)
        afc = carve(D)
        bfc = carve(FC * R).rearrange("p (c r) -> p c r", c=FC)
        apj = carve(FF)
        bpj = carve(R)
        bT = carve(FF + D)
        w1T = carve(FF)
        w2T = carve(FC * D).rearrange("p (c n) -> p c n", c=FC)
        amx = carve(8)
        fs4 = carve(2 * GW).rearrange("p (b j n) -> p b j n", b=2, j=GT)
        fr4 = carve(2 * GW).rearrange("p (b j n) -> p b j n", b=2, j=GT)
        fxT = carve(2 * GW).rearrange("p (b n) -> p b n", b=2)
        hT = carve(2 * FC * GW).rearrange("p (b c n) -> p b c n", b=2, c=FC)

        ld_const, ld_x, ld_mamba, ld_attn, ld_moe = (sem(f"ld_{n}") for n in ("const", "x", "mamba", "attn", "moe"))
        ld_eb, ld_ret, ld_xa1, ld_ffn = (sem(f"ld_{n}") for n in ("eb", "ret", "xa1", "ffn"))
        ld_xs4 = [sem("ld_xs4_0"), sem("ld_xs4_1")]
        ld_ctx = [sem("ld_ctx0"), sem("ld_ctx1")]
        ld_mask = [sem("ld_mask0"), sem("ld_mask1")]
        ld_ew = [sem(f"ld_ew{i}") for i in range(4)]
        stored = sem("stored")
        set_v, set_p, set_w = sem("set_v"), sem("set_p"), sem("set_w")
        lny_s, lnst_s, lnmv_s, lnve_s, lnrs_s, x_ready = (sem(n) for n in ("ln_y", "ln_stats", "ln_mv", "ln_ve", "ln_rstd", "x_ready"))
        m_tr, m_xT, m_mm, m_silu, m_silz = (sem(f"m_{n}") for n in ("tr", "xT", "mm", "silu", "silz"))
        m_wx, m_dtin, m_bs, m_dtp, m_abs, m_ln1, m_relu, m_dt, m_dtx = (sem(f"m_{n}") for n in ("wx", "dtin", "bs", "dtp", "abs", "ln", "relu", "dt", "dtx"))
        m_dA, m_dz, m_B, m_dBx, m_h, m_sum, m_y, m_o, m_A = (sem(f"m_{n}") for n in ("dA", "dz", "B", "dBx", "h", "sum", "y", "o", "A"))
        m_bc, m_dBp, ld_win = sem("m_bc"), sem("m_dBp"), sem("ld_win")
        m_split = sem("m_split")
        a_xs, a_xr, a_tr, a_xT, a_qkv, a_qk, a_v, a_kexp, a_mb, a_esc = (sem(f"a_{n}") for n in ("xs", "xr", "tr", "xT", "qkv", "qk", "v", "kexp", "mb", "esc"))
        a_s, a_max, a_sub, a_exp, a_pt, a_ptc, a_pv, a_po, a_sel = (sem(f"a_{n}") for n in ("s", "max", "sub", "exp", "pt", "ptc", "pv", "po", "sel"))
        a_rden, a_on, a_ot, a_otc, a_out, a_flag, a_bvo, a_bias = (sem(f"a_{n}") for n in ("rden", "on", "ot", "otc", "out", "flag", "bvo", "bias"))
        e_xs, e_tr, e_xT, e_log, e_lgc, e_mxp, e_mxn, e_subD, e_subC, e_expD, e_expC = (sem(f"e_{n}") for n in ("xs", "tr", "xT", "log", "lgc", "mxp", "mxn", "subD", "subC", "expD", "expC"))
        e_sum, e_sumC, e_rD, e_rC, e_Dn, e_xt, e_pb, e_phi, e_fold, e_sum32 = (sem(f"e_{n}") for n in ("sum", "sumC", "rD", "rC", "Dn", "xt", "pb", "phi", "fold", "sum32"))
        y_xt, y_clip, y_mv, y_ve, y_tanh, y_tr, y_trc, y_mm, y_out = (sem(f"y_{n}") for n in ("xt", "clip", "mv", "ve", "tanh", "tr", "trc", "mm", "out"))
        c_n, c_tr, c_ca, c_cv, c_y = (sem(f"c_{n}") for n in ("n", "tr", "ca", "cv", "y"))
        r_xs, r_xr, r_tr, r_xT, r_qkv, r_cr, r_qk, r_crc, r_v, r_qe, r_s, r_rd, r_pv, r_po, r_sel = (sem(f"r_{n}") for n in ("xs", "xr", "tr", "xT", "qkv", "cr", "qk", "crc", "v", "qe", "s", "rd", "pv", "po", "sel"))
        r_r, r_st, r_mv, r_m1, r_d, r_v2, r_m2, r_ve, r_rs, r_t1, r_t2 = (sem(f"r_{n}") for n in ("r", "st", "mv", "m1", "d", "v2", "m2", "ve", "rs", "t1", "t2"))
        f_w, f_wp, f_wt, f_wc, f_xs, f_tr, f_xT, f_h, f_g, f_o = (sem(f"f_{n}") for n in ("w", "wp", "wt", "wc", "xs", "tr", "xT", "h", "g", "o"))

        passed_dve, passed_act, passed_pool = sem("passed_dve"), sem("passed_act"), sem("passed_pool")
        block = ctx.enter_context(nc.Block())

        def tile(buf, t, k=1):
            v = buf[:, ds(t, k), :]
            return v.rearrange("p a n -> p (a n)") if k == 1 else v

        def pairs(eng, n, step, last_peeled=False):
            step(0, 0)
            step(0, 1)
            end = n // 2 - (1 if last_peeled else 0)
            if end > 1:
                with eng.Fori(1, end) as j:
                    step(j, 0)
                    step(j, 1)
            if last_peeled:
                step(n // 2 - 1, 0)
                step(n // 2 - 1, 1)

        def steps(eng, step, last=NT):
            for t in range(-2, 2):
                step(t // 2, t % 2)
            with eng.Fori(1, NT // 2 - 2) as j:
                step(j, 0)
                step(j, 1)
            for t in range(NT - 4, last + 1):
                step(t // 2, t % 2)

        def ok(t):
            return not isinstance(t, int) or 0 <= t < NT

        def bc(ap, n):
            return ap.to_broadcast([ap.shape[0], ap.shape[1], n])

        def mid(ap, n):
            return ap.unsqueeze(1).to_broadcast([ap.shape[0], n, ap.shape[1]])

        def num(x):
            return isinstance(x, int)

        @block.sync
        def _(sp):
            xt = a["x"].rearrange("t p d -> p t d")
            sp.dma_start(xs4[:, 0, :, :], xt[:, 0:GT, :]).then_inc(ld_xs4[0], 16)
            for dst, name in ((ident, "c_ident"), (selcol, "c_selcol"), (hmask, "c_hmask"), (sel9, "c_sel9"), (sel8, "c_sel8")):
                sp.dma_start(dst[:, :], a[name]).then_inc(ld_const, 16)
            sp.dma_start(sel4[0:4, :], a["c_sel4"]).then_inc(ld_const, 16)
            sp.dma_start(xs4[:, 1, :, :], xt[:, GT:2 * GT, :]).then_inc(ld_xs4[1], 16)
            for dst, name in ((convb, "L0_attn_conv_b"), (bdt, "L0_attn_b_dt"), (Dv, "L0_attn_D")):
                sp.dma_start(dst, a[name].rearrange("(c p) -> p c", p=P), allow_slow_non_contiguous=True).then_inc(ld_mamba, 16)
            sp.dma_start(alog, a["L0_attn_A_log"].rearrange("(c p) n -> p c n", p=P)).then_inc(ld_mamba, 16)
            sp.dma_start(wout, a["L0_attn_W_out"].rearrange("(c p) n -> p c n", p=P)).then_inc(ld_mamba, 16)
            sp.dma_start(wdt[0:R, :], a["L0_attn_W_dt"]).then_inc(ld_mamba, 16)
            sp.wait_ge(set_w, 1)
            wxr = a["L0_attn_W_x"].rearrange("(c p) n -> p c n", p=P)
            for q in range(4):
                sp.dma_start(wx[:, :, 32 * q:32 * q + NS],
                             wxr[:, :, (0 if q == 0 else NS):(NS if q == 0 else 2 * NS)]).then_inc(ld_mamba, 16)
            sp.dma_start(X[:, :, :], xt).then_inc(ld_x, 16)
            for g in range(2, G):
                sp.wait_ge(m_tr, g - 1)
                sp.dma_start(xs4[:, g % 2, :, :], xt[:, GT * g:GT * g + GT, :]).then_inc(ld_xs4[g % 2], 16)
            for i, n in enumerate(("Wq", "Wk", "Wv", "Wo")):
                sp.dma_start(wa[:, 0, i, :], a["L0_xattn_" + n]).then_inc(ld_attn, 16)
            for lay in range(2):
                for i, n in enumerate(("bq", "bk", "bv")):
                    sp.dma_start(ab[:, lay, i:i + 1], a[f"L{lay}_xattn_{n}"].rearrange("(p o) -> p o", o=1)).then_inc(ld_attn, 16)
                sp.dma_start(abr[:, lay, :], a[f"L{lay}_xattn_bo"].partition_broadcast(P)).then_inc(ld_attn, 16)
            sp.wait_ge(x_ready, LN_XA0)
            sp.dma_start(phir, a["L0_ffn_phi_w"].rearrange("(c p) d -> p c d", p=P)).then_inc(ld_moe, 16)
            sp.wait_ge(set_w, 2)
            pb_row = a["L0_ffn_phi_b"].rearrange("(o n) -> o n", o=1)
            for row in (0, 64, 96):
                sp.dma_start(slots[row:row + 1, 0, :], pb_row).then_inc(ld_moe, 16)

            def attn_loads(lay):
                def step(j, par):
                    t, u = 2 * j + par, NT * lay + 2 * j + par
                    if not (num(u) and u < 2):
                        sp.wait_ge(a_tr, u - 1)
                    sp.dma_start(ctxb[0:SK, par, :], tile(a["ctx_1024"].rearrange("t s d -> s t d"), t)).then_inc(ld_ctx[par], 16)
                    if lay == 0:
                        if not (num(t) and t < 2):
                            sp.wait_ge(a_mb, t - 1)
                        sp.dma_start(maskb[:, par, :], tile(a["mask_Bx1xSxS2_ik1"].rearrange("t o q k -> q t (o k)"), t)).then_inc(ld_mask[par], 16)
                pairs(sp, NT, step)

            attn_loads(0)
            sp.wait_ge(e_log, 4 * NT)
            sp.dma_start(phiT[0:4, :].rearrange("p (c h) -> p c h", c=EC_N), a["L0_ffn_expert_b"].rearrange("(c n) h -> n c h", n=4)).then_inc(ld_eb, 16)
            sp.wait_ge(y_xt, 4)
            ewv = a["L0_ffn_expert_w"].rearrange("(b n) d h -> b d n h", b=4)
            for b in range(4):
                if b >= len(ring):
                    sp.wait_ge(y_mm, b - len(ring) + 1)
                sp.dma_start(ring[b % len(ring)], ewv[b]).then_inc(ld_ew[b], 16)
            sp.wait_ge(x_ready, LN_RET)
            sp.dma_start(decay, a["c_decay"]).then_inc(ld_ret, 16)
            sp.dma_start(wqkv, a["L1_attn_W_qkv"]).then_inc(ld_ret, 16)
            sp.dma_start(kvl, a["L1_attn_past_kv"].rearrange("h d e -> (h d) e")).then_inc(ld_ret, 16)
            sp.dma_start(gnw, a["L1_attn_gn_weight"].partition_broadcast(P)).then_inc(ld_ret, 16)
            sp.dma_start(gnb, a["L1_attn_gn_bias"].partition_broadcast(P)).then_inc(ld_ret, 16)
            sp.dma_start(wf1, a["L1_ffn_W_fc"].rearrange("(c p) d -> p c d", p=P)).then_inc(ld_ffn, 16)
            sp.dma_start(wf2, a["L1_ffn_W_proj"]).then_inc(ld_ffn, 16)
            sp.dma_start(bfcr, a["L1_ffn_b_fc"].rearrange("(c p) -> p c", p=P), allow_slow_non_contiguous=True).then_inc(ld_ffn, 16)
            sp.dma_start(bpr, a["L1_ffn_b_proj"].partition_broadcast(P)).then_inc(ld_ffn, 16)
            sp.dma_start(afc[0:R, :], a["L1_ffn_A_fc"]).then_inc(ld_ffn, 16)
            sp.dma_start(bfc, a["L1_ffn_B_fc"].rearrange("(c p) r -> p c r", p=P)).then_inc(ld_ffn, 16)
            sp.dma_start(apj[0:R, :], a["L1_ffn_A_proj"]).then_inc(ld_ffn, 16)
            sp.dma_start(bpj, a["L1_ffn_B_proj"]).then_inc(ld_ffn, 16)
            sp.wait_ge(x_ready, LN_XA1)
            for i, n in enumerate(("Wq", "Wk", "Wv", "Wo")):
                sp.dma_start(wraw[:, i, :], a["L1_xattn_" + n]).then_inc(ld_xa1, 16)
            attn_loads(1)
            ot = out.rearrange("t p d -> p t d")
            for g in range(G):
                sp.wait_ge(x_ready, LN_FFN + g + 1)
                sp.dma_start(ot[:, GT * g:GT * g + GT, :], X[:, GT * g:GT * g + GT, :]).then_inc(stored, 16)
            sp.wait_ge(stored, 16 * OUT_DMAS)

        @block.gpsimd
        def _(pool):
            def ln_rstd(e, par, k):
                pool.wait_ge(lnmv_s, e + 1)
                pool.sem_inc(passed_pool, 1)
                pool.tensor_scalar(lnve[:, par, 0:k], lnmv[:, par, 0:k, 1], LN_EPS, None, ALU.add).then_inc(lnve_s, 1)
                pool.wait_ge(lnve_s, e + 1)
                pool.tensor_tensor(lnrs[:, par, 0:k], lnve[:, par, 0:k], mhalf[:, 0:k], ALU.pow).then_inc(lnrs_s, 1)

            pool.memset(mhalf[:, :], -0.5)
            pool.memset(mean_w[:, :], 1.0 / P)
            pool.memset(onesb[:, :], 1.0).then_inc(set_p, 1)
            pool.wait_ge(set_p, 1)

            def scan_reset(g, k):
                kk = 8 * g + k
                pool.wait_ge(m_dA, kk + 1)
                v = dA[:, k % 2, :].rearrange("p (s n) -> p s n", n=P)[:, :, 0:1]
                pool.memset(v, 0.0).then_inc(m_dz, 1)

            def times_B(g, q):
                pp = 4 * g + q
                pool.wait_ge(m_bc, pp + 1)
                if not (num(g) and g == 0 and q < 2):
                    pool.wait_ge(m_sum, 2 * pp - 2)
                pool.tensor_tensor(hb[(2 * q + 1) % 4].rearrange("p (s n) -> p s n", s=4), Bb[:, q % 2, :].rearrange("p (s n) -> p s n", s=4),
                                   mid(dtx_all[:, 1, ds(GW * g, GW)], 4), ALU.mult).then_inc(m_dBp, 1)

            def mamba_group(g, par):
                for q in range(4):
                    times_B(g, q)
                    scan_reset(g, 2 * q)
                    scan_reset(g, 2 * q + 1)
                    if q == 1 and not (num(g) and g == 0):
                        ln_rstd(g - 1, 1 - par, GT)
            pool.wait_ge(m_dtx, G)
            pairs(pool, G, lambda j, par: mamba_group(2 * j + par, par))
            ln_rstd(G - 1, (G - 1) % 2, GT)

            def attention(lay, ln0):
                def stage(t, par):
                    u = NT * lay + t
                    if not (num(u) and u < 2):
                        pool.wait_ge(a_tr, u - 1)
                    pool.tensor_copy(xs[:, par, :], tile(X, t)).then_inc(a_xs, 1)

                pool.wait_ge(x_ready, ln0)
                stage(0, 0)
                pool.wait_ge(a_bias, lay + 1)

                def step(j, par):
                    t = 2 * j + par
                    u = NT * lay + t
                    if ok(t + 3):
                        stage(t + 3, 1 - par)
                    if ok(t):
                        if not (num(t) and t < 2):
                            pool.wait_ge(lny_s, ln0 + t - 1)
                        pool.tensor_tensor(xr[:, par, :], tile(X, t), abr[:, lay, :], ALU.add).then_inc(a_xr, 1)
                    if ok(t + 2):
                        pool.wait_ge(a_qk, u + 3)
                        if not (num(u) and u < 0):
                            pool.wait_ge(a_s, 2 * u + 2)
                        pool.tensor_tensor(kexp[:, par, :, :], mid(kT[:, par, :], NH), bc(hmask[:, :].unsqueeze(2), SK),
                                           ALU.mult).then_inc(a_kexp, 1)
                    if ok(t - 1):
                        ln_rstd(ln0 + t - 1, 1 - par, 1)
                steps(pool, step)

            pool.wait_ge(ld_const, 96)
            attention(0, LN_XA0)

            pool.wait_ge(x_ready, LN_MOE)

            def step(j, par):
                t = 2 * j + par
                if ok(t + 1):
                    pool.wait_ge(e_mxp, t + 2)
                    pool.tensor_tensor(tile(EC, t + 1).rearrange("p (n s) -> p n s", s=PS), lgc[:, 1 - par, :].rearrange("p (n s) -> p n s", s=PS),
                                       mid(mxp[:, 1 - par, :], NE), ALU.subtract).then_inc(e_subC, 1)
                if ok(t):
                    pool.wait_ge(e_rD, t + 1)
                    v = slots[:, par, :].rearrange("p (n s) -> p n s", s=PS)
                    pool.tensor_tensor(v, v, bc(rD[:, par, :].unsqueeze(2), PS), ALU.mult).then_inc(e_Dn, 1)
                if ok(t + 1):
                    pool.wait_ge(e_expC, t + 2)
                    if not (num(t) and t < 0):
                        pool.wait_ge(e_sum32, t + 1)
                    c = tile(EC, t + 1)
                    pool.tensor_tensor(fold, c[:, 0:E // 2], c[:, E // 2:E], ALU.add).then_inc(e_fold, 1)
            steps(pool, step)

            for b in range(4):
                mv = sm[:, 8 * b:8 * b + 8].rearrange("p (c n) -> p c n", n=2)
                k = slice(4 * b, 4 * b + 4)
                pool.wait_ge(y_mv, 2 * b + 2)
                pool.tensor_scalar(bve[:, k], mv[:, :, 1], LN_EPS, None, ALU.add)
                pool.tensor_scalar(bnm[:, k], mv[:, :, 0], -1.0, None, ALU.mult).then_inc(y_ve, 1)
                pool.wait_ge(y_ve, 3 * b + 1)
                pool.tensor_tensor(brs[:, k], bve[:, k], mhalf[:, 0:4], ALU.pow).then_inc(y_ve, 1)
                pool.wait_ge(y_ve, 3 * b + 2)
                pool.tensor_tensor(bof[:, k], bnm[:, k], brs[:, k], ALU.mult).then_inc(y_ve, 1)

            pool.wait_ge(e_rC, NT)

            def step(j, par):
                t = 2 * j + par
                if ok(t + 2):
                    if num(t) and t == 1:
                        pool.wait_ge(y_mm, 4)
                    if not (num(t) and t < 2):
                        pool.wait_ge(c_tr, 4 * t + 4)
                    v = tile(EC, t + 2).rearrange("p (n s) -> p n s", s=PS)
                    dst = v if in_place(t + 2) else slots[:, par, :].rearrange("p (n s) -> p n s", s=PS)
                    pool.tensor_tensor(dst, v, mid(tile(rC, t + 2), NE), ALU.mult).then_inc(c_n, 1)
                if ok(t):
                    ln_rstd(LN_MOE + t, par, 1)
            steps(pool, step)

            pool.wait_ge(x_ready, LN_RET)
            pool.wait_ge(ld_ret, 16 * 5)

            def stage(t, par):
                if not (num(t) and t < 2):
                    pool.wait_ge(r_tr, t - 1)
                pool.tensor_copy(xs[:, par, :], tile(X, t)).then_inc(r_xs, 1)

            stage(0, 0)

            def step(j, par):
                t = 2 * j + par
                if ok(t + 3):
                    stage(t + 3, 1 - par)
                if ok(t - 2):
                    ln_rstd(LN_RET + t - 2, par, 1)
                if ok(t):
                    if not (num(t) and t < 2):
                        pool.wait_ge(lny_s, LN_RET + t - 1)
                    pool.tensor_tensor(xr[:, par, :].rearrange("p (h e) -> p h e", e=HD), tile(X, t).rearrange("p (h e) -> p h e", e=HD),
                                       bc(gnb.unsqueeze(2), HD), ALU.add).then_inc(r_xr, 1)
                if ok(t + 2):
                    pool.wait_ge(r_qk, t + 3)
                    if not (num(t) and t < 0):
                        pool.wait_ge(r_s, 2 * t + 2)
                    pool.tensor_tensor(qexp[:, par, :, :], mid(qkT[:, par, 0:P], NH), bc(hmask[:, :].unsqueeze(2), P),
                                       ALU.mult).then_inc(r_qe, 1)
                if ok(t - 1):
                    pool.wait_ge(r_ve, t)
                    pool.tensor_tensor(gsc[:, 1 - par, 3:4], gsc[:, 1 - par, 2:3], mhalf[:, 0:1], ALU.pow).then_inc(r_rs, 1)
            steps(pool, step, NT + 1)

            attention(1, LN_XA1)

            pool.wait_ge(f_w, 1)
            pool.partition_all_reduce(amx[:, 2:4], amx[:, 0:2], P, bass.bass_isa.ReduceOp.max).then_inc(f_w, 1)
            pool.wait_ge(x_ready, LN_FFN)

            def step(j, par):
                g = 2 * j + par
                if not (num(g) and g < 2):
                    pool.wait_ge(f_tr, g - 1)
                    pool.wait_ge(lny_s, LN_FFN + g - 1)
                pool.tensor_copy(fs4[:, par, :, :], tile(X, GT * g, GT)).then_inc(f_xs, 1)
                pool.tensor_tensor(fr4[:, par, :, :], tile(X, GT * g, GT), mid(bpr, GT), ALU.add).then_inc(f_xs, 1)
                if not (num(g) and g == 0):
                    ln_rstd(LN_FFN + g - 1, 1 - par, GT)
            pairs(pool, G, step)
            ln_rstd(LN_FFN + G - 1, 1, GT)

        @block.scalar
        def _(act):
            A = act.activation
            def x_transposed(g):
                act.wait_ge(m_tr, g + 1)
                if g == 0:
                    act.wait_ge(set_v, 1)
                if g >= 2:
                    act.wait_ge(m_mm, 4 * (g - 1))
                act.copy(xTp[:, g % 2, :, KC - 1:], bank[:, 0, :].rearrange("p (j n) -> p j n", j=GT)).then_inc(m_xT, 1)

            def conv_silu(g):
                if g == 0:
                    act.wait_ge(ld_mamba, 16 * 10)
                for c in range(NC):
                    act.wait_ge(m_mm, 4 * g + c + 1)
                    A(xconv[:, c, GW * g:GW * g + GW], bank[:, 1 + c, :], ACT.Silu, bias=convb[:, c:c + 1]).then_inc(m_silu, 1)
                for c in range(NC):
                    act.wait_ge(m_mm, 4 * g + 2 + c + 1)
                    A(sz[:, c, GW * g:GW * g + GW], bank[:, 3 + c, :], ACT.Silu).then_inc(m_silz, 1)

            def steps_soft(g):
                act.wait_ge(m_wx, g + 1)
                if g >= 1:
                    act.wait_ge(m_dtp, 2 * g)
                act.copy(dtin[0:R, :], bank[0:R, 7, :]).then_inc(m_dtin, 1)
                if g >= 1:
                    act.wait_ge(m_dt, g)
                for c in range(NC):
                    act.wait_ge(m_dtp, 2 * g + c + 1)
                    A(sp_l[:, c, :], bank[:, 5 + c, :], ACT.Abs, bias=bdt[:, c:c + 1]).then_inc(m_abs, 1)
                act.wait_ge(m_abs, 2 * g + 2)
                A(sp_l, sp_l, ACT.Exp, scale=-1.0).then_inc(m_ln1, 1)
                act.wait_ge(m_ln1, 2 * g + 1)
                A(sp_l, sp_l, ACT.Ln, bias=1.0).then_inc(m_ln1, 1)
            act.dma_start(w_in, a["L0_attn_W_in"]).then_inc(ld_win, 16)
            act.dma_start(cwb.rearrange("p d k -> p (d k)"),
                          a["L0_attn_conv_w"].rearrange("d k -> (d k)").partition_broadcast(P)).then_inc(ld_win, 16)
            x_transposed(0)
            for g in range(G + 1):
                if g < G:
                    conv_silu(g)
                if g < G - 1:
                    x_transposed(g + 1)
                if g > 0:
                    act.preload_act_table_set("natural_log_exp_and_others")
                    steps_soft(g - 1)
            A(Am, alog, ACT.Exp).then_inc(m_A, 1)

            act.wait_ge(m_A, 2)
            act.wait_ge(m_dtx, G)

            def decays(g):
                for q in range(4):
                    pp = 4 * g + q
                    act.wait_ge(m_B, pp + 1)
                    if not (num(g) and g == 0 and q < 2):
                        act.wait_ge(m_dBx, pp - 1)
                        act.wait_ge(m_dBp, pp - 1)
                    act.copy(Bb[:, q % 2, :].rearrange("p (s n) -> p s n", s=4), bank[:, 0:4, :]).then_inc(m_bc, 1)
                    for c in range(NC):
                        kk = 2 * pp + c
                        if not (num(g) and g == 0 and q == 0):
                            act.wait_ge(m_h, kk - 1)
                            act.sem_inc(passed_act, 1)
                        for i in range(4):
                            n = 4 * q + i
                            ins = A(dA[:, c, GW * i:GW * i + GW], dt_all[:, c, ds(GW * g, GW)], ACT.Exp, scale=Am[:, c, n:n + 1])
                        ins.then_inc(m_dA, 1)
            decays(0)
            with act.Fori(1, G) as g:
                decays(g)

            def attention(lay, ln0):
                def probs(u, par, hf):
                    act.wait_ge(a_sub, 2 * u + hf + 1)
                    v = sc[:, par, 8 * hf:8 * hf + 8, :]
                    if lay == 0:
                        if hf == 0:
                            act.wait_ge(a_esc, u + 1)
                        A(v, v, ACT.Exp, scale=escale[:, par, :]).then_inc(a_exp, 1)
                    else:
                        A(v, v, ACT.Exp, scale=HD ** -0.5).then_inc(a_exp, 1)

                def probsT(u, par, r):
                    act.wait_ge(a_pt, 4 * u + r + 1)
                    if r == 0 and not (num(u) and u < 2):
                        act.wait_ge(a_pv, u - 1)
                    act.copy(pT[0:SK, par, 4 * r:4 * r + 4, :], bank[0:SK, 6 + r % 2, :].rearrange("p (h n) -> p h n", h=4)).then_inc(a_ptc, 1)

                def step(j, par):
                    t = 2 * j + par
                    u = NT * lay + t
                    if ok(t + 2):
                        act.wait_ge(a_tr, u + 3)
                        if not (num(u) and u < 0):
                            act.wait_ge(a_qkv, u + 1)
                        act.copy(xT[:, par, 0:P + SK], bank[:, 1, 0:P + SK]).then_inc(a_xT, 1)
                    if ok(t + 2):
                        act.wait_ge(a_qkv, u + 3)
                        if not (num(u) and u < 0):
                            act.wait_ge(a_s, 2 * u + 2)
                            act.wait_ge(a_kexp, u + 1)
                        A(qT[:, par, :], bank[:, 0, 0:P], ACT.Identity, bias=ab[:, lay, 0:1])
                        A(kT[:, par, :], bank[:, 0, P:P + SK], ACT.Identity, bias=ab[:, lay, 1:2]).then_inc(a_qk, 1)
                    if ok(t + 1):
                        probs(u + 1, 1 - par, 0)
                    if ok(t - 1):
                        act.wait_ge(a_ot, u)
                        if not (num(u) and u < 3):
                            act.wait_ge(a_out, u - 2)
                        act.copy(oT[:, 1 - par, :], bank[:, 1, 0:D]).then_inc(a_otc, 1)
                    if ok(t):
                        probsT(u, par, 0)
                        probsT(u, par, 1)
                        probsT(u, par, 2)
                        probsT(u, par, 3)
                    if ok(t + 1):
                        probs(u + 1, 1 - par, 1)
                    if ok(t):
                        act.wait_ge(a_pv, u + 1)
                        if not (num(u) and u < 2):
                            act.wait_ge(a_sel, u - 1)
                        act.copy(poT[:, par, :, :], bank[:, 6, :].rearrange("p (r n) -> p r n", r=4)).then_inc(a_po, 1)
                steps(act, step)

            act.wait_ge(ld_attn, 16 * 12)
            attention(0, LN_XA0)

            for b in range(4):
                act.wait_ge(set_w, 3 + b)
                act.copy(phiT[:, 512 * b:512 * b + 512], bank[:, b, :]).then_inc(e_phi, 1)

            def stage(t, par):
                if not (num(t) and t < 2):
                    act.wait_ge(e_tr, t - 1)
                    act.sem_inc(passed_act, 1)
                act.copy(xs[:, par, :], tile(X, t)).then_inc(e_xs, 1)
            stage(0, 0)

            def step(j, par):
                t = 2 * j + par
                if ok(t + 2):
                    act.wait_ge(e_tr, t + 3)
                    if not (num(t) and t < 0):
                        act.wait_ge(e_log, 4 * t + 4)
                    act.copy(xT[:, par, 0:P], bank[:, 2, 0:P]).then_inc(e_xT, 1)
                if ok(t + 3):
                    stage(t + 3, 1 - par)
                if ok(t + 2):
                    if not (num(t) and t < 0):
                        act.wait_ge(e_subD, t + 1)
                        act.wait_ge(e_subC, t + 1)
                    for b in range(4):
                        act.wait_ge(e_log, 4 * (t + 2) + b + 1)
                        act.copy(lgc[:, par, 512 * b:512 * b + 512], bank[:, b % 2, :]).then_inc(e_lgc, 1)
                if ok(t + 1):
                    act.wait_ge(e_subC, t + 2)
                    act.sem_inc(passed_act, 1)
                    A(tile(EC, t + 1), tile(EC, t + 1), ACT.Exp).then_inc(e_expC, 1)
                    act.wait_ge(e_subD, t + 2)
                    A(slots[:, 1 - par, :], slots[:, 1 - par, :], ACT.Exp).then_inc(e_expD, 1)
            steps(act, step)

            def xtl_T(b):
                act.wait_ge(y_tr, b + 1)
                act.copy(xtlT[:, 4 * b:4 * b + 4, :], bank[:, b, :].rearrange("p (c n) -> p c n", c=4)).then_inc(y_trc, 1)

            for b in range(4):
                act.wait_ge(y_ve, 3 * b + 3)
                for c in range(4 * b, 4 * b + 4):
                    ins = A(xtl[:, c, :], xtl[:, c, :], ACT.Tanh, bias=bof[:, c:c + 1], scale=brs[:, c:c + 1])
                ins.then_inc(y_tanh, 1)
                if b > 0:
                    xtl_T(b - 1)
            xtl_T(3)

            act.wait_ge(y_out, 4)

            def step(j, par):
                t = 2 * j + par
                if ok(t + 1):
                    for b in range(2):
                        act.wait_ge(c_tr, 4 * (t + 1) + b + 1)
                        if b == 0 and not (num(t) and t < 1):
                            act.wait_ge(c_y, t)
                        act.copy(slotsT[:, 1 - par, 4 * b:4 * b + 4, :], bank[:, b, :].rearrange("p (c n) -> p c n", c=4)).then_inc(c_ca, 1)
            steps(act, step)

            act.wait_ge(x_ready, LN_RET)

            def step(j, par):
                t = 2 * j + par
                if ok(t + 2):
                    act.wait_ge(r_tr, t + 3)
                    if not (num(t) and t < 0):
                        act.wait_ge(r_qkv, t + 1)
                    act.copy(xT[:, par, 0:P], bank[:, 1, 0:P]).then_inc(r_xT, 1)
                if ok(t + 1):
                    act.wait_ge(r_cr, t + 2)
                    if not (num(t) and t < 1):
                        act.wait_ge(r_r, t)
                    act.copy(crs[:, 1 - par, :], bank[:, 0, 3 * P:4 * P]).then_inc(r_crc, 1)
                if ok(t + 2):
                    act.wait_ge(r_qkv, t + 3)
                    if not (num(t) and t < 0):
                        act.wait_ge(r_s, 2 * t + 2)
                        act.wait_ge(r_qe, t + 1)
                        act.wait_ge(r_cr, t + 1)
                    act.copy(qkT[:, par, :], bank[:, 0, 0:2 * P]).then_inc(r_qk, 1)
                if ok(t):
                    act.wait_ge(r_pv, t + 1)
                    if not (num(t) and t < 2):
                        act.wait_ge(r_sel, t - 1)
                    act.copy(rpo[:, par, :, :], bank[:, 6, :].rearrange("p (r n) -> p r n", r=4)).then_inc(r_po, 1)
            steps(act, step)

            act.wait_ge(set_w, 7)
            act.copy(wa[:, 1, :, :], bank[:, 0, :].rearrange("p (i n) -> p i n", i=4)).then_inc(set_w, 1)
            act.preload_act_table_set("exp_and_others")
            attention(1, LN_XA1)

            act.wait_ge(f_wt, 1)
            act.copy(bT[0:R, 0:FF], bank[0:R, 0, :]).then_inc(f_wc, 1)
            act.wait_ge(f_wt, 2)
            act.copy(bT[0:R, FF:FF + D], bank[0:R, 1, 0:D]).then_inc(f_wc, 1)
            act.wait_ge(f_wt, 3)
            act.copy(w1T, bank[:, 2, :]).then_inc(f_wc, 1)
            act.wait_ge(f_wt, 4)
            act.copy(w2T, bank[:, 3, :].rearrange("p (c n) -> p c n", c=FC)).then_inc(f_wc, 1)

            def step(j, par):
                g = 2 * j + par
                act.wait_ge(f_tr, g + 1)
                if not (num(g) and g < 2):
                    act.wait_ge(f_h, 4 * (g - 1))
                act.copy(fxT[:, par, :], bank[:, 0, :]).then_inc(f_xT, 1)
                for c in range(FC):
                    act.wait_ge(f_h, 4 * g + c + 1)
                    if c == 0 and not (num(g) and g < 2):
                        act.wait_ge(f_o, g - 1)
                    A(hT[:, par, c, :], bank[:, 2 + c, :], ACT.Gelu, bias=bfcr[:, c:c + 1]).then_inc(f_g, 1)
            pairs(act, G, step)

        @block.vector
        def _(dve):
            TT, TS, STT, RED = dve.tensor_tensor, dve.tensor_scalar, dve.scalar_tensor_tensor, dve.tensor_reduce

            def ln_stats(e, par, acc, res, k):
                y = lny[:, par, 0:k, :] if k > 1 else lny[:, par, 0, :]
                TT(y, acc, res, ALU.add).then_inc(lny_s, 1)
                dve.wait_ge(lny_s, e + 1)
                for i in range(k):
                    ins = dve.bn_stats(lnst[:, par, i, :], lny[:, par, i, :])
                ins.then_inc(lnst_s, 1)
                dve.wait_ge(lnst_s, e + 1)
                dve.sem_inc(passed_dve, 1)
                for i in range(k):
                    ins = dve.bn_aggr(lnmv[:, par, i, :], lnst[:, par, i, :])
                ins.then_inc(lnmv_s, 1)

            def ln_norm(e, par, t, k):
                dve.wait_ge(lnrs_s, e + 1)
                for i in range(k):
                    ins = TS(tile(X, t + i), lny[:, par, i, :], lnmv[:, par, i, 0:1], lnrs[:, par, i:i + 1], ALU.subtract, ALU.mult)
                ins.then_inc(x_ready, 1)

            dve.memset(wx, 0.0).then_inc(set_w, 1)
            dve.memset(xTp[:, :, :, 0:KC - 1], 0.0)
            dve.wait_ge(ld_win, 32)
            for k in range(KC):
                ins = TT(wk[:, k, :], w_in[:, 0:DI], cwb[:, :, k], ALU.mult)
            ins.then_inc(set_v, 1)
            dve.wait_ge(ld_const, 96)
            dve.tensor_copy(identb[:, :], ident[:, :])
            dve.tensor_copy(sel, bc(selcol[:, :].unsqueeze(2), P))
            dve.wait_ge(ld_mamba, 16 * 10)

            for g in range(G):
                gw = slice(GW * g, GW * g + GW)
                n = 3 * g
                dve.wait_ge(m_dtin, g + 1)
                dve.tensor_copy(Bs[:, gw], bank[:, 7, :]).then_inc(m_split, 1)
                dve.wait_ge(m_split, n + 1)
                TT(bres, bank[:, 7, :], Bs[:, gw], ALU.subtract).then_inc(m_split, 1)
                dve.wait_ge(m_split, n + 2)
                dve.tensor_copy(Bs[64:128, gw], bres[64:128, :]).then_inc(m_split, 1)
                dve.wait_ge(m_split, n + 3)
                TT(Bs[96:128, gw], bres[96:128, :], Bs[96:128, gw], ALU.subtract).then_inc(m_bs, 1)
                dve.wait_ge(m_abs, 2 * g + 2)
                for c in range(NC):
                    ins = TS(sp_r[:, c, :], bank[:, 5 + c, :], bdt[:, c:c + 1], 0.0, ALU.add, ALU.max)
                ins.then_inc(m_relu, 1)
                dve.wait_ge(m_relu, g + 1)
                dve.wait_ge(m_ln1, 2 * g + 2)
                TT(dt_all[:, :, gw], sp_r, sp_l, ALU.add).then_inc(m_dt, 1)
                dve.wait_ge(m_dt, g + 1)
                TT(dtx_all[:, :, gw], dt_all[:, :, gw], xconv[:, :, gw], ALU.mult).then_inc(m_dtx, 1)
            dve.wait_ge(m_A, 1)
            TS(Am, Am, -1.0, None, ALU.mult).then_inc(m_A, 1)
            dve.wait_ge(m_dtx, G)

            def times_B(g, q):
                pp = 4 * g + q
                dve.wait_ge(m_bc, pp + 1)
                if not (num(g) and g == 0 and q < 2):
                    dve.wait_ge(m_sum, 2 * pp - 3)
                TT(hb[2 * q % 4].rearrange("p (s n) -> p s n", s=4), Bb[:, q % 2, :].rearrange("p (s n) -> p s n", s=4),
                   mid(dtx_all[:, 0, ds(GW * g, GW)], 4), ALU.mult).then_inc(m_dBx, 1)

            def scan(g, q, c):
                pp = 4 * g + q
                dve.wait_ge(m_dz, 2 * pp + c + 1)
                dve.wait_ge((m_dBx, m_dBp)[c], pp + 1)
                h = hb[(2 * q + c) % 4]
                dve.tensor_tensor_scan(h, dA[:, c, :], h, 0.0, ALU.mult, ALU.add).then_inc(m_h, 1)

            def gate(g, c):
                dve.wait_ge(m_sum, 8 * g + 6 + c + 1)
                if not (num(g) and g == 0):
                    dve.wait_ge(m_o, g)
                n = 4 * g + 2 * c
                STT(yTm[:, c, :], xconv[:, c, ds(GW * g, GW)], Dv[:, c:c + 1], bank[:, 4 + c, :], ALU.mult, ALU.add).then_inc(m_y, 1)
                dve.wait_ge(m_y, n + 1)
                TT(yTm[:, c, :], yTm[:, c, :], sz[:, c, ds(GW * g, GW)], ALU.mult).then_inc(m_y, 1)

            def block_stats(g, par):
                dve.wait_ge(m_o, g + 1)
                ln_stats(g, par, bank[:, 7, :].rearrange("p (j n) -> p j n", j=GT), tile(X, GT * g, GT), GT)

            def group(g, par):
                for q in range(4):
                    times_B(g, q)
                    scan(g, q, 0)
                    if not (num(g) and g == 0):
                        if q == 0:
                            gate(g - 1, 0)
                            gate(g - 1, 1)
                        if q == 1:
                            block_stats(g - 1, 1 - par)
                        if q == 3:
                            ln_norm(g - 1, 1 - par, GT * (g - 1), GT)
                    scan(g, q, 1)
            dve.wait_ge(ld_x, 16)
            pairs(dve, G, lambda j, par: group(2 * j + par, par))
            gate(G - 1, 0)
            gate(G - 1, 1)
            block_stats(G - 1, 1)
            ln_norm(G - 1, 1, GT * (G - 1), GT)

            def attention(lay, ln0):
                def mask_bias(j, par, t):
                    dve.wait_ge(ld_mask[par], 16 * (j + 1))
                    if not (num(t) and t < 2):
                        dve.wait_ge(a_s, 2 * (t - 1))
                        dve.wait_ge(a_exp, 2 * (t - 1))
                    TS(mflag[:, par, :], maskb[:, par, :], 0.0, None, ALU.is_equal).then_inc(a_flag, 1)
                    dve.wait_ge(a_flag, 2 * t + 1)
                    TS(mbias[:, par, :], mflag[:, par, :], MASKED, None, ALU.mult).then_inc(a_mb, 1)
                    RED(allm[:, par, :], mflag[:, par, :], AX.X, ALU.min).then_inc(a_flag, 1)
                    dve.wait_ge(a_flag, 2 * t + 2)
                    TS(escale[:, par, :], allm[:, par, :], -(HD ** -0.5), HD ** -0.5, ALU.mult, ALU.add).then_inc(a_esc, 1)

                def shift(u, par, hf):
                    dve.wait_ge(a_s, 2 * u + hf + 1)
                    if hf == 0 and not (num(u) and u < 2):
                        dve.wait_ge(a_pt, 4 * (u - 1))
                    s = bank[:, 2 + 2 * hf:4 + 2 * hf, 0:4 * SK].rearrange("p b (h n) -> p b h n", h=4)
                    m = nmx[:, par, 8 * hf:8 * hf + 8, :].rearrange("p (b h) n -> p b h n", b=2)
                    RED(m.rearrange("p b h n -> p b (h n)"), s, AX.X, ALU.max).then_inc(a_max, 1)
                    dve.wait_ge(a_max, 2 * u + hf + 1)
                    TT(sc[:, par, 8 * hf:8 * hf + 8, :].rearrange("p (b h) n -> p b h n", b=2), s,
                       m.to_broadcast([P, 2, 4, SK]), ALU.subtract).then_inc(a_sub, 1)

                dve.wait_ge(a_bvo, lay + 1)
                TT(abr[:, lay, :], abr[:, lay, :], bank[:, 7, 0:D], ALU.add).then_inc(a_bias, 1)
                dve.memset(vaug[:, :, :, HD + 1:32], 0.0)
                dve.memset(vaug[:, :, :, HD:HD + 1], 1.0)

                def step(j, par):
                    t = 2 * j + par
                    u = NT * lay + t
                    if ok(t + 1):
                        shift(u + 1, 1 - par, 0)
                    if ok(t - 1):
                        dve.wait_ge(a_sel, u)
                        o = bank[:, 1, 0:NH * (HD + 1)].rearrange("p (h n) -> p h n", h=NH)
                        dve.reciprocal(rden[:, 1 - par, :, :], o[:, :, HD:HD + 1]).then_inc(a_rden, 1)
                        dve.wait_ge(a_rden, u)
                        if not (num(u) and u < 3):
                            dve.wait_ge(a_ot, u - 2)
                        TT(on[:, 1 - par, :].rearrange("p (h n) -> p h n", h=NH), o[:, :, 0:HD], bc(rden[:, 1 - par, :, :], HD), ALU.mult).then_inc(a_on, 1)
                    if ok(t + 1):
                        shift(u + 1, 1 - par, 1)
                    if ok(t - 2):
                        ln_norm(ln0 + t - 2, par, t - 2, 1)
                    if ok(t - 1):
                        dve.wait_ge(a_out, u)
                        dve.wait_ge(a_xr, u)
                        ln_stats(ln0 + t - 1, 1 - par, bank[:, 1, 0:D], xr[:, 1 - par, :], 1)
                    if ok(t + 2):
                        if lay == 0:
                            mask_bias(j + 1, par, t + 2)
                        dve.wait_ge(a_qk, u + 3)
                        if not (num(u) and u < 0):
                            dve.wait_ge(a_pv, u + 1)
                        dve.tensor_copy(vaug[0:SK, par, :, 0:HD], bank[0:SK, 0, 256:384].rearrange("p (h n) -> p h n", h=NH)).then_inc(a_v, 1)
                steps(dve, step)
                ln_norm(ln0 + NT - 1, 1, NT - 1, 1)

            dve.wait_ge(ld_attn, 16 * 12)
            dve.memset(slots[:, 0, :], 0.0).then_inc(set_w, 1)
            attention(0, LN_XA0)

            dve.wait_ge(ld_moe, 64)
            dve.tensor_copy(phib[:, :], slots[:, 0, :]).then_inc(e_pb, 1)
            dve.wait_ge(e_pb, 1)
            TT(slots[:, 1, :], slots[:, 0, :], phib[:, :], ALU.subtract).then_inc(e_pb, 1)
            dve.wait_ge(e_pb, 2)
            dve.tensor_copy(phib[64:128, :], slots[64:128, 1, :]).then_inc(e_pb, 1)
            dve.wait_ge(e_pb, 3)
            TT(phib[96:128, :], slots[96:128, 1, :], phib[96:128, :], ALU.subtract).then_inc(e_pb, 1)
            dve.wait_ge(e_pb, 4)

            def step(j, par):
                t = 2 * j + par
                lg = lgc[:, 1 - par, :].rearrange("p (n s) -> p n s", s=PS)
                if ok(t + 1):
                    dve.wait_ge(e_lgc, 4 * (t + 1) + 4)
                    if not (num(t) and t < 1):
                        dve.wait_ge(e_rC, t)
                    RED(mxp[:, 1 - par, :], lg.rearrange("p n s -> p s n"), AX.X, ALU.max).then_inc(e_mxp, 1)
                if ok(t):
                    dve.wait_ge(e_expD, t + 1)
                    RED(mxn[:, par, :], slots[:, par, :].rearrange("p (n s) -> p n s", s=PS), AX.X, ALU.add).then_inc(e_sum, 1)
                    dve.wait_ge(e_sum, t + 1)
                    dve.reciprocal(rD[:, par, :], mxn[:, par, :]).then_inc(e_rD, 1)
                if ok(t + 1):
                    if not (num(t) and t < 1):
                        dve.wait_ge(e_rD, t)
                    RED(mxn[:, 1 - par, :], lg, AX.X, ALU.max).then_inc(e_mxn, 1)
                    dve.wait_ge(e_mxn, t + 2)
                    if not (num(t) and t < 1):
                        dve.wait_ge(e_xt, t)
                    TT(slots[:, 1 - par, :].rearrange("p (n s) -> p n s", s=PS), lg, bc(mxn[:, 1 - par, :].unsqueeze(2), PS), ALU.subtract).then_inc(e_subD, 1)
                if ok(t):
                    dve.wait_ge(e_sum32, t + 1)
                    RED(mxp[:, par, :], bank[:, 3, :].rearrange("p (n s) -> p s n", s=PS), AX.X, ALU.add).then_inc(e_sumC, 1)
                    dve.wait_ge(e_sumC, t + 1)
                    dve.reciprocal(tile(rC, t), mxp[:, par, :]).then_inc(e_rC, 1)
            steps(dve, step)

            bst = lny[:, :, :, :].rearrange("p b j n -> p (b j n)")[:, 0:EC_N * 6].rearrange("p (c n) -> p c n", n=6)
            for b in range(4):
                dve.wait_ge(y_xt, b + 1)
                TS(xtl[:, 4 * b:4 * b + 4, :], bank[:, 4 + b, :].rearrange("p (c n) -> p c n", n=D), -33000.0, 65000.0, ALU.max, ALU.min).then_inc(y_clip, 1)
                dve.wait_ge(y_clip, b + 1)
                for c in range(4 * b, 4 * b + 4):
                    ins = dve.bn_stats(bst[:, c, :], xtl[:, c, :])
                ins.then_inc(y_mv, 1)
                dve.wait_ge(y_mv, 2 * b + 1)
                for c in range(4 * b, 4 * b + 4):
                    ins = dve.bn_aggr(sm[:, 2 * c:2 * c + 2], bst[:, c, :])
                ins.then_inc(y_mv, 1)
            for b in range(4):
                dve.wait_ge(y_mm, b + 1)
                dve.tensor_copy(Yt[:, 4 * b:4 * b + 4, :], bank[:, 4 + b, :].rearrange("p (c n) -> p c n", n=D)).then_inc(y_out, 1)

            def step(j, par):
                t = 2 * j + par
                if ok(t + 1):
                    for b in range(2, 4):
                        dve.wait_ge(c_tr, 4 * (t + 1) + b + 1)
                        if b == 2 and not (num(t) and t < 1):
                            dve.wait_ge(c_y, t)
                        dve.tensor_copy(slotsT[:, 1 - par, 4 * b:4 * b + 4, :], bank[:, b, :].rearrange("p (c n) -> p c n", c=4)).then_inc(c_cv, 1)
                if ok(t - 1):
                    ln_norm(LN_MOE + t - 1, 1 - par, t - 1, 1)
                if ok(t):
                    dve.wait_ge(c_y, t + 1)
                    ln_stats(LN_MOE + t, par, bank[:, 4 + par, 0:D], tile(X, t), 1)
            steps(dve, step)

            dve.wait_ge(ld_ret, 16 * 5)
            STT(kvbd.rearrange("p (h e) -> p h e", e=HD), mid(kvl, NH), float(NH * HD), bc(hmask[:, :].unsqueeze(2), HD), ALU.mult, ALU.mult).then_inc(set_v, 1)

            dve.memset(vpad[:, :, :, HD:32], 0.0)

            def decayed(t, par, hf):
                dve.wait_ge(r_s, 2 * t + hf + 1)
                if hf == 0 and not (num(t) and t < 2):
                    dve.wait_ge(r_pv, t - 1)
                TT(rd[:, par, 8 * hf:8 * hf + 8, :].rearrange("p (b h) n -> p b (h n)", b=2), bank[:, 2 + 2 * hf:4 + 2 * hf, :],
                   decay[:, 8 * hf:8 * hf + 8, :].rearrange("p (b h) n -> p b (h n)", b=2), ALU.mult).then_inc(r_rd, 1)

            def step(j, par):
                t = 2 * j + par
                q = 1 - par
                if ok(t - 2):
                    dve.wait_ge(r_rs, t - 1)
                    TS(gt1[:, par, :], gr[:, par, :], gsc[:, par, 0:1], gsc[:, par, 3:4], ALU.subtract, ALU.mult).then_inc(r_t1, 1)
                    dve.wait_ge(r_t1, t - 1)
                    TT(gt2[:, par, :].rearrange("p (h e) -> p h e", e=HD), gt1[:, par, :].rearrange("p (h e) -> p h e", e=HD),
                       bc(gnw.unsqueeze(2), HD), ALU.mult).then_inc(r_t2, 1)
                    dve.wait_ge(r_t2, t - 1)
                    dve.wait_ge(r_xr, t - 1)
                    ln_stats(LN_RET + t - 2, par, gt2[:, par, :], xr[:, par, :], 1)
                if ok(t - 1):
                    dve.wait_ge(r_sel, t)
                    dve.wait_ge(r_crc, t)
                    TT(gr[:, q, :], bank[:, 7, 0:D], crs[:, q, :], ALU.add).then_inc(r_r, 1)
                    dve.wait_ge(r_r, t)
                    dve.bn_stats(gst[:, q, :], gr[:, q, :]).then_inc(r_st, 1)
                    dve.wait_ge(r_st, t)
                    dve.sem_inc(passed_dve, 1)
                    dve.bn_aggr(gmv[:, q, :], gst[:, q, :]).then_inc(r_mv, 1)
                if ok(t + 1):
                    decayed(t + 1, q, 0)
                if ok(t - 1):
                    dve.wait_ge(r_m1, t)
                    dve.tensor_copy(gsc[:, q, 0:1], bank[:, 7, P:P + 1]).then_inc(r_d, 1)
                    dve.wait_ge(r_d, 2 * t - 1)
                    TT(gsc[:, q, 1:2], gmv[:, q, 0:1], gsc[:, q, 0:1], ALU.subtract).then_inc(r_d, 1)
                    dve.wait_ge(r_d, 2 * t)
                    TS(gmv[:, q, 0:1], gsc[:, q, 1:2], gsc[:, q, 1:2], gmv[:, q, 1:2], ALU.mult, ALU.add).then_inc(r_v2, 1)
                if ok(t + 1):
                    decayed(t + 1, q, 1)
                if ok(t + 2):
                    dve.wait_ge(r_qk, t + 3)
                    if not (num(t) and t < 0):
                        dve.wait_ge(r_pv, t + 1)
                    dve.tensor_copy(vpad[:, par, :, 0:HD], bank[:, 0, 2 * P:3 * P].rearrange("p (h n) -> p h n", h=NH)).then_inc(r_v, 1)
                if ok(t - 1):
                    dve.wait_ge(r_m2, t)
                    TS(gsc[:, q, 2:3], bank[:, 7, P + 1:P + 2], LN_EPS, None, ALU.add).then_inc(r_ve, 1)
                if ok(t - 2):
                    ln_norm(LN_RET + t - 2, par, t - 2, 1)
            steps(dve, step, NT + 1)


            attention(1, LN_XA1)

            dve.wait_ge(ld_ffn, 16 * 8)
            RED(amx[:, 0:1], wf1.rearrange("p c n -> p (c n)"), AX.X, ALU.max, apply_absolute_value=True)
            RED(amx[:, 1:2], wf2, AX.X, ALU.max, apply_absolute_value=True).then_inc(f_w, 1)
            dve.wait_ge(f_w, 2)
            TS(amx[:, 4:6], amx[:, 2:4], 1.0 / QMAX, None, ALU.mult).then_inc(f_wp, 1)
            dve.wait_ge(f_wp, 1)
            dve.reciprocal(amx[:, 6:8], amx[:, 4:6]).then_inc(f_wp, 1)
            dve.wait_ge(f_wp, 2)
            n = 2
            for i, (w, tq) in enumerate(((wf1.rearrange("p c n -> p (c n)"), tq1), (wf2, tq2))):
                TS(tq, w, amx[:, 6 + i:7 + i], ROUND, ALU.mult, ALU.add).then_inc(f_wp, 1)
                dve.wait_ge(f_wp, n + 1)
                TS(tq, tq, ROUND, QMAX, ALU.subtract, ALU.min).then_inc(f_wp, 1)
                dve.wait_ge(f_wp, n + 2)
                TS(tq, tq, -QMAX - 1.0, amx[:, 4 + i:5 + i], ALU.max, ALU.mult).then_inc(f_wp, 1)
                dve.wait_ge(f_wp, n + 3)
                TT(tq, tq, w, ALU.subtract).then_inc(f_wp, 1)
                dve.wait_ge(f_wp, n + 4)
                TT(w, w, tq, ALU.add).then_inc(f_wp, 1)
                n += 5
            TS(afc[0:R, :], afc[0:R, :], 2.0, None, ALU.mult)
            TS(apj[0:R, :], apj[0:R, :], 2.0, None, ALU.mult).then_inc(f_wp, 1)

            def step(j, par):
                g = 2 * j + par
                if not (num(g) and g == 0):
                    ln_norm(LN_FFN + g - 1, 1 - par, GT * (g - 1), GT)
                dve.wait_ge(f_o, g + 1)
                dve.wait_ge(f_xs, 2 * g + 2)
                ln_stats(LN_FFN + g, par, bank[:, 6 + par, :].rearrange("p (j n) -> p j n", j=GT), fr4[:, par, :, :], GT)
            pairs(dve, G, step)
            ln_norm(LN_FFN + G - 1, 1, GT * (G - 1), GT)

        @block.tensor
        def _(pe):
            MM = pe.matmul
            I = ident[:, :]
            def transpose_x(g):
                par = g % 2
                pe.wait_ge(ld_xs4[par], 16 * (g // 2 + 1))
                if g >= 1:
                    pe.wait_ge(m_xT, g)
                for j in range(GT):
                    ins = pe.transpose(bank[:, 0, P * j:P * j + P], xs4[:, par, j, :], I)
                ins.then_inc(m_tr, 1)

            def project(g):
                par = g % 2
                pe.wait_ge(m_xT, g + 1)
                if g == 0:
                    pe.wait_ge(set_v, 1)
                for c in range(NC):
                    if g >= 1:
                        pe.wait_ge(m_silu, 2 * (g - 1) + c + 1)
                    for k in range(KC):
                        ins = MM(bank[:, 1 + c, :], wk[:, k, P * c:P * c + P], xTp[:, par, :, k:k + P], start=(k == 0), stop=(k == KC - 1))
                    ins.then_inc(m_mm, 1)
                for c in range(NC):
                    if g >= 1:
                        pe.wait_ge(m_silz, 2 * (g - 1) + c + 1)
                    MM(bank[:, 3 + c, :], w_in[:, DI + P * c:DI + P * c + P], xTp[:, par, :, KC - 1:], start=True, stop=True).then_inc(m_mm, 1)

            def steps_and_B(g):
                gw = slice(GW * g, GW * g + GW)
                pe.wait_ge(m_silu, 2 * g + 2)
                if g >= 1:
                    pe.wait_ge(m_bs, g)
                for c in range(NC):
                    ins = MM(bank[:, 7, :], wx[:, c, :], xconv[:, c, gw], start=(c == 0), stop=(c == NC - 1))
                ins.then_inc(m_wx, 1)
                pe.wait_ge(m_dtin, g + 1)
                if g >= 1:
                    pe.wait_ge(m_relu, g)
                for c in range(NC):
                    MM(bank[:, 5 + c, :], wdt[0:R, P * c:P * c + P], dtin[0:R, :], start=True, stop=True).then_inc(m_dtp, 1)

            pe.wait_ge(ld_const, 96)
            transpose_x(0)
            for g in range(G + 1):
                if g < G:
                    project(g)
                if g < G - 1:
                    transpose_x(g + 1)
                if g > 0:
                    steps_and_B(g - 1)

            def spread(g, q):
                pp = 4 * g + q
                if not (num(g) and g == 0 and q == 0):
                    pe.wait_ge(m_bc, pp)
                for i in range(4):
                    ins = MM(bank[:, i, :], sel[:, 4 * q + i, :], Bs[:, ds(GW * g, GW)], start=True, stop=True)
                ins.then_inc(m_B, 1)

            def sum_states(g, q):
                for c in range(NC):
                    pe.wait_ge(m_h, 8 * g + 2 * q + c + 1)
                    if q == 0 and not (num(g) and g == 0):
                        pe.wait_ge(m_y, 4 * (g - 1) + 2 * c + 1)
                    for i in range(4):
                        ins = MM(bank[:, 4 + c, :], I, hb[(2 * q + c) % 4][:, GW * i:GW * i + GW],
                                 start=(q == 0 and i == 0), stop=(q == 3 and i == 3))
                    ins.then_inc(m_sum, 1)

            def project_out(g):
                pe.wait_ge(m_y, 4 * g + 4)
                if not (num(g) and g == 0):
                    pe.wait_ge(lny_s, g)
                for j in range(GT):
                    for c in range(NC):
                        ins = MM(bank[:, 7, P * j:P * j + P], yTm[:, c, P * j:P * j + P], wout[:, c, :], start=(c == 0), stop=(c == NC - 1))
                ins.then_inc(m_o, 1)

            def scans(g):
                for q in range(4):
                    spread(g, q)
                    if q > 0:
                        sum_states(g, q - 1)
                    elif not (num(g) and g == 0):
                        sum_states(g - 1, 3)
                    if q == 1 and not (num(g) and g == 0):
                        project_out(g - 1)
            pe.wait_ge(m_bs, G)
            pe.wait_ge(m_dtx, G)
            scans(0)
            scans(1)
            with pe.Fori(2, G) as g:
                scans(g)
            sum_states(G - 1, 3)
            project_out(G - 1)

            def attention(lay, ln0):
                wq, wkk, wv, wo = (wa[:, lay, i, :] for i in range(4))
                MM(bank[:, 7, 0:D], ab[:, lay, 2:3].to_broadcast([P, P]), wo, start=True, stop=True).then_inc(a_bvo, 1)
                pe.wait_ge(a_bias, lay + 1)

                def scores(u, par, hf):
                    if hf == 0:
                        pe.wait_ge(a_kexp, u + 1)
                        if lay == 0:
                            pe.wait_ge(a_mb, u + 1)
                    if not (num(u) and u == 0):
                        pe.wait_ge(a_sub, 2 * (u - 1) + hf + 1)
                    for b in (2 * hf, 2 * hf + 1):
                        ins = MM(bank[:, 2 + b, 0:4 * SK], qT[:, par, :], kexp[:, par, 4 * b:4 * b + 4, :], start=True, stop=(lay == 1))
                        if lay == 0:
                            ins = MM(bank[:, 2 + b, 0:4 * SK].rearrange("p (h n) -> p h n", h=4), identb[:, :], mid(mbias[:, par, :], 4), start=False, stop=True)
                    ins.then_inc(a_s, 1)

                def step(j, par):
                    t = 2 * j + par
                    u = NT * lay + t
                    if ok(t + 2):
                        pe.wait_ge(a_xs, u + 3)
                        pe.wait_ge(ld_ctx[par], 16 * (8 * lay + j + 2))
                    if not (num(t) and t < 2):
                        pe.wait_ge(lny_s, ln0 + t - 1)
                    if ok(t + 2):
                        pe.transpose(bank[:, 1, 0:P], xs[:, par, :], I)
                        pe.transpose(bank[:, 1, P:P + SK], ctxb[0:SK, par, :], ident[0:SK, 0:SK]).then_inc(a_tr, 1)
                    if ok(t + 1):
                        scores(u + 1, 1 - par, 0)
                    if ok(t + 2):
                        pe.wait_ge(a_xT, u + 3)
                        if not (num(u) and u < -1):
                            pe.wait_ge(a_qk, u + 2)
                            pe.wait_ge(a_v, u + 2)
                        MM(bank[:, 0, 0:P], wq, xT[:, par, 0:P], start=True, stop=True)
                        MM(bank[:, 0, P:P + SK], wkk, xT[:, par, P:P + SK], start=True, stop=True)
                        MM(bank[0:SK, 0, 256:384], xT[:, par, P:P + SK], wv, start=True, stop=True).then_inc(a_qkv, 1)
                    if ok(t - 1):
                        pe.wait_ge(a_po, u)
                        for r in range(4):
                            ins = MM(bank[:, 1, 36 * r:36 * r + 36], poT[:, 1 - par, r, :], sel9[:, :], start=True, stop=True)
                        ins.then_inc(a_sel, 1)
                    if ok(t + 1):
                        scores(u + 1, 1 - par, 1)
                    if ok(t - 1):
                        pe.wait_ge(a_on, u)
                        pe.transpose(bank[:, 1, 0:D], on[:, 1 - par, :], I).then_inc(a_ot, 1)
                    if ok(t - 1):
                        pe.wait_ge(a_otc, u)
                        MM(bank[:, 1, 0:D], oT[:, 1 - par, :], wo, start=True, stop=True).then_inc(a_out, 1)
                    if ok(t):
                        for r in range(4):
                            if r % 2 == 0:
                                pe.wait_ge(a_exp, 2 * u + r // 2 + 1)
                            if r == 0 and not (num(u) and u == 0):
                                pe.wait_ge(a_po, u)
                            if r > 0 and not (num(u) and u == 0 and r == 1):
                                pe.wait_ge(a_ptc, 4 * u + r - 1)
                            for i in range(4):
                                ins = pe.transpose(bank[0:SK, 6 + r % 2, P * i:P * i + P], sc[:, par, 4 * r + i, :], I)
                            ins.then_inc(a_pt, 1)
                        pe.wait_ge(a_v, u + 1)
                        for r in range(4):
                            if r in (0, 3):
                                pe.wait_ge(a_ptc, 4 * u + (3 if r == 0 else 4))
                            for i in range(4):
                                ins = MM(bank[32 * i:32 * i + 32, 6, P * r:P * r + P], vaug[0:SK, par, 4 * r + i, :], pT[0:SK, par, 4 * r + i, :],
                                         start=True, stop=True, skip_group_check=True)
                        ins.then_inc(a_pv, 1)
                steps(pe, step)

            pe.wait_ge(ld_attn, 16 * 12)
            pe.wait_ge(x_ready, LN_XA0)
            attention(0, LN_XA0)

            pe.wait_ge(x_ready, LN_MOE)
            pe.wait_ge(ld_moe, 64)
            for b in range(4):
                for i in range(4):
                    ins = pe.transpose(bank[:, b, P * i:P * i + P], phir[:, 4 * b + i, :], I)
                ins.then_inc(set_w, 1)
            pe.wait_ge(e_phi, 4)
            pe.wait_ge(e_pb, 4)

            def step(j, par):
                t = 2 * j + par
                if ok(t + 2):
                    pe.wait_ge(e_xs, t + 3)
                    if not (num(t) and t < -1):
                        pe.wait_ge(e_xT, t + 2)
                    pe.transpose(bank[:, 2, 0:P], xs[:, par, :], I).then_inc(e_tr, 1)
                if ok(t - 1):
                    pe.wait_ge(e_Dn, t)
                    for c in range(EC_N):
                        ins = MM(bank[:, 4 + c // 4, P * (c % 4):P * (c % 4) + P], slots[:, 1 - par, P * c:P * c + P], tile(X, t - 1),
                                 start=(num(t) and t == 1 and c % 4 == 0), stop=(num(t) and t == NT), skip_group_check=True)
                        if num(t) and t == NT and c % 4 == 3:
                            ins.then_inc(y_xt, 1)
                    if not (num(t) and t == NT):
                        ins.then_inc(e_xt, 1)
                if ok(t + 2):
                    pe.wait_ge(e_xT, t + 3)
                    for b in range(4):
                        if b > 1 or not (num(t) and t < -1):
                            pe.wait_ge(e_lgc, 4 * (t + 2) + b - 1)
                        MM(bank[:, b % 2, :], xT[:, par, 0:P], phiT[:, 512 * b:512 * b + 512], start=True, stop=False)
                        MM(bank[:, b % 2, :], onesb[:, :], phib[:, 512 * b:512 * b + 512], start=False, stop=True).then_inc(e_log, 1)
                if ok(t):
                    pe.wait_ge(e_fold, t + 1)
                    if not (num(t) and t < 1):
                        pe.wait_ge(e_sumC, t)
                    MM(bank[:, 3, :], I, fold[:, 0:512], start=True, stop=False)
                    MM(bank[:, 3, :], I, fold[:, 512:1024], start=False, stop=True).then_inc(e_sum32, 1)
            steps(pe, step)

            pe.wait_ge(ld_eb, 16)
            for b in range(4):
                pe.wait_ge(y_clip, b + 1)
                MM(bank[:, 4 + b, :], sel4[0:4, :], phiT[0:4, 512 * b:512 * b + 512], start=True, stop=False, skip_group_check=True)
            pe.wait_ge(e_rC, NT)

            def experts(b):
                pe.wait_ge(y_trc, b + 1)
                pe.wait_ge(ld_ew[b], 16)
                for c in range(4 * b, 4 * b + 4):
                    for n in range(4):
                        ins = MM(bank[32 * n:32 * n + 32, 4 + b, P * (c % 4):P * (c % 4) + P], xtlT[:, c, 32 * n:32 * n + 32],
                                 ring[b % len(ring)][:, 4 * (c % 4) + n, :], start=False, stop=True, skip_group_check=True)
                ins.then_inc(y_mm, 1)

            for b in range(4):
                pe.wait_ge(y_tanh, b + 1)
                for i in range(4):
                    ins = pe.transpose(bank[:, b, P * i:P * i + P], xtl[:, 4 * b + i, :], I)
                ins.then_inc(y_tr, 1)
                if b > 0:
                    experts(b - 1)
            experts(3)

            pe.wait_ge(y_out, 4)

            def step(j, par):
                t = 2 * j + par
                if ok(t + 1):
                    pe.wait_ge(c_n, t + 2)
                    for b in range(4):
                        if not (num(t) and t < 0):
                            if b < 2:
                                pe.wait_ge(c_ca, 2 * t + b + 1)
                            else:
                                pe.wait_ge(c_cv, 2 * t + b - 2 + 1)
                        for i in range(4):
                            src = EC[:, t + 1, :] if in_place(t + 1) else slots[:, 1 - par, :]
                            ins = pe.transpose(bank[:, b, P * i:P * i + P], src[:, P * (4 * b + i):P * (4 * b + i) + P], I)
                        ins.then_inc(c_tr, 1)
                if ok(t):
                    if not (num(t) and t < 2):
                        pe.wait_ge(lny_s, LN_MOE + t - 1)
                    pe.wait_ge(c_ca, 2 * t + 2)
                    pe.wait_ge(c_cv, 2 * t + 2)
                    for c in range(EC_N):
                        ins = MM(bank[:, 4 + par, 0:D], slotsT[:, par, c, :], Yt[:, c, :], start=(c == 0), stop=(c == EC_N - 1))
                    ins.then_inc(c_y, 1)
            steps(pe, step)

            pe.wait_ge(x_ready, LN_RET)
            pe.wait_ge(ld_ret, 16 * 5)
            pe.wait_ge(set_v, 2)

            def scores(t, par, hf):
                if hf == 0:
                    pe.wait_ge(r_qe, t + 1)
                if not (num(t) and t == 0):
                    pe.wait_ge(r_rd, 2 * (t - 1) + hf + 1)
                for b in (2 * hf, 2 * hf + 1):
                    ins = MM(bank[:, 2 + b, :], qkT[:, par, P:2 * P], qexp[:, par, 4 * b:4 * b + 4, :], start=True, stop=True)
                ins.then_inc(r_s, 1)

            def step(j, par):
                t = 2 * j + par
                if ok(t + 2):
                    pe.wait_ge(r_xs, t + 3)
                    if not (num(t) and t < -1):
                        pe.wait_ge(r_xT, t + 2)
                    pe.transpose(bank[:, 1, 0:P], xs[:, par, :], I).then_inc(r_tr, 1)
                if ok(t - 1):
                    pe.wait_ge(r_po, t)
                    if not (num(t) and t < 2):
                        pe.wait_ge(r_ve, t - 1)
                    for r in range(4):
                        ins = MM(bank[:, 7, 32 * r:32 * r + 32], rpo[:, 1 - par, r, :], sel8[:, :], start=True, stop=True)
                    ins.then_inc(r_sel, 1)
                if ok(t + 1):
                    pe.wait_ge(r_qk, t + 2)
                    pe.wait_ge(r_v, t + 2)
                    MM(bank[:, 0, 3 * P:4 * P], qkT[:, 1 - par, 0:P], kvbd, start=True, stop=True).then_inc(r_cr, 1)
                    scores(t + 1, 1 - par, 0)
                if ok(t + 2):
                    pe.wait_ge(r_xT, t + 3)
                    if not (num(t) and t < -1):
                        pe.wait_ge(r_crc, t + 2)
                    MM(bank[:, 0, 0:P], wqkv[:, 0:D], xT[:, par, 0:P], start=True, stop=True)
                    MM(bank[:, 0, P:2 * P], wqkv[:, D:2 * D], xT[:, par, 0:P], start=True, stop=True)
                    MM(bank[:, 0, 2 * P:3 * P], xT[:, par, 0:P], wqkv[:, 2 * D:3 * D], start=True, stop=True).then_inc(r_qkv, 1)
                if ok(t - 1):
                    pe.wait_ge(r_mv, t)
                    MM(bank[:, 7, P:P + 1], mean_w[:, :], gmv[:, 1 - par, 0:1], start=True, stop=True).then_inc(r_m1, 1)
                if ok(t + 1):
                    scores(t + 1, 1 - par, 1)
                if ok(t):
                    pe.wait_ge(r_v, t + 1)
                    pe.wait_ge(r_rd, 2 * t + 2)
                    if not (num(t) and t == 0):
                        pe.wait_ge(r_po, t)
                    for r in range(4):
                        for i in range(4):
                            ins = MM(bank[32 * i:32 * i + 32, 6, P * r:P * r + P], vpad[:, par, 4 * r + i, :], rd[:, par, 4 * r + i, :],
                                     start=True, stop=True, skip_group_check=True)
                    ins.then_inc(r_pv, 1)
                if ok(t - 1):
                    pe.wait_ge(r_v2, t)
                    MM(bank[:, 7, P + 1:P + 2], mean_w[:, :], gmv[:, 1 - par, 0:1], start=True, stop=True).then_inc(r_m2, 1)
            steps(pe, step)

            pe.wait_ge(x_ready, LN_XA1)
            pe.wait_ge(ld_xa1, 64)
            for i in range(4):
                ins = pe.transpose(bank[:, 0, P * i:P * i + P], wraw[:, i, :], I)
            ins.then_inc(set_w, 1)
            pe.wait_ge(set_w, 8)
            attention(1, LN_XA1)

            pe.wait_ge(x_ready, LN_FFN)
            pe.wait_ge(f_wp, 13)
            for c in range(FC):
                ins = MM(bank[0:R, 0, P * c:P * c + P], bfc[:, c, :], I, start=True, stop=True)
            ins.then_inc(f_wt, 1)
            MM(bank[0:R, 1, 0:D], bpj, I, start=True, stop=True).then_inc(f_wt, 1)
            pe.wait_ge(f_wc, 2)
            for c in range(FC):
                MM(bank[:, 2, P * c:P * c + P], wf1[:, c, :], I, start=True, stop=False)
                ins = MM(bank[:, 2, P * c:P * c + P], afc[0:R, :], bT[0:R, P * c:P * c + P], start=False, stop=True)
            ins.then_inc(f_wt, 1)
            for c in range(FC):
                MM(bank[:, 3, P * c:P * c + P], wf2[:, P * c:P * c + P], I, start=True, stop=False)
                ins = MM(bank[:, 3, P * c:P * c + P], apj[0:R, P * c:P * c + P], bT[0:R, FF:FF + D], start=False, stop=True)
            ins.then_inc(f_wt, 1)
            pe.wait_ge(f_wc, 4)

            def up(g, par):
                pe.wait_ge(f_xs, 2 * g + 1)
                if not (num(g) and g == 0):
                    pe.wait_ge(f_xT, g)
                for j in range(GT):
                    ins = pe.transpose(bank[:, 0, P * j:P * j + P], fs4[:, par, j, :], I)
                ins.then_inc(f_tr, 1)
                pe.wait_ge(f_xT, g + 1)
                for c in range(FC):
                    if not (num(g) and g == 0):
                        pe.wait_ge(f_g, 4 * (g - 1) + c + 1)
                    MM(bank[:, 2 + c, :], w1T[:, P * c:P * c + P], fxT[:, par, :], start=True, stop=True).then_inc(f_h, 1)

            def down(g, par):
                pe.wait_ge(f_g, 4 * g + 4)
                if not (num(g) and g < 2):
                    pe.wait_ge(lny_s, LN_FFN + g - 1)
                for j in range(GT):
                    for c in range(FC):
                        ins = MM(bank[:, 6 + par, P * j:P * j + P], hT[:, par, c, P * j:P * j + P], w2T[:, c, :], start=(c == 0), stop=(c == FC - 1))
                ins.then_inc(f_o, 1)
            up(0, 0)

            def step(j, par):
                g = 2 * j + par
                if not (num(g) and g == G - 1):
                    up(g + 1, 1 - par)
                down(g, par)
            pairs(pe, G, step, last_peeled=True)


def shape_constants():
    p = np.arange(P)
    gamma = 1.0 - 2.0 ** (-5.0 - np.arange(NH, dtype=np.float64))
    diff = p[None, :] - p[:, None]
    decay = np.where(diff[:, None, :] >= 0, gamma[None, :, None] ** np.maximum(diff, 0)[:, None, :], 0.0)
    part = p[:, None]
    return {
        "c_ident": np.eye(P, dtype=np.float32),
        "c_hmask": (part // HD == np.arange(NH)[None, :]).astype(np.float32),
        "c_selcol": ((part >= 32) & (part % 32 == np.arange(NS)[None, :])).astype(np.float32),
        "c_sel9": ((p % 32 < HD + 1)[:, None] & ((HD + 1) * (p // 32) + p % 32)[:, None].__eq__(np.arange(4 * (HD + 1))[None, :])).astype(np.float32),
        "c_sel8": ((p % 32 < HD)[:, None] & (HD * (p // 32) + p % 32)[:, None].__eq__(np.arange(4 * HD)[None, :])).astype(np.float32),
        "c_sel4": (np.arange(P)[None, :] // PS == np.arange(4)[:, None]).astype(np.float32),
        "c_decay": decay.astype(np.float32),
    }


def kernel(**inputs):
    import numpy as _np
    import concourse.bacc as _bacc
    from concourse import mybir as _mybir
    from concourse.bass_utils import run_bass_kernel_spmd as _run

    nc = _bacc.Bacc("TRN2", target_bir_lowering=False, num_devices=1)
    arrays, aps = {}, {}
    for name, value in {**inputs, **shape_constants()}.items():
        v = _np.ascontiguousarray(value)
        arrays[f"in_{name}"] = v
        aps[name] = nc.dram_tensor(f"in_{name}", v.shape, _mybir.dt.from_np(v.dtype), kind="ExternalInput").ap()
    out = nc.dram_tensor("out_0", (NT, P, D), F32, kind="ExternalOutput").ap()
    build(nc, aps, out)
    r = _run(nc, [arrays], core_ids=[0])
    return r.results[0]["out_0"]
```

```python
from contextlib import ExitStack

import numpy as np
import concourse.bass as bass
from concourse import mybir
from concourse.bass import ds

F32 = mybir.dt.float32
BF16 = mybir.dt.bfloat16
I32 = mybir.dt.int32
ALU = mybir.AluOpType
ACT = mybir.ActivationFunctionType
AX = mybir.AxisListType

NT, P, D = 16, 128, 128
NH, HD = 16, 8
SK = 120
G, GT = 4, 4
GW = GT * P
NS, DI, NC = 16, 256, 2
KC = 4
NE, PS = 64, 32
E = NE * PS
EC_N = E // P
FF, R = 512, 16
FC = FF // P
LN_EPS = 1e-5
MASKED = -float(2 ** 30)
QMAX = 127.0
ROUND = 12582912.0

LN_MAMBA, LN_XA0, LN_MOE, LN_RET, LN_XA1, LN_FFN, LN_END = 0, 4, 20, 36, 52, 68, 72
OUT_DMAS = G


def build(nc, a, out):
    ctx = ExitStack()
    with ctx:
        def sb(name, shape, dt=F32):
            return ctx.enter_context(nc.sbuf_tensor(name, shape, dt))

        def sem(name):
            return ctx.enter_context(nc.semaphore(name))

        bank = ctx.enter_context(nc.psum_tensor("bank", [P, 8, 512], F32))
        arena = sb("arena", [P, NT * E])
        X = sb("X", [P, NT, D])
        slots = sb("slots", [P, 2, E])
        slotsT = sb("slotsT", [P, 2, EC_N, P])
        phiT = sb("phiT", [P, E])
        phib = sb("phib", [P, E], BF16)
        spare = sb("spare", [P, E])
        ident = sb("ident", [P, P])
        identb = sb("identb", [P, P], BF16)
        onesb = sb("onesb", [P, P], BF16)
        mean_w = sb("mean_w", [P, P])
        hmask = sb("hmask", [P, NH])
        selcol = sb("selcol", [P, NS])
        mhalf = sb("mhalf", [P, 16])
        xs = sb("xs", [P, 2, D])
        xr = sb("xr", [P, 2, D])
        xT = sb("xT", [P, 2, 256])
        lny = sb("lny", [P, 2, GT, D])
        lnst = sb("lnst", [P, 2, GT, 6])
        lnmv = sb("lnmv", [P, 2, GT, 2])
        lnve = sb("lnve", [P, 2, GT])
        lnrs = sb("lnrs", [P, 2, GT])
        wa = sb("wa", [P, 2, 4, D])
        ab = sb("ab", [P, 2, 3])
        abr = sb("abr", [P, 2, D])
        sel9 = sb("sel9", [P, 4 * (HD + 1)])
        sel8 = sb("sel8", [P, 4 * HD])
        sel4 = sb("sel4", [P, P])
        rC = sb("rC", [P, NT, PS])
        staged = rC[:, :, :].rearrange("p t s -> p (t s)")
        ctxb = staged[:, 0:2 * P].rearrange("p (b n) -> p b n", b=2)
        maskb = staged[:, 2 * P:2 * P + 2 * SK].rearrange("p (b n) -> p b n", b=2).bitcast(I32)
        mxn = sb("mxn", [P, 2, NE])
        mxp = sb("mxp", [P, 2, PS])
        rD = sb("rD", [P, 2, NE])
        sm = sb("sm", [P, 96 + 4])

        off = [0]

        def carve(cols, dt=F32):
            v = arena[:, off[0]:off[0] + cols]
            off[0] += cols
            assert off[0] <= NT * E
            return v if dt == F32 else v.bitcast(dt)

        xconv = carve(NC * NT * P).rearrange("p (c n) -> p c n", c=NC)
        sz = carve(NC * NT * P).rearrange("p (c n) -> p c n", c=NC)
        dt_all = carve(NC * NT * P).rearrange("p (c n) -> p c n", c=NC)
        dtx_all = carve(NC * NT * P).rearrange("p (c n) -> p c n", c=NC)
        dA = carve(2 * 4 * GW).rearrange("p (b n) -> p b n", b=2)
        dBx = carve(2 * 4 * GW).rearrange("p (b n) -> p b n", b=2)
        hb = [dBx[:, 0, :], dBx[:, 1, :], spare[:, :], slotsT[:, 1, :, :].rearrange("p c n -> p (c n)")]
        Bb = slots
        Bs = carve(NT * P // 2, BF16)
        sel = carve(NS * P // 2, BF16).rearrange("p (n m) -> p n m", n=NS)
        w_in = carve(2 * DI)
        cwb = carve(DI * KC).rearrange("p (d k) -> p d k", k=KC)
        wk = carve(KC * DI).rearrange("p (k d) -> p k d", k=KC)
        wx = carve(NC * P).rearrange("p (c n) -> p c n", c=NC)
        wdt = carve(DI)
        wout = carve(NC * D).rearrange("p (c n) -> p c n", c=NC)
        alog = carve(NC * NS).rearrange("p (c n) -> p c n", c=NC)
        Am = carve(NC * NS).rearrange("p (c n) -> p c n", c=NC)
        convb, bdt, Dv = carve(NC), carve(NC), carve(NC)
        xTp = carve(2 * GT * (P + KC - 1)).rearrange("p (b j n) -> p b j n", b=2, j=GT)
        xs4 = carve(2 * GW).rearrange("p (b j n) -> p b j n", b=2, j=GT)
        bres = spare[:, 0:GW]
        dtin = spare[:, GW:2 * GW]
        sp_l = dA[:, 0, :].rearrange("p (c n) -> p c n", c=4)[:, 0:2, :]
        sp_r = dA[:, 1, :].rearrange("p (c n) -> p c n", c=4)[:, 0:2, :]
        yTm = slotsT[:, 0, 0:2 * GT, :].rearrange("p (c j) n -> p c (j n)", c=NC)

        off[0] = 0
        mbias = carve(SK, BF16).rearrange("p (b n) -> p b n", b=2)
        mflag = carve(2 * SK).rearrange("p (b n) -> p b n", b=2)
        allm = carve(2).rearrange("p (b n) -> p b n", b=2)
        escale = carve(2).rearrange("p (b n) -> p b n", b=2)
        qT = carve(2 * P).rearrange("p (b n) -> p b n", b=2)
        kT = carve(2 * SK).rearrange("p (b n) -> p b n", b=2)
        kexp = carve(2 * NH * SK).rearrange("p (b h n) -> p b h n", b=2, h=NH)
        vaug = carve(2 * NH * 32).rearrange("p (b h n) -> p b h n", b=2, h=NH)
        poT = carve(2 * 4 * P).rearrange("p (b r n) -> p b r n", b=2, r=4)
        nmx = carve(2 * NH).rearrange("p (b h n) -> p b h n", b=2, n=1)
        sc = carve(2 * NH * SK).rearrange("p (b h n) -> p b h n", b=2, h=NH)
        pT = carve(2 * NH * P).rearrange("p (b h n) -> p b h n", b=2, h=NH)
        rden = carve(2 * NH).rearrange("p (b h n) -> p b h n", b=2, n=1)
        on = carve(2 * D).rearrange("p (b n) -> p b n", b=2)
        oT = carve(2 * D).rearrange("p (b n) -> p b n", b=2)
        wraw = carve(4 * D).rearrange("p (i n) -> p i n", i=4)
        top_attn = off[0]

        EC = arena[:, :].rearrange("p (t e) -> p t e", t=NT)
        xtl = slotsT[:, 0, :, :]
        xtlT = slotsT[:, 1, :, :]
        phir = slotsT[:, 0, :, :]
        lgc = slotsT[:, :, :, :].rearrange("p b c n -> p b (c n)")
        fold = spare[:, 0:E // 2]
        Yt = phiT[:, :].rearrange("p (c n) -> p c n", c=EC_N)
        ring = [b.rearrange("p (e n) -> p e n", e=16) for b in (slots[:, 0, :], slots[:, 1, :], spare[:, :])]
        bve, bnm, brs, bof = (sm[:, 32 + EC_N * i:32 + EC_N * (i + 1)] for i in range(4))

        NP = 5 * NE // 8

        def in_place(t):
            return isinstance(t, int) and t < 3

        off[0] = 0
        decay = carve(NH * P).rearrange("p (h n) -> p h n", h=NH)
        qexp = carve(2 * NH * P).rearrange("p (b h n) -> p b h n", b=2, h=NH)
        rd = carve(2 * NH * P).rearrange("p (b h n) -> p b h n", b=2, h=NH)
        qkT = carve(2 * 2 * D).rearrange("p (b n) -> p b n", b=2)
        vpad = carve(2 * NH * 32).rearrange("p (b h n) -> p b h n", b=2, h=NH)
        rpo = carve(2 * 4 * P).rearrange("p (b r n) -> p b r n", b=2, r=4)
        crs = carve(2 * D).rearrange("p (b n) -> p b n", b=2)
        gr = carve(2 * D).rearrange("p (b n) -> p b n", b=2)
        gst = carve(2 * 6).rearrange("p (b n) -> p b n", b=2)
        gmv = carve(2 * 2).rearrange("p (b n) -> p b n", b=2)
        gsc = carve(2 * 4).rearrange("p (b n) -> p b n", b=2)
        gt1 = carve(2 * D).rearrange("p (b n) -> p b n", b=2)
        gt2 = carve(2 * D).rearrange("p (b n) -> p b n", b=2)
        wqkv = carve(3 * D)
        kvl = carve(HD)
        kvbd = carve(D)
        gnw, gnb = carve(NH), carve(NH)

        off_ret, off_attn = off[0], top_attn
        assert max(off_ret, off_attn) <= 17920
        off[0] = 17920
        wf1 = carve(FC * D).rearrange("p (c n) -> p c n", c=FC)
        wf2 = carve(FF)
        tq1 = carve(FF)
        tq2 = carve(FF)
        bfcr = carve(FC)
        bpr = carve(D)
        afc = carve(D)
        bfc = carve(FC * R).rearrange("p (c r) -> p c r", c=FC)
        apj = carve(FF)
        bpj = carve(R)
        bT = carve(FF + D)
        w1T = carve(FF)
        w2T = carve(FC * D).rearrange("p (c n) -> p c n", c=FC)
        amx = carve(8)
        fs4 = carve(2 * GW).rearrange("p (b j n) -> p b j n", b=2, j=GT)
        fr4 = carve(2 * GW).rearrange("p (b j n) -> p b j n", b=2, j=GT)
        fxT = carve(2 * GW).rearrange("p (b n) -> p b n", b=2)
        hT = carve(2 * FC * GW).rearrange("p (b c n) -> p b c n", b=2, c=FC)

        ld_const, ld_x, ld_mamba, ld_attn, ld_moe = (sem(f"ld_{n}") for n in ("const", "x", "mamba", "attn", "moe"))
        ld_eb, ld_ret, ld_xa1, ld_ffn = (sem(f"ld_{n}") for n in ("eb", "ret", "xa1", "ffn"))
        ld_xs4 = [sem("ld_xs4_0"), sem("ld_xs4_1")]
        ld_ctx = [sem("ld_ctx0"), sem("ld_ctx1")]
        ld_mask = [sem("ld_mask0"), sem("ld_mask1")]
        ld_ew = [sem(f"ld_ew{i}") for i in range(4)]
        stored = sem("stored")
        set_v, set_p, set_w = sem("set_v"), sem("set_p"), sem("set_w")
        lny_s, lnst_s, lnmv_s, lnve_s, lnrs_s, x_ready = (sem(n) for n in ("ln_y", "ln_stats", "ln_mv", "ln_ve", "ln_rstd", "x_ready"))
        m_tr, m_xT, m_mm, m_silu, m_silz = (sem(f"m_{n}") for n in ("tr", "xT", "mm", "silu", "silz"))
        m_wx, m_dtin, m_bs, m_dtp, m_abs, m_ln1, m_relu, m_dt, m_dtx = (sem(f"m_{n}") for n in ("wx", "dtin", "bs", "dtp", "abs", "ln", "relu", "dt", "dtx"))
        m_dA, m_dz, m_add, m_B, m_dBx, m_h, m_sum, m_y, m_o, m_A = (sem(f"m_{n}") for n in ("dA", "dz", "add", "B", "dBx", "h", "sum", "y", "o", "A"))
        m_bc, m_dBp, ld_win = sem("m_bc"), sem("m_dBp"), sem("ld_win")
        m_split = sem("m_split")
        a_xs, a_xr, a_tr, a_xT, a_qkv, a_qk, a_v, a_kexp, a_mb, a_esc = (sem(f"a_{n}") for n in ("xs", "xr", "tr", "xT", "qkv", "qk", "v", "kexp", "mb", "esc"))
        a_s, a_max, a_sub, a_exp, a_pt, a_ptc, a_pv, a_po, a_sel = (sem(f"a_{n}") for n in ("s", "max", "sub", "exp", "pt", "ptc", "pv", "po", "sel"))
        a_rden, a_on, a_ot, a_otc, a_out, a_flag, a_bvo, a_bias = (sem(f"a_{n}") for n in ("rden", "on", "ot", "otc", "out", "flag", "bvo", "bias"))
        e_xs, e_tr, e_xT, e_log, e_lgc, e_mxp, e_mxn, e_subD, e_subC, e_expD, e_expC = (sem(f"e_{n}") for n in ("xs", "tr", "xT", "log", "lgc", "mxp", "mxn", "subD", "subC", "expD", "expC"))
        e_sum, e_sumC, e_rD, e_rC, e_Dn, e_xt, e_pb, e_phi, e_fold, e_sum32 = (sem(f"e_{n}") for n in ("sum", "sumC", "rD", "rC", "Dn", "xt", "pb", "phi", "fold", "sum32"))
        y_xt, y_clip, y_mv, y_ve, y_tanh, y_tr, y_trc, y_mm, y_out = (sem(f"y_{n}") for n in ("xt", "clip", "mv", "ve", "tanh", "tr", "trc", "mm", "out"))
        c_np, c_nv, c_tr, c_ca, c_cv, c_y = (sem(f"c_{n}") for n in ("np", "nv", "tr", "ca", "cv", "y"))
        r_xs, r_xr, r_tr, r_xT, r_qkv, r_cr, r_qk, r_crc, r_v, r_qe, r_s, r_rd, r_pv, r_po, r_sel = (sem(f"r_{n}") for n in ("xs", "xr", "tr", "xT", "qkv", "cr", "qk", "crc", "v", "qe", "s", "rd", "pv", "po", "sel"))
        r_r, r_mv, r_m1, r_d, r_v2, r_m2, r_ve, r_rs, r_t1 = (sem(f"r_{n}") for n in ("r", "mv", "m1", "d", "v2", "m2", "ve", "rs", "t1"))
        f_w, f_wp, f_wt, f_wc, f_xs, f_tr, f_xT, f_h, f_g, f_o = (sem(f"f_{n}") for n in ("w", "wp", "wt", "wc", "xs", "tr", "xT", "h", "g", "o"))

        passed_dve, passed_act, passed_pool = sem("passed_dve"), sem("passed_act"), sem("passed_pool")
        block = ctx.enter_context(nc.Block())

        def tile(buf, t, k=1):
            v = buf[:, ds(t, k), :]
            return v.rearrange("p a n -> p (a n)") if k == 1 else v

        def pairs(eng, n, step, last_peeled=False):
            step(0, 0)
            step(0, 1)
            end = n // 2 - (1 if last_peeled else 0)
            if end > 1:
                with eng.Fori(1, end) as j:
                    step(j, 0)
                    step(j, 1)
            if last_peeled:
                step(n // 2 - 1, 0)
                step(n // 2 - 1, 1)

        def at(step, t):
            step(t // 2, t % 2)

        def steps(eng, step, first=-2, last=NT, looped=2):
            for t in range(first, looped):
                at(step, t)
            with eng.Fori(looped // 2, NT // 2 - 2) as j:
                step(j, 0)
                step(j, 1)
            for t in range(NT - 4, last + 1):
                at(step, t)

        def ok(t):
            return not isinstance(t, int) or 0 <= t < NT

        def bc(ap, n):
            return ap.to_broadcast([ap.shape[0], ap.shape[1], n])

        def mid(ap, n):
            return ap.unsqueeze(1).to_broadcast([ap.shape[0], n, ap.shape[1]])

        def num(x):
            return isinstance(x, int)

        @block.sync
        def _(sp):
            xt = a["x"].rearrange("t p d -> p t d")
            sp.dma_start(xs4[:, 0, :, :], xt[:, 0:GT, :]).then_inc(ld_xs4[0], 16)
            for dst, name in ((ident, "c_ident"), (selcol, "c_selcol"), (hmask, "c_hmask"), (sel9, "c_sel9"), (sel8, "c_sel8")):
                sp.dma_start(dst[:, :], a[name]).then_inc(ld_const, 16)
            sp.dma_start(sel4[0:4, :], a["c_sel4"]).then_inc(ld_const, 16)
            sp.dma_start(xs4[:, 1, :, :], xt[:, GT:2 * GT, :]).then_inc(ld_xs4[1], 16)
            for dst, name in ((convb, "L0_attn_conv_b"), (bdt, "L0_attn_b_dt"), (Dv, "L0_attn_D")):
                sp.dma_start(dst, a[name].rearrange("(c p) -> p c", p=P), allow_slow_non_contiguous=True).then_inc(ld_mamba, 16)
            sp.dma_start(alog, a["L0_attn_A_log"].rearrange("(c p) n -> p c n", p=P)).then_inc(ld_mamba, 16)
            sp.dma_start(wout, a["L0_attn_W_out"].rearrange("(c p) n -> p c n", p=P)).then_inc(ld_mamba, 16)
            sp.dma_start(wdt[0:R, :], a["L0_attn_W_dt"]).then_inc(ld_mamba, 16)
            sp.wait_ge(set_w, 1)
            wxr = a["L0_attn_W_x"].rearrange("(c p) n -> p c n", p=P)
            for q in range(4):
                sp.dma_start(wx[:, :, 32 * q:32 * q + NS],
                             wxr[:, :, (0 if q == 0 else NS):(NS if q == 0 else 2 * NS)]).then_inc(ld_mamba, 16)
            sp.dma_start(X[:, :, :], xt).then_inc(ld_x, 16)
            for g in range(2, G):
                sp.wait_ge(m_tr, g - 1)
                sp.dma_start(xs4[:, g % 2, :, :], xt[:, GT * g:GT * g + GT, :]).then_inc(ld_xs4[g % 2], 16)
            for i, n in enumerate(("Wq", "Wk", "Wv", "Wo")):
                sp.dma_start(wa[:, 0, i, :], a["L0_xattn_" + n]).then_inc(ld_attn, 16)
            for lay in range(2):
                for i, n in enumerate(("bq", "bk", "bv")):
                    sp.dma_start(ab[:, lay, i:i + 1], a[f"L{lay}_xattn_{n}"].rearrange("(p o) -> p o", o=1)).then_inc(ld_attn, 16)
                sp.dma_start(abr[:, lay, :], a[f"L{lay}_xattn_bo"].partition_broadcast(P)).then_inc(ld_attn, 16)
            def attn_loads(lay):
                def step(j, par):
                    t, u = 2 * j + par, NT * lay + 2 * j + par
                    if not (num(u) and u < 2):
                        sp.wait_ge(a_tr, u - 1)
                    sp.dma_start(ctxb[0:SK, par, :], tile(a["ctx_1024"].rearrange("t s d -> s t d"), t)).then_inc(ld_ctx[par], 16)
                    if lay == 0:
                        if not (num(t) and t < 2):
                            sp.wait_ge(a_mb, t - 1)
                        sp.dma_start(maskb[:, par, :], tile(a["mask_Bx1xSxS2_ik1"].rearrange("t o q k -> q t (o k)"), t)).then_inc(ld_mask[par], 16)
                pairs(sp, NT, step)

            attn_loads(0)
            sp.wait_ge(e_log, 4 * NT)
            sp.dma_start(phiT[0:4, :].rearrange("p (c h) -> p c h", c=EC_N), a["L0_ffn_expert_b"].rearrange("(c n) h -> n c h", n=4)).then_inc(ld_eb, 16)
            sp.wait_ge(y_xt, 4)
            ewv = a["L0_ffn_expert_w"].rearrange("(b n) d h -> b d n h", b=4)
            for b in range(4):
                if b >= len(ring):
                    sp.wait_ge(y_mm, b - len(ring) + 1)
                sp.dma_start(ring[b % len(ring)], ewv[b]).then_inc(ld_ew[b], 16)
            sp.wait_ge(c_np, (max(off_ret, off_attn) + E - 1) // E)
            sp.wait_ge(c_nv, (max(off_ret, off_attn) + E - 1) // E)
            sp.wait_ge(c_tr, 4 * 3)
            sp.dma_start(decay, a["c_decay"]).then_inc(ld_ret, 16)
            sp.dma_start(wqkv, a["L1_attn_W_qkv"]).then_inc(ld_ret, 16)
            sp.dma_start(kvl, a["L1_attn_past_kv"].rearrange("h d e -> (h d) e")).then_inc(ld_ret, 16)
            sp.dma_start(gnw, a["L1_attn_gn_weight"].partition_broadcast(P)).then_inc(ld_ret, 16)
            sp.dma_start(gnb, a["L1_attn_gn_bias"].partition_broadcast(P)).then_inc(ld_ret, 16)
            sp.wait_ge(c_np, NT)
            sp.wait_ge(c_nv, NT)
            sp.dma_start(wf1, a["L1_ffn_W_fc"].rearrange("(c p) d -> p c d", p=P)).then_inc(ld_ffn, 16)
            sp.dma_start(wf2, a["L1_ffn_W_proj"]).then_inc(ld_ffn, 16)
            sp.dma_start(bfcr, a["L1_ffn_b_fc"].rearrange("(c p) -> p c", p=P), allow_slow_non_contiguous=True).then_inc(ld_ffn, 16)
            sp.dma_start(bpr, a["L1_ffn_b_proj"].partition_broadcast(P)).then_inc(ld_ffn, 16)
            sp.dma_start(afc[0:R, :], a["L1_ffn_A_fc"]).then_inc(ld_ffn, 16)
            sp.dma_start(bfc, a["L1_ffn_B_fc"].rearrange("(c p) r -> p c r", p=P)).then_inc(ld_ffn, 16)
            sp.dma_start(apj[0:R, :], a["L1_ffn_A_proj"]).then_inc(ld_ffn, 16)
            sp.dma_start(bpj, a["L1_ffn_B_proj"]).then_inc(ld_ffn, 16)
            attn_loads(1)
            ot = out.rearrange("t p d -> p t d")
            for g in range(G):
                sp.wait_ge(x_ready, LN_FFN + g + 1)
                sp.dma_start(ot[:, GT * g:GT * g + GT, :], X[:, GT * g:GT * g + GT, :]).then_inc(stored, 16)
            sp.wait_ge(stored, 16 * OUT_DMAS)

        @block.gpsimd
        def _(pool):
            def ln_rstd(e, par, k):
                pool.wait_ge(lnmv_s, e + 1)
                pool.sem_inc(passed_pool, 1)
                pool.tensor_scalar(lnve[:, par, 0:k], lnmv[:, par, 0:k, 1], LN_EPS, None, ALU.add).then_inc(lnve_s, 1)
                pool.wait_ge(lnve_s, e + 1)
                pool.tensor_tensor(lnrs[:, par, 0:k], lnve[:, par, 0:k], mhalf[:, 0:k], ALU.pow).then_inc(lnrs_s, 1)

            pool.memset(mhalf[:, :], -0.5)
            pool.memset(mean_w[:, :], 1.0 / P)
            pool.memset(onesb[:, :], 1.0).then_inc(set_p, 1)
            pool.wait_ge(set_p, 1)

            def times_B(g, q):
                pp = 4 * g + q
                pool.wait_ge(m_bc, pp + 1)
                if not (num(g) and g == 0 and q < 2):
                    pool.wait_ge(m_sum, 2 * pp - 2)
                pool.tensor_tensor(hb[(2 * q + 1) % 4].rearrange("p (s n) -> p s n", s=4), Bb[:, q % 2, :].rearrange("p (s n) -> p s n", s=4),
                                   mid(dtx_all[:, 1, ds(GW * g, GW)], 4), ALU.mult).then_inc(m_dBp, 1)

            def add_states(g, q):
                pool.wait_ge(m_h, 8 * g + 2 * q + 1)
                h = hb[2 * q % 4]
                pool.tensor_tensor(h[:, 0:GW], h[:, 0:GW], h[:, GW:2 * GW], ALU.add).then_inc(m_add, 1)

            def mamba_group(g, par):
                for q in range(4):
                    times_B(g, q)
                    add_states(g, q)
                    if q == 1 and not (num(g) and g == 0):
                        ln_rstd(g - 1, 1 - par, GT)
            pool.wait_ge(m_dtx, G)
            for c in range(NC):
                ins = pool.memset(dA[:, c, :].rearrange("p (s n) -> p s n", n=P)[:, :, 0:1], 0.0)
            ins.then_inc(m_dz, 1)
            pairs(pool, G, lambda j, par: mamba_group(2 * j + par, par))
            ln_rstd(G - 1, (G - 1) % 2, GT)

            def attention(lay, ln0):
                def stage(t, par):
                    u = NT * lay + t
                    if not (num(u) and u < 2):
                        pool.wait_ge(a_tr, u - 1)
                    pool.tensor_copy(xs[:, par, :], tile(X, t)).then_inc(a_xs, 1)

                def step(j, par):
                    t = 2 * j + par
                    u = NT * lay + t
                    if num(t) and t == -2:
                        stage(0, 0)
                    if num(t) and t == 0:
                        pool.wait_ge(a_bias, lay + 1)
                    if ok(t + 3):
                        stage(t + 3, 1 - par)
                    if ok(t):
                        if not (num(t) and t < 2):
                            pool.wait_ge(lny_s, ln0 + t - 1)
                        pool.tensor_tensor(xr[:, par, :], tile(X, t), abr[:, lay, :], ALU.add).then_inc(a_xr, 1)
                    if ok(t + 2):
                        pool.wait_ge(a_qk, u + 3)
                        if not (num(u) and u < 0):
                            pool.wait_ge(a_s, 2 * u + 2)
                        pool.tensor_tensor(kexp[:, par, :, :], mid(kT[:, par, :], NH), bc(hmask[:, :].unsqueeze(2), SK),
                                           ALU.mult).then_inc(a_kexp, 1)
                    if ok(t - 1):
                        ln_rstd(ln0 + t - 1, 1 - par, 1)
                return step

            pool.wait_ge(ld_const, 96)
            pool.wait_ge(x_ready, LN_XA0)
            xa0 = attention(0, LN_XA0)
            steps(pool, xa0, last=NT - 1)


            def dispatch(j, par):
                t = 2 * j + par
                if ok(t + 1):
                    pool.wait_ge(e_mxp, t + 2)
                    pool.tensor_tensor(tile(EC, t + 1).rearrange("p (n s) -> p n s", s=PS), lgc[:, 1 - par, :].rearrange("p (n s) -> p n s", s=PS),
                                       mid(mxp[:, 1 - par, :], NE), ALU.subtract).then_inc(e_subC, 1)
                if ok(t):
                    pool.wait_ge(e_rD, t + 1)
                    v = slots[:, par, :].rearrange("p (n s) -> p n s", s=PS)
                    pool.tensor_tensor(v, v, bc(rD[:, par, :].unsqueeze(2), PS), ALU.mult).then_inc(e_Dn, 1)
                if ok(t + 1):
                    pool.wait_ge(e_expC, t + 2)
                    if not (num(t) and t < 0):
                        pool.wait_ge(e_sum32, t + 1)
                    c = tile(EC, t + 1)
                    pool.tensor_tensor(fold, c[:, 0:E // 2], c[:, E // 2:E], ALU.add).then_inc(e_fold, 1)
            pool.wait_ge(a_s, 2 * NT)
            at(dispatch, -1)
            at(xa0, NT)
            pool.wait_ge(x_ready, LN_MOE)
            steps(pool, dispatch, first=0)

            for b in range(4):
                mv = sm[:, 8 * b:8 * b + 8].rearrange("p (c n) -> p c n", n=2)
                k = slice(4 * b, 4 * b + 4)
                pool.wait_ge(y_mv, 2 * b + 2)
                pool.tensor_scalar(bve[:, k], mv[:, :, 1], LN_EPS, None, ALU.add)
                pool.tensor_scalar(bnm[:, k], mv[:, :, 0], -1.0, None, ALU.mult).then_inc(y_ve, 1)
                pool.wait_ge(y_ve, 3 * b + 1)
                pool.tensor_tensor(brs[:, k], bve[:, k], mhalf[:, 0:4], ALU.pow).then_inc(y_ve, 1)
                pool.wait_ge(y_ve, 3 * b + 2)
                pool.tensor_tensor(bof[:, k], bnm[:, k], brs[:, k], ALU.mult).then_inc(y_ve, 1)

            pool.wait_ge(e_rC, NT)

            def combine(j, par):
                t = 2 * j + par
                if ok(t + 2):
                    if num(t) and t == 1:
                        pool.wait_ge(y_mm, 4)
                    if not (num(t) and t < 2):
                        pool.wait_ge(c_tr, 4 * t + 4)
                    v = tile(EC, t + 2).rearrange("p (n s) -> p n s", s=PS)
                    dst = v if in_place(t + 2) else slots[:, par, :].rearrange("p (n s) -> p n s", s=PS)
                    pool.tensor_tensor(dst[:, 0:NP, :], v[:, 0:NP, :], mid(tile(rC, t + 2), NP), ALU.mult).then_inc(c_np, 1)
                if ok(t):
                    ln_rstd(LN_MOE + t, par, 1)
            steps(pool, combine, last=NT - 2)

            pool.wait_ge(ld_ret, 16 * 5)

            def stage(t, par):
                if not (num(t) and t < 2):
                    pool.wait_ge(r_tr, t - 1)
                pool.tensor_copy(xs[:, par, :], tile(X, t)).then_inc(r_xs, 1)

            def retention(j, par):
                t = 2 * j + par
                if num(t) and t == -2:
                    stage(0, 0)
                if ok(t + 3):
                    stage(t + 3, 1 - par)
                if ok(t - 2):
                    ln_rstd(LN_RET + t - 2, par, 1)
                if ok(t):
                    if not (num(t) and t < 2):
                        pool.wait_ge(lny_s, LN_RET + t - 1)
                    pool.tensor_tensor(xr[:, par, :].rearrange("p (h e) -> p h e", e=HD), tile(X, t).rearrange("p (h e) -> p h e", e=HD),
                                       bc(gnb.unsqueeze(2), HD), ALU.add).then_inc(r_xr, 1)
                if ok(t + 2):
                    pool.wait_ge(r_qk, t + 3)
                    if not (num(t) and t < 0):
                        pool.wait_ge(r_s, 2 * t + 2)
                    pool.tensor_tensor(qexp[:, par, :, :], mid(qkT[:, par, 0:P], NH), bc(hmask[:, :].unsqueeze(2), P),
                                       ALU.mult).then_inc(r_qe, 1)
                if ok(t - 1):
                    pool.wait_ge(r_ve, t)
                    pool.tensor_tensor(gsc[:, 1 - par, 3:4], gsc[:, 1 - par, 2:3], mhalf[:, 0:1], ALU.pow).then_inc(r_rs, 1)
            pool.wait_ge(x_ready, LN_MOE + 3)
            at(retention, -2)
            at(combine, NT - 1)
            at(retention, -1)
            at(combine, NT)
            pool.wait_ge(x_ready, LN_RET)
            at(retention, 0)
            at(retention, 1)
            pool.wait_ge(f_w, 1)
            pool.partition_all_reduce(amx[:, 2:4], amx[:, 0:2], P, bass.bass_isa.ReduceOp.max).then_inc(f_w, 1)
            steps(pool, retention, first=2, last=NT - 2)
            xa1 = attention(1, LN_XA1)
            pool.wait_ge(x_ready, LN_RET + 3)
            pool.wait_ge(r_tr, NT)
            pool.wait_ge(r_rd, 2 * NT)
            at(xa1, -2)
            at(retention, NT - 1)
            at(xa1, -1)
            at(retention, NT)
            at(retention, NT + 1)
            pool.wait_ge(x_ready, LN_XA1)
            steps(pool, xa1, first=0, last=NT - 2)

            def stage_group(g, par):
                if not (num(g) and g < 2):
                    pool.wait_ge(f_tr, g - 1)
                    pool.wait_ge(lny_s, LN_FFN + g - 1)
                pool.tensor_copy(fs4[:, par, :, :], tile(X, GT * g, GT)).then_inc(f_xs, 1)
                pool.tensor_tensor(fr4[:, par, :, :], tile(X, GT * g, GT), mid(bpr, GT), ALU.add).then_inc(f_xs, 1)

            pool.wait_ge(x_ready, LN_XA1 + GT)
            pool.wait_ge(ld_ffn, 16 * 8)
            stage_group(0, 0)
            at(xa1, NT - 1)
            pool.wait_ge(x_ready, LN_XA1 + 2 * GT)
            stage_group(1, 1)
            at(xa1, NT)
            pool.wait_ge(x_ready, LN_FFN)
            for g in range(G):
                if g + 2 < G:
                    stage_group(g + 2, g % 2)
                ln_rstd(LN_FFN + g, g % 2, GT)

        @block.scalar
        def _(act):
            A = act.activation
            def x_transposed(g):
                act.wait_ge(m_tr, g + 1)
                if g == 0:
                    act.wait_ge(set_v, 1)
                if g >= 2:
                    act.wait_ge(m_mm, 4 * (g - 1))
                act.copy(xTp[:, g % 2, :, KC - 1:], bank[:, 0, :].rearrange("p (j n) -> p j n", j=GT)).then_inc(m_xT, 1)

            def conv_silu(g):
                if g == 0:
                    act.wait_ge(ld_mamba, 16 * 10)
                for c in range(NC):
                    act.wait_ge(m_mm, 4 * g + c + 1)
                    A(xconv[:, c, GW * g:GW * g + GW], bank[:, 1 + c, :], ACT.Silu, bias=convb[:, c:c + 1]).then_inc(m_silu, 1)
                for c in range(NC):
                    act.wait_ge(m_mm, 4 * g + 2 + c + 1)
                    A(sz[:, c, GW * g:GW * g + GW], bank[:, 3 + c, :], ACT.Silu).then_inc(m_silz, 1)

            def steps_soft(g):
                act.wait_ge(m_wx, g + 1)
                if g >= 1:
                    act.wait_ge(m_dtp, 2 * g)
                act.copy(dtin[0:R, :], bank[0:R, 7, :]).then_inc(m_dtin, 1)
                if g >= 1:
                    act.wait_ge(m_dt, g)
                for c in range(NC):
                    act.wait_ge(m_dtp, 2 * g + c + 1)
                    A(sp_l[:, c, :], bank[:, 5 + c, :], ACT.Abs, bias=bdt[:, c:c + 1]).then_inc(m_abs, 1)
                act.wait_ge(m_abs, 2 * g + 2)
                A(sp_l, sp_l, ACT.Exp, scale=-1.0).then_inc(m_ln1, 1)
                act.wait_ge(m_ln1, 2 * g + 1)
                A(sp_l, sp_l, ACT.Ln, bias=1.0).then_inc(m_ln1, 1)
            act.dma_start(w_in, a["L0_attn_W_in"]).then_inc(ld_win, 16)
            act.dma_start(cwb.rearrange("p d k -> p (d k)"),
                          a["L0_attn_conv_w"].rearrange("d k -> (d k)").partition_broadcast(P)).then_inc(ld_win, 16)
            x_transposed(0)
            for g in range(G + 1):
                if g < G:
                    conv_silu(g)
                if g < G - 1:
                    x_transposed(g + 1)
                if g > 0:
                    act.preload_act_table_set("natural_log_exp_and_others")
                    steps_soft(g - 1)
            A(Am, alog, ACT.Exp).then_inc(m_A, 1)

            act.wait_ge(m_A, 2)
            act.wait_ge(m_dtx, G)

            def decays(g):
                for q in range(4):
                    pp = 4 * g + q
                    act.wait_ge(m_B, pp + 1)
                    if not (num(g) and g == 0 and q < 2):
                        act.wait_ge(m_dBx, pp - 1)
                        act.wait_ge(m_dBp, pp - 1)
                    act.copy(Bb[:, q % 2, :].rearrange("p (s n) -> p s n", s=4), bank[:, 0:4, :]).then_inc(m_bc, 1)
                    for c in range(NC):
                        kk = 2 * pp + c
                        if not (num(g) and g == 0 and q == 0):
                            act.wait_ge(m_h, kk - 1)
                            act.sem_inc(passed_act, 1)
                        for i in range(4):
                            n = 4 * q + i
                            ins = A(dA[:, c, GW * i:GW * i + GW].rearrange("p (j n) -> p j n", j=GT)[:, :, 1:P],
                                    dt_all[:, c, ds(GW * g, GW)].rearrange("p (j n) -> p j n", j=GT)[:, :, 1:P], ACT.Exp, scale=Am[:, c, n:n + 1])
                        ins.then_inc(m_dA, 1)
            decays(0)
            with act.Fori(1, G) as g:
                decays(g)

            def attention(lay, ln0):
                def probs(u, par, hf):
                    act.wait_ge(a_sub, 2 * u + hf + 1)
                    v = sc[:, par, 8 * hf:8 * hf + 8, :]
                    if lay == 0:
                        if hf == 0:
                            act.wait_ge(a_esc, u + 1)
                        A(v, v, ACT.Exp, scale=escale[:, par, :]).then_inc(a_exp, 1)
                    else:
                        A(v, v, ACT.Exp, scale=HD ** -0.5).then_inc(a_exp, 1)

                def probsT(u, par, r):
                    act.wait_ge(a_pt, 4 * u + r + 1)
                    if r == 0 and not (num(u) and u < 2):
                        act.wait_ge(a_pv, u - 1)
                    act.copy(pT[0:SK, par, 4 * r:4 * r + 4, :], bank[0:SK, 6 + r % 2, :].rearrange("p (h n) -> p h n", h=4)).then_inc(a_ptc, 1)

                def step(j, par):
                    t = 2 * j + par
                    u = NT * lay + t
                    if ok(t + 2):
                        act.wait_ge(a_tr, u + 3)
                        if not (num(u) and u < 0):
                            act.wait_ge(a_qkv, u + 1)
                        act.copy(xT[:, par, 0:P + SK], bank[:, 1, 0:P + SK]).then_inc(a_xT, 1)
                    if ok(t + 2):
                        act.wait_ge(a_qkv, u + 3)
                        if not (num(u) and u < 0):
                            act.wait_ge(a_s, 2 * u + 2)
                            act.wait_ge(a_kexp, u + 1)
                        A(qT[:, par, :], bank[:, 0, 0:P], ACT.Identity, bias=ab[:, lay, 0:1])
                        A(kT[:, par, :], bank[:, 0, P:P + SK], ACT.Identity, bias=ab[:, lay, 1:2]).then_inc(a_qk, 1)
                    if ok(t + 1):
                        probs(u + 1, 1 - par, 0)
                    if ok(t):
                        probsT(u, par, 0)
                    if ok(t - 1):
                        act.wait_ge(a_ot, u)
                        if not (num(u) and u < 3):
                            act.wait_ge(a_out, u - 2)
                        act.copy(oT[:, 1 - par, :], bank[:, 1, 0:D]).then_inc(a_otc, 1)
                    if ok(t):
                        probsT(u, par, 1)
                        probsT(u, par, 2)
                        probsT(u, par, 3)
                    if ok(t + 1):
                        probs(u + 1, 1 - par, 1)
                    if ok(t):
                        act.wait_ge(a_pv, u + 1)
                        if not (num(u) and u < 2):
                            act.wait_ge(a_sel, u - 1)
                        act.copy(poT[:, par, :, :], bank[:, 6, :].rearrange("p (r n) -> p r n", r=4)).then_inc(a_po, 1)
                return step

            act.wait_ge(ld_attn, 16 * 12)
            act.wait_ge(x_ready, LN_XA0)
            act.dma_start(phir, a["L0_ffn_phi_w"].rearrange("(c p) d -> p c d", p=P)).then_inc(ld_moe, 16)
            for i, n in enumerate(("Wq", "Wk", "Wv", "Wo")):
                act.dma_start(wraw[:, i, :], a["L1_xattn_" + n]).then_inc(ld_xa1, 16)
            act.wait_ge(set_w, 2)
            pb_row = a["L0_ffn_phi_b"].rearrange("(o n) -> o n", o=1)
            for row in (0, 64, 96):
                act.dma_start(slots[row:row + 1, 0, :], pb_row).then_inc(ld_moe, 16)

            xa0 = attention(0, LN_XA0)
            at(xa0, -2)
            act.wait_ge(set_w, 3)
            act.copy(wa[:, 1, :, :], bank[:, 6, :].rearrange("p (i n) -> p i n", i=4)).then_inc(set_w, 1)
            for b in range(4):
                act.wait_ge(set_w, 5 + b)
                act.copy(phiT[:, 512 * b:512 * b + 512], bank[:, 6 + b % 2, :]).then_inc(e_phi, 1)
            at(xa0, -1)
            steps(act, xa0, first=0, last=NT - 2, looped=4)

            def stage(t, par):
                if not (num(t) and t < 2):
                    act.wait_ge(e_tr, t - 1)
                    act.sem_inc(passed_act, 1)
                act.copy(xs[:, par, :], tile(X, t)).then_inc(e_xs, 1)

            def dispatch(j, par):
                t = 2 * j + par
                if num(t) and t == -2:
                    stage(0, 0)
                if ok(t + 2):
                    act.wait_ge(e_tr, t + 3)
                    if not (num(t) and t < 0):
                        act.wait_ge(e_log, 4 * t + 4)
                    act.copy(xT[:, par, 0:P], bank[:, 3, 0:P]).then_inc(e_xT, 1)
                if ok(t + 3):
                    stage(t + 3, 1 - par)
                if ok(t + 2):
                    if not (num(t) and t < 0):
                        act.wait_ge(e_subD, t + 1)
                        act.wait_ge(e_subC, t + 1)
                    for b in range(4):
                        act.wait_ge(e_log, 4 * (t + 2) + b + 1)
                        act.copy(lgc[:, par, 512 * b:512 * b + 512], bank[:, 2 * (b % 2), :]).then_inc(e_lgc, 1)
                if ok(t + 1):
                    act.wait_ge(e_subC, t + 2)
                    act.sem_inc(passed_act, 1)
                    A(tile(EC, t + 1), tile(EC, t + 1), ACT.Exp).then_inc(e_expC, 1)
                    act.wait_ge(e_subD, t + 2)
                    A(slots[:, 1 - par, :], slots[:, 1 - par, :], ACT.Exp).then_inc(e_expD, 1)
            act.wait_ge(x_ready, LN_XA0 + 3)
            at(dispatch, -2)
            at(xa0, NT - 1)
            at(dispatch, -1)
            at(xa0, NT)
            act.wait_ge(x_ready, LN_MOE)
            steps(act, dispatch, first=0)

            def xtl_T(b):
                act.wait_ge(y_tr, b + 1)
                act.copy(xtlT[:, 4 * b:4 * b + 4, :], bank[:, b, :].rearrange("p (c n) -> p c n", c=4)).then_inc(y_trc, 1)

            for b in range(4):
                act.wait_ge(y_ve, 3 * b + 3)
                for c in range(4 * b, 4 * b + 4):
                    ins = A(xtl[:, c, :], xtl[:, c, :], ACT.Tanh, bias=bof[:, c:c + 1], scale=brs[:, c:c + 1])
                ins.then_inc(y_tanh, 1)
                if b > 0:
                    xtl_T(b - 1)
            xtl_T(3)

            act.wait_ge(y_out, 4)

            def combine(j, par):
                t = 2 * j + par
                if ok(t + 1):
                    for b in range(2):
                        act.wait_ge(c_tr, 4 * (t + 1) + b + 1)
                        if b == 0 and not (num(t) and t < 1):
                            act.wait_ge(c_y, t)
                        act.copy(slotsT[:, 1 - par, 4 * b:4 * b + 4, :], bank[:, b, :].rearrange("p (c n) -> p c n", c=4)).then_inc(c_ca, 1)
            steps(act, combine, last=NT - 2)

            def retention(j, par):
                t = 2 * j + par
                if ok(t + 2):
                    act.wait_ge(r_tr, t + 3)
                    if not (num(t) and t < 0):
                        act.wait_ge(r_qkv, t + 1)
                    act.copy(xT[:, par, 0:P], bank[:, 1, 0:P]).then_inc(r_xT, 1)
                if ok(t + 1):
                    act.wait_ge(r_cr, t + 2)
                    if not (num(t) and t < 1):
                        act.wait_ge(r_r, t)
                    act.copy(crs[:, 1 - par, :], bank[:, 0, 3 * P:4 * P]).then_inc(r_crc, 1)
                if ok(t + 2):
                    act.wait_ge(r_qkv, t + 3)
                    if not (num(t) and t < 0):
                        act.wait_ge(r_s, 2 * t + 2)
                        act.wait_ge(r_qe, t + 1)
                        act.wait_ge(r_cr, t + 1)
                    act.copy(qkT[:, par, :], bank[:, 0, 0:2 * P]).then_inc(r_qk, 1)
                if ok(t):
                    act.wait_ge(r_pv, t + 1)
                    if not (num(t) and t < 2):
                        act.wait_ge(r_sel, t - 1)
                    act.copy(rpo[:, par, :, :], bank[:, 6, :].rearrange("p (r n) -> p r n", r=4)).then_inc(r_po, 1)
            at(retention, -2)
            at(combine, NT - 1)
            at(retention, -1)
            at(combine, NT)
            steps(act, retention, first=0, last=NT - 2)

            act.preload_act_table_set("exp_and_others")
            xa1 = attention(1, LN_XA1)
            act.wait_ge(r_rd, 2 * NT)
            at(xa1, -2)
            at(retention, NT - 1)
            at(xa1, -1)
            at(retention, NT)
            act.wait_ge(x_ready, LN_XA1)
            at(xa1, 0)
            at(xa1, 1)
            act.wait_ge(f_wt, 1)
            act.copy(bT[0:R, 0:FF], bank[0:R, 6, :]).then_inc(f_wc, 1)
            act.wait_ge(f_wt, 2)
            act.copy(bT[0:R, FF:FF + D], bank[0:R, 7, 0:D]).then_inc(f_wc, 1)
            act.wait_ge(f_wt, 3)
            act.copy(w1T, bank[:, 6, :]).then_inc(f_wc, 1)
            act.wait_ge(f_wt, 4)
            act.copy(w2T, bank[:, 7, :].rearrange("p (c n) -> p c n", c=FC)).then_inc(f_wc, 1)
            steps(act, xa1, first=2, last=NT - 2)

            def step(j, par):
                g = 2 * j + par
                act.wait_ge(f_tr, g + 1)
                if not (num(g) and g < 2):
                    act.wait_ge(f_h, 4 * (g - 1))
                act.copy(fxT[:, par, :], bank[:, 0, :]).then_inc(f_xT, 1)
                for c in range(FC):
                    act.wait_ge(f_h, 4 * g + c + 1)
                    if c == 0 and not (num(g) and g < 2):
                        act.wait_ge(f_o, g - 1)
                    A(hT[:, par, c, :], bank[:, 2 + c, :], ACT.Gelu, bias=bfcr[:, c:c + 1]).then_inc(f_g, 1)
            step(0, 0)
            at(xa1, NT - 1)
            step(0, 1)
            at(xa1, NT)
            with act.Fori(1, G // 2) as j:
                step(j, 0)
                step(j, 1)

        @block.vector
        def _(dve):
            TT, TS, STT, RED = dve.tensor_tensor, dve.tensor_scalar, dve.scalar_tensor_tensor, dve.tensor_reduce

            def ln_stats(e, par, acc, res, k):
                y = lny[:, par, 0:k, :] if k > 1 else lny[:, par, 0, :]
                TT(y, acc, res, ALU.add).then_inc(lny_s, 1)
                dve.wait_ge(lny_s, e + 1)
                for i in range(k):
                    ins = dve.bn_stats(lnst[:, par, i, :], lny[:, par, i, :])
                ins.then_inc(lnst_s, 1)
                dve.wait_ge(lnst_s, e + 1)
                dve.sem_inc(passed_dve, 1)
                for i in range(k):
                    ins = dve.bn_aggr(lnmv[:, par, i, :], lnst[:, par, i, :])
                ins.then_inc(lnmv_s, 1)

            def ln_norm(e, par, t, k):
                dve.wait_ge(lnrs_s, e + 1)
                for i in range(k):
                    ins = TS(tile(X, t + i), lny[:, par, i, :], lnmv[:, par, i, 0:1], lnrs[:, par, i:i + 1], ALU.subtract, ALU.mult)
                ins.then_inc(x_ready, 1)

            dve.memset(wx, 0.0).then_inc(set_w, 1)
            dve.memset(xTp[:, :, :, 0:KC - 1], 0.0)
            dve.wait_ge(ld_win, 32)
            for k in range(KC):
                ins = TT(wk[:, k, :], w_in[:, 0:DI], cwb[:, :, k], ALU.mult)
            ins.then_inc(set_v, 1)
            dve.wait_ge(ld_const, 96)
            dve.tensor_copy(identb[:, :], ident[:, :])
            dve.tensor_copy(sel, bc(selcol[:, :].unsqueeze(2), P))
            dve.wait_ge(ld_mamba, 16 * 10)

            for g in range(G):
                gw = slice(GW * g, GW * g + GW)
                n = 3 * g
                dve.wait_ge(m_dtin, g + 1)
                dve.tensor_copy(Bs[:, gw], bank[:, 7, :]).then_inc(m_split, 1)
                dve.wait_ge(m_split, n + 1)
                TT(bres, bank[:, 7, :], Bs[:, gw], ALU.subtract).then_inc(m_split, 1)
                dve.wait_ge(m_split, n + 2)
                dve.tensor_copy(Bs[64:128, gw], bres[64:128, :]).then_inc(m_split, 1)
                dve.wait_ge(m_split, n + 3)
                TT(Bs[96:128, gw], bres[96:128, :], Bs[96:128, gw], ALU.subtract).then_inc(m_bs, 1)
                dve.wait_ge(m_abs, 2 * g + 2)
                for c in range(NC):
                    ins = TS(sp_r[:, c, :], bank[:, 5 + c, :], bdt[:, c:c + 1], 0.0, ALU.add, ALU.max)
                ins.then_inc(m_relu, 1)
                dve.wait_ge(m_relu, g + 1)
                dve.wait_ge(m_ln1, 2 * g + 2)
                TT(dt_all[:, :, gw], sp_r, sp_l, ALU.add).then_inc(m_dt, 1)
                dve.wait_ge(m_dt, g + 1)
                TT(dtx_all[:, :, gw], dt_all[:, :, gw], xconv[:, :, gw], ALU.mult).then_inc(m_dtx, 1)
            dve.wait_ge(m_A, 1)
            TS(Am, Am, -1.0, None, ALU.mult).then_inc(m_A, 1)
            dve.wait_ge(m_dtx, G)

            def times_B(g, q):
                pp = 4 * g + q
                dve.wait_ge(m_bc, pp + 1)
                if not (num(g) and g == 0 and q < 2):
                    dve.wait_ge(m_sum, 2 * pp - 3)
                TT(hb[2 * q % 4].rearrange("p (s n) -> p s n", s=4), Bb[:, q % 2, :].rearrange("p (s n) -> p s n", s=4),
                   mid(dtx_all[:, 0, ds(GW * g, GW)], 4), ALU.mult).then_inc(m_dBx, 1)

            def scan(g, q, c):
                pp = 4 * g + q
                dve.wait_ge(m_dA, 2 * pp + c + 1)
                dve.wait_ge((m_dBx, m_dBp)[c], pp + 1)
                h = hb[(2 * q + c) % 4]
                dve.tensor_tensor_scan(h, dA[:, c, :], h, 0.0, ALU.mult, ALU.add).then_inc(m_h, 1)

            def gate(g, c):
                dve.wait_ge(m_sum, 8 * g + 6 + c + 1)
                if not (num(g) and g == 0):
                    dve.wait_ge(m_o, g)
                n = 4 * g + 2 * c
                STT(yTm[:, c, :], xconv[:, c, ds(GW * g, GW)], Dv[:, c:c + 1], bank[:, 4 + c, :], ALU.mult, ALU.add).then_inc(m_y, 1)
                dve.wait_ge(m_y, n + 1)
                TT(yTm[:, c, :], yTm[:, c, :], sz[:, c, ds(GW * g, GW)], ALU.mult).then_inc(m_y, 1)

            def block_stats(g, par):
                dve.wait_ge(m_o, g + 1)
                ln_stats(g, par, bank[:, 7, :].rearrange("p (j n) -> p j n", j=GT), tile(X, GT * g, GT), GT)

            def group(g, par):
                for q in range(4):
                    times_B(g, q)
                    scan(g, q, 0)
                    if not (num(g) and g == 0):
                        if q == 0:
                            gate(g - 1, 0)
                            gate(g - 1, 1)
                        if q == 1:
                            block_stats(g - 1, 1 - par)
                        if q == 3:
                            ln_norm(g - 1, 1 - par, GT * (g - 1), GT)
                    scan(g, q, 1)
            dve.wait_ge(ld_x, 16)
            dve.wait_ge(m_dz, 1)
            pairs(dve, G, lambda j, par: group(2 * j + par, par))
            gate(G - 1, 0)
            gate(G - 1, 1)
            block_stats(G - 1, 1)
            ln_norm(G - 1, 1, GT * (G - 1), GT)

            def attention(lay, ln0):
                def mask_bias(j, par, t):
                    dve.wait_ge(ld_mask[par], 16 * (j + 1))
                    if not (num(t) and t < 2):
                        dve.wait_ge(a_s, 2 * (t - 1))
                        dve.wait_ge(a_exp, 2 * (t - 1))
                    TS(mflag[:, par, :], maskb[:, par, :], 0.0, None, ALU.is_equal).then_inc(a_flag, 1)
                    dve.wait_ge(a_flag, 2 * t + 1)
                    TS(mbias[:, par, :], mflag[:, par, :], MASKED, None, ALU.mult).then_inc(a_mb, 1)
                    RED(allm[:, par, :], mflag[:, par, :], AX.X, ALU.min).then_inc(a_flag, 1)
                    dve.wait_ge(a_flag, 2 * t + 2)
                    TS(escale[:, par, :], allm[:, par, :], -(HD ** -0.5), HD ** -0.5, ALU.mult, ALU.add).then_inc(a_esc, 1)

                def shift(u, par, hf):
                    dve.wait_ge(a_s, 2 * u + hf + 1)
                    if hf == 0 and not (num(u) and u < 2):
                        dve.wait_ge(a_pt, 4 * (u - 1))
                    s = bank[:, 2 + 2 * hf:4 + 2 * hf, 0:4 * SK].rearrange("p b (h n) -> p b h n", h=4)
                    m = nmx[:, par, 8 * hf:8 * hf + 8, :].rearrange("p (b h) n -> p b h n", b=2)
                    RED(m.rearrange("p b h n -> p b (h n)"), s, AX.X, ALU.max).then_inc(a_max, 1)
                    dve.wait_ge(a_max, 2 * u + hf + 1)
                    TT(sc[:, par, 8 * hf:8 * hf + 8, :].rearrange("p (b h) n -> p b h n", b=2), s,
                       m.to_broadcast([P, 2, 4, SK]), ALU.subtract).then_inc(a_sub, 1)

                dve.memset(vaug[:, :, :, HD + 1:32], 0.0)
                dve.memset(vaug[:, :, :, HD:HD + 1], 1.0)

                def step(j, par):
                    t = 2 * j + par
                    u = NT * lay + t
                    if ok(t + 1):
                        shift(u + 1, 1 - par, 0)
                    if ok(t - 1):
                        dve.wait_ge(a_sel, u)
                        o = bank[:, 1, 0:NH * (HD + 1)].rearrange("p (h n) -> p h n", h=NH)
                        dve.reciprocal(rden[:, 1 - par, :, :], o[:, :, HD:HD + 1]).then_inc(a_rden, 1)
                        dve.wait_ge(a_rden, u)
                        if not (num(u) and u < 3):
                            dve.wait_ge(a_ot, u - 2)
                        TT(on[:, 1 - par, :].rearrange("p (h n) -> p h n", h=NH), o[:, :, 0:HD], bc(rden[:, 1 - par, :, :], HD), ALU.mult).then_inc(a_on, 1)
                    if ok(t + 1):
                        shift(u + 1, 1 - par, 1)
                    if ok(t - 2):
                        ln_norm(ln0 + t - 2, par, t - 2, 1)
                    if ok(t - 1):
                        dve.wait_ge(a_out, u)
                        dve.wait_ge(a_xr, u)
                        ln_stats(ln0 + t - 1, 1 - par, bank[:, 1, 0:D], xr[:, 1 - par, :], 1)
                    if ok(t + 2):
                        if lay == 0:
                            mask_bias(j + 1, par, t + 2)
                        dve.wait_ge(a_qk, u + 3)
                        if not (num(u) and u < 0):
                            dve.wait_ge(a_pv, u + 1)
                        dve.tensor_copy(vaug[0:SK, par, :, 0:HD], bank[0:SK, 0, 256:384].rearrange("p (h n) -> p h n", h=NH)).then_inc(a_v, 1)
                return step

            def output_bias(lay):
                dve.wait_ge(a_bvo, lay + 1)
                TT(abr[:, lay, :], abr[:, lay, :], bank[:, 7, 0:D], ALU.add).then_inc(a_bias, 1)

            dve.wait_ge(ld_attn, 16 * 12)
            dve.memset(slots[:, 0, :], 0.0).then_inc(set_w, 1)
            xa0 = attention(0, LN_XA0)
            output_bias(0)
            at(xa0, -2)
            output_bias(1)
            dve.wait_ge(ld_moe, 64)
            dve.tensor_copy(phib[:, :], slots[:, 0, :]).then_inc(e_pb, 1)
            dve.wait_ge(e_pb, 1)
            TT(slots[:, 1, :], slots[:, 0, :], phib[:, :], ALU.subtract).then_inc(e_pb, 1)
            dve.wait_ge(e_pb, 2)
            dve.tensor_copy(phib[64:128, :], slots[64:128, 1, :]).then_inc(e_pb, 1)
            dve.wait_ge(e_pb, 3)
            TT(phib[96:128, :], slots[96:128, 1, :], phib[96:128, :], ALU.subtract).then_inc(e_pb, 1)
            at(xa0, -1)
            steps(dve, xa0, first=0, last=NT - 1, looped=4)

            def dispatch(j, par):
                t = 2 * j + par
                lg = lgc[:, 1 - par, :].rearrange("p (n s) -> p n s", s=PS)
                if ok(t + 1):
                    dve.wait_ge(e_lgc, 4 * (t + 1) + 4)
                    if not (num(t) and t < 1):
                        dve.wait_ge(e_rC, t)
                    RED(mxp[:, 1 - par, :], lg.rearrange("p n s -> p s n"), AX.X, ALU.max).then_inc(e_mxp, 1)
                if ok(t):
                    dve.wait_ge(e_expD, t + 1)
                    RED(mxn[:, par, :], slots[:, par, :].rearrange("p (n s) -> p n s", s=PS), AX.X, ALU.add).then_inc(e_sum, 1)
                    dve.wait_ge(e_sum, t + 1)
                    dve.reciprocal(rD[:, par, :], mxn[:, par, :]).then_inc(e_rD, 1)
                if ok(t + 1):
                    if not (num(t) and t < 1):
                        dve.wait_ge(e_rD, t)
                    RED(mxn[:, 1 - par, :], lg, AX.X, ALU.max).then_inc(e_mxn, 1)
                    dve.wait_ge(e_mxn, t + 2)
                    if not (num(t) and t < 1):
                        dve.wait_ge(e_xt, t)
                    TT(slots[:, 1 - par, :].rearrange("p (n s) -> p n s", s=PS), lg, bc(mxn[:, 1 - par, :].unsqueeze(2), PS), ALU.subtract).then_inc(e_subD, 1)
                if ok(t):
                    dve.wait_ge(e_sum32, t + 1)
                    RED(mxp[:, par, :], bank[:, 1, :].rearrange("p (n s) -> p s n", s=PS), AX.X, ALU.add).then_inc(e_sumC, 1)
                    dve.wait_ge(e_sumC, t + 1)
                    dve.reciprocal(tile(rC, t), mxp[:, par, :]).then_inc(e_rC, 1)
            at(dispatch, -1)
            at(xa0, NT)
            ln_norm(LN_XA0 + NT - 1, 1, NT - 1, 1)
            steps(dve, dispatch, first=0)

            bst = lny[:, :, :, :].rearrange("p b j n -> p (b j n)")[:, 0:EC_N * 6].rearrange("p (c n) -> p c n", n=6)
            for b in range(4):
                dve.wait_ge(y_xt, b + 1)
                TS(xtl[:, 4 * b:4 * b + 4, :], bank[:, 4 + b, :].rearrange("p (c n) -> p c n", n=D), -33000.0, 65000.0, ALU.max, ALU.min).then_inc(y_clip, 1)
                dve.wait_ge(y_clip, b + 1)
                for c in range(4 * b, 4 * b + 4):
                    ins = dve.bn_stats(bst[:, c, :], xtl[:, c, :])
                ins.then_inc(y_mv, 1)
                dve.wait_ge(y_mv, 2 * b + 1)
                for c in range(4 * b, 4 * b + 4):
                    ins = dve.bn_aggr(sm[:, 2 * c:2 * c + 2], bst[:, c, :])
                ins.then_inc(y_mv, 1)
            dve.wait_ge(e_rC, NT)
            for b in range(4):
                dve.wait_ge(y_mm, b + 1)
                dve.tensor_copy(Yt[:, 4 * b:4 * b + 4, :], bank[:, 4 + b, :].rearrange("p (c n) -> p c n", n=D)).then_inc(y_out, 1)

            def combine(j, par):
                t = 2 * j + par
                if ok(t + 2):
                    if num(t) and t == 1:
                        dve.wait_ge(y_mm, 4)
                    if not (num(t) and t < 2):
                        dve.wait_ge(c_tr, 4 * t + 4)
                    v = tile(EC, t + 2).rearrange("p (n s) -> p n s", s=PS)
                    dst = v if in_place(t + 2) else slots[:, par, :].rearrange("p (n s) -> p n s", s=PS)
                    TT(dst[:, NP:NE, :], v[:, NP:NE, :], mid(tile(rC, t + 2), NE - NP), ALU.mult).then_inc(c_nv, 1)
                if ok(t + 1):
                    for b in range(2, 4):
                        dve.wait_ge(c_tr, 4 * (t + 1) + b + 1)
                        if b == 2 and not (num(t) and t < 1):
                            dve.wait_ge(c_y, t)
                        dve.tensor_copy(slotsT[:, 1 - par, 4 * b:4 * b + 4, :], bank[:, b, :].rearrange("p (c n) -> p c n", c=4)).then_inc(c_cv, 1)
                if ok(t - 1):
                    ln_norm(LN_MOE + t - 1, 1 - par, t - 1, 1)
                if ok(t):
                    dve.wait_ge(c_y, t + 1)
                    ln_stats(LN_MOE + t, par, bank[:, 4 + par, 0:D], tile(X, t), 1)
            steps(dve, combine, last=NT - 2)

            dve.wait_ge(ld_ret, 16 * 5)
            STT(kvbd.rearrange("p (h e) -> p h e", e=HD), mid(kvl, NH), float(NH * HD), bc(hmask[:, :].unsqueeze(2), HD), ALU.mult, ALU.mult).then_inc(set_v, 1)

            dve.memset(vpad[:, :, :, HD:32], 0.0)

            def decayed(t, par, hf):
                dve.wait_ge(r_s, 2 * t + hf + 1)
                if hf == 0 and not (num(t) and t < 2):
                    dve.wait_ge(r_pv, t - 1)
                TT(rd[:, par, 8 * hf:8 * hf + 8, :].rearrange("p (b h) n -> p b (h n)", b=2), bank[:, 2 + 2 * hf:4 + 2 * hf, :],
                   decay[:, 8 * hf:8 * hf + 8, :].rearrange("p (b h) n -> p b (h n)", b=2), ALU.mult).then_inc(r_rd, 1)

            def retention(j, par):
                t = 2 * j + par
                q = 1 - par
                if ok(t - 1):
                    dve.wait_ge(r_sel, t)
                    dve.wait_ge(r_crc, t)
                    TT(gr[:, q, :], bank[:, 7, 0:D], crs[:, q, :], ALU.add).then_inc(r_r, 1)
                    dve.wait_ge(r_r, t)
                    dve.bn_stats(gst[:, q, :], gr[:, q, :]).then_inc(r_d, 1)
                    dve.wait_ge(r_d, 3 * t - 2)
                    dve.sem_inc(passed_dve, 1)
                    dve.bn_aggr(gmv[:, q, :], gst[:, q, :]).then_inc(r_mv, 1)
                if ok(t - 2):
                    dve.wait_ge(r_rs, t - 1)
                    TS(gt1[:, par, :], gr[:, par, :], gsc[:, par, 0:1], gsc[:, par, 3:4], ALU.subtract, ALU.mult).then_inc(r_t1, 1)
                    dve.wait_ge(r_t1, 2 * t - 3)
                    TT(gt2[:, par, :].rearrange("p (h e) -> p h e", e=HD), gt1[:, par, :].rearrange("p (h e) -> p h e", e=HD),
                       bc(gnw.unsqueeze(2), HD), ALU.mult).then_inc(r_t1, 1)
                    dve.wait_ge(r_t1, 2 * t - 2)
                    dve.wait_ge(r_xr, t - 1)
                    ln_stats(LN_RET + t - 2, par, gt2[:, par, :], xr[:, par, :], 1)
                if ok(t + 1):
                    decayed(t + 1, q, 0)
                if ok(t - 1):
                    dve.wait_ge(r_m1, t)
                    dve.tensor_copy(gsc[:, q, 0:1], bank[:, 7, P:P + 1]).then_inc(r_d, 1)
                    dve.wait_ge(r_d, 3 * t - 1)
                    TT(gsc[:, q, 1:2], gmv[:, q, 0:1], gsc[:, q, 0:1], ALU.subtract).then_inc(r_d, 1)
                    dve.wait_ge(r_d, 3 * t)
                    TS(gmv[:, q, 0:1], gsc[:, q, 1:2], gsc[:, q, 1:2], gmv[:, q, 1:2], ALU.mult, ALU.add).then_inc(r_v2, 1)
                if ok(t + 1):
                    decayed(t + 1, q, 1)
                if ok(t + 2):
                    dve.wait_ge(r_qk, t + 3)
                    if not (num(t) and t < 0):
                        dve.wait_ge(r_pv, t + 1)
                    dve.tensor_copy(vpad[:, par, :, 0:HD], bank[:, 0, 2 * P:3 * P].rearrange("p (h n) -> p h n", h=NH)).then_inc(r_v, 1)
                if ok(t - 1):
                    dve.wait_ge(r_m2, t)
                    TS(gsc[:, q, 2:3], bank[:, 7, P + 1:P + 2], LN_EPS, None, ALU.add).then_inc(r_ve, 1)
                if ok(t - 2):
                    ln_norm(LN_RET + t - 2, par, t - 2, 1)
            at(retention, -2)
            at(combine, NT - 1)
            at(retention, -1)
            at(combine, NT)
            at(retention, 0)
            dve.wait_ge(ld_ffn, 16 * 8)
            RED(amx[:, 0:1], wf1.rearrange("p c n -> p (c n)"), AX.X, ALU.max, apply_absolute_value=True)
            RED(amx[:, 1:2], wf2, AX.X, ALU.max, apply_absolute_value=True).then_inc(f_w, 1)
            steps(dve, retention, first=1, last=NT - 2)

            xa1 = attention(1, LN_XA1)
            at(xa1, -2)
            dve.wait_ge(f_w, 2)
            TS(amx[:, 4:6], amx[:, 2:4], 1.0 / QMAX, None, ALU.mult).then_inc(f_wp, 1)
            dve.wait_ge(f_wp, 1)
            dve.reciprocal(amx[:, 6:8], amx[:, 4:6]).then_inc(f_wp, 1)
            dve.wait_ge(f_wp, 2)

            def fake_quant(i, w, tq):
                n = 2 + 5 * i
                TS(tq, w, amx[:, 6 + i:7 + i], ROUND, ALU.mult, ALU.add).then_inc(f_wp, 1)
                dve.wait_ge(f_wp, n + 1)
                TS(tq, tq, ROUND, QMAX, ALU.subtract, ALU.min).then_inc(f_wp, 1)
                dve.wait_ge(f_wp, n + 2)
                TS(tq, tq, -QMAX - 1.0, amx[:, 4 + i:5 + i], ALU.max, ALU.mult).then_inc(f_wp, 1)
                dve.wait_ge(f_wp, n + 3)
                TT(tq, tq, w, ALU.subtract).then_inc(f_wp, 1)
                dve.wait_ge(f_wp, n + 4)
                TT(w, w, tq, ALU.add).then_inc(f_wp, 1)

            fake_quant(0, wf1.rearrange("p c n -> p (c n)"), tq1)
            at(retention, NT - 1)
            dve.wait_ge(r_pv, NT)
            at(xa1, -1)
            fake_quant(1, wf2, tq2)
            TS(afc[0:R, :], afc[0:R, :], 2.0, None, ALU.mult)
            TS(apj[0:R, :], apj[0:R, :], 2.0, None, ALU.mult).then_inc(f_wp, 1)
            at(retention, NT)
            at(retention, NT + 1)
            steps(dve, xa1, first=0)
            ln_norm(LN_XA1 + NT - 1, 1, NT - 1, 1)

            def step(j, par):
                g = 2 * j + par
                if not (num(g) and g == 0):
                    ln_norm(LN_FFN + g - 1, 1 - par, GT * (g - 1), GT)
                dve.wait_ge(f_o, g + 1)
                dve.wait_ge(f_xs, 2 * g + 2)
                ln_stats(LN_FFN + g, par, bank[:, 6 + par, :].rearrange("p (j n) -> p j n", j=GT), fr4[:, par, :, :], GT)
            pairs(dve, G, step)
            ln_norm(LN_FFN + G - 1, 1, GT * (G - 1), GT)

        @block.tensor
        def _(pe):
            MM = pe.matmul
            I = ident[:, :]
            def transpose_x(g):
                par = g % 2
                pe.wait_ge(ld_xs4[par], 16 * (g // 2 + 1))
                if g >= 1:
                    pe.wait_ge(m_xT, g)
                for j in range(GT):
                    ins = pe.transpose(bank[:, 0, P * j:P * j + P], xs4[:, par, j, :], I)
                ins.then_inc(m_tr, 1)

            def project(g):
                par = g % 2
                pe.wait_ge(m_xT, g + 1)
                if g == 0:
                    pe.wait_ge(set_v, 1)
                for c in range(NC):
                    if g >= 1:
                        pe.wait_ge(m_silu, 2 * (g - 1) + c + 1)
                    for k in range(KC):
                        ins = MM(bank[:, 1 + c, :], wk[:, k, P * c:P * c + P], xTp[:, par, :, k:k + P], start=(k == 0), stop=(k == KC - 1))
                    ins.then_inc(m_mm, 1)
                for c in range(NC):
                    if g >= 1:
                        pe.wait_ge(m_silz, 2 * (g - 1) + c + 1)
                    MM(bank[:, 3 + c, :], w_in[:, DI + P * c:DI + P * c + P], xTp[:, par, :, KC - 1:], start=True, stop=True).then_inc(m_mm, 1)

            def steps_and_B(g):
                gw = slice(GW * g, GW * g + GW)
                pe.wait_ge(m_silu, 2 * g + 2)
                if g >= 1:
                    pe.wait_ge(m_bs, g)
                for c in range(NC):
                    ins = MM(bank[:, 7, :], wx[:, c, :], xconv[:, c, gw], start=(c == 0), stop=(c == NC - 1))
                ins.then_inc(m_wx, 1)
                pe.wait_ge(m_dtin, g + 1)
                if g >= 1:
                    pe.wait_ge(m_relu, g)
                for c in range(NC):
                    MM(bank[:, 5 + c, :], wdt[0:R, P * c:P * c + P], dtin[0:R, :], start=True, stop=True).then_inc(m_dtp, 1)

            pe.wait_ge(ld_const, 96)
            transpose_x(0)
            for g in range(G + 1):
                if g < G:
                    project(g)
                if g < G - 1:
                    transpose_x(g + 1)
                if g > 0:
                    steps_and_B(g - 1)

            def spread(g, q):
                pp = 4 * g + q
                if not (num(g) and g == 0 and q == 0):
                    pe.wait_ge(m_bc, pp)
                for i in range(4):
                    ins = MM(bank[:, i, :], sel[:, 4 * q + i, :], Bs[:, ds(GW * g, GW)], start=True, stop=True)
                ins.then_inc(m_B, 1)

            def sum_states(g, q, c):
                pe.wait_ge(m_h, 8 * g + 2 * q + c + 1)
                if q == 0 and not (num(g) and g == 0):
                    pe.wait_ge(m_y, 4 * (g - 1) + 2 * c + 1)
                for i in ((2, 3, 0) if c == 0 else (0, 1, 2, 3)):
                    if c == 0 and i == 0:
                        pe.wait_ge(m_add, 4 * g + q + 1)
                    ins = MM(bank[:, 4 + c, :], I, hb[(2 * q + c) % 4][:, GW * i:GW * i + GW],
                             start=(q == 0 and i == 2 - 2 * c), stop=(q == 3 and i == 3 * c))
                ins.then_inc(m_sum, 1)

            def project_out(g):
                pe.wait_ge(m_y, 4 * g + 4)
                if not (num(g) and g == 0):
                    pe.wait_ge(lny_s, g)
                for j in range(GT):
                    for c in range(NC):
                        ins = MM(bank[:, 7, P * j:P * j + P], yTm[:, c, P * j:P * j + P], wout[:, c, :], start=(c == 0), stop=(c == NC - 1))
                ins.then_inc(m_o, 1)

            def scans(g):
                for q in range(4):
                    sum_states(g, q, 0)
                    if q < 2:
                        spread(g, q + 2)
                    elif not (num(g) and g == G - 1):
                        spread(g + 1, q - 2)
                    sum_states(g, q, 1)
                    if q == 0 and not (num(g) and g == 0):
                        project_out(g - 1)
            pe.wait_ge(m_bs, G)
            pe.wait_ge(m_dtx, G)
            spread(0, 0)
            spread(0, 1)
            scans(0)
            scans(1)
            with pe.Fori(2, G - 1) as g:
                scans(g)
            scans(G - 1)
            project_out(G - 1)

            def attention(lay, ln0):
                wq, wkk, wv, wo = (wa[:, lay, i, :] for i in range(4))
                def scores(u, par, hf):
                    if hf == 0:
                        pe.wait_ge(a_kexp, u + 1)
                        if lay == 0:
                            pe.wait_ge(a_mb, u + 1)
                    if not (num(u) and u == 0):
                        pe.wait_ge(a_sub, 2 * (u - 1) + hf + 1)
                    for b in (2 * hf, 2 * hf + 1):
                        ins = MM(bank[:, 2 + b, 0:4 * SK], qT[:, par, :], kexp[:, par, 4 * b:4 * b + 4, :], start=True, stop=(lay == 1))
                        if lay == 0:
                            ins = MM(bank[:, 2 + b, 0:4 * SK].rearrange("p (h n) -> p h n", h=4), identb[:, :], mid(mbias[:, par, :], 4), start=False, stop=True)
                    ins.then_inc(a_s, 1)

                def probs_T(u, par, r):
                    if r % 2 == 0:
                        pe.wait_ge(a_exp, 2 * u + r // 2 + 1)
                    if r == 0 and not (num(u) and u == 0):
                        pe.wait_ge(a_po, u)
                    if r > 0 and not (num(u) and u == 0 and r == 1):
                        pe.wait_ge(a_ptc, 4 * u + r - 1)
                    for i in range(4):
                        ins = pe.transpose(bank[0:SK, 6 + r % 2, P * i:P * i + P], sc[:, par, 4 * r + i, :], I)
                    ins.then_inc(a_pt, 1)

                def step(j, par):
                    t = 2 * j + par
                    u = NT * lay + t
                    if ok(t + 2):
                        pe.wait_ge(a_xs, u + 3)
                        pe.wait_ge(ld_ctx[par], 16 * (8 * lay + j + 2))
                    if not (num(t) and t < 2):
                        pe.wait_ge(lny_s, ln0 + t - 1)
                    if ok(t + 2):
                        pe.transpose(bank[:, 1, 0:P], xs[:, par, :], I)
                        pe.transpose(bank[:, 1, P:P + SK], ctxb[0:SK, par, :], ident[0:SK, 0:SK]).then_inc(a_tr, 1)
                    if ok(t + 1):
                        scores(u + 1, 1 - par, 0)
                    if ok(t + 2):
                        pe.wait_ge(a_xT, u + 3)
                        if not (num(u) and u < -1):
                            pe.wait_ge(a_qk, u + 2)
                            pe.wait_ge(a_v, u + 2)
                        MM(bank[:, 0, 0:P], wq, xT[:, par, 0:P], start=True, stop=True)
                        MM(bank[:, 0, P:P + SK], wkk, xT[:, par, P:P + SK], start=True, stop=True)
                        MM(bank[0:SK, 0, 256:384], xT[:, par, P:P + SK], wv, start=True, stop=True).then_inc(a_qkv, 1)
                    if ok(t - 1):
                        pe.wait_ge(a_po, u)
                        for r in range(4):
                            ins = MM(bank[:, 1, 36 * r:36 * r + 36], poT[:, 1 - par, r, :], sel9[:, :], start=True, stop=True)
                        ins.then_inc(a_sel, 1)
                    if ok(t + 1):
                        scores(u + 1, 1 - par, 1)
                    if ok(t):
                        probs_T(u, par, 0)
                    if ok(t - 1):
                        pe.wait_ge(a_on, u)
                        pe.transpose(bank[:, 1, 0:D], on[:, 1 - par, :], I).then_inc(a_ot, 1)
                    if ok(t):
                        probs_T(u, par, 1)
                    if ok(t - 1):
                        pe.wait_ge(a_otc, u)
                        MM(bank[:, 1, 0:D], oT[:, 1 - par, :], wo, start=True, stop=True).then_inc(a_out, 1)
                    if ok(t):
                        probs_T(u, par, 2)
                        probs_T(u, par, 3)
                        pe.wait_ge(a_v, u + 1)
                        for r in range(4):
                            if r in (0, 3):
                                pe.wait_ge(a_ptc, 4 * u + (3 if r == 0 else 4))
                            for i in range(4):
                                ins = MM(bank[32 * i:32 * i + 32, 6, P * r:P * r + P], vaug[0:SK, par, 4 * r + i, :], pT[0:SK, par, 4 * r + i, :],
                                         start=True, stop=True, skip_group_check=True)
                        ins.then_inc(a_pv, 1)
                return step

            pe.wait_ge(ld_attn, 16 * 12)
            def output_bias(lay):
                MM(bank[:, 7, 0:D], ab[:, lay, 2:3].to_broadcast([P, P]), wa[:, lay, 3, :], start=True, stop=True).then_inc(a_bvo, 1)

            pe.wait_ge(x_ready, LN_XA0)
            output_bias(0)
            xa0 = attention(0, LN_XA0)
            at(xa0, -2)
            pe.wait_ge(ld_xa1, 64)
            pe.wait_ge(set_w, 2)
            for i in range(4):
                ins = pe.transpose(bank[:, 6, P * i:P * i + P], wraw[:, i, :], I)
            ins.then_inc(set_w, 1)
            pe.wait_ge(set_w, 4)
            pe.wait_ge(a_bias, 1)
            output_bias(1)
            pe.wait_ge(ld_moe, 64)
            for b in range(4):
                if b == 1:
                    pe.wait_ge(a_bias, 2)
                if b >= 2:
                    pe.wait_ge(e_phi, b - 1)
                for i in range(4):
                    ins = pe.transpose(bank[:, 6 + b % 2, P * i:P * i + P], phir[:, 4 * b + i, :], I)
                ins.then_inc(set_w, 1)
            at(xa0, -1)
            pe.wait_ge(e_phi, 4)
            steps(pe, xa0, first=0, last=NT - 2)

            def dispatch(j, par):
                t = 2 * j + par
                if ok(t + 2):
                    pe.wait_ge(e_xs, t + 3)
                    if not (num(t) and t < -1):
                        pe.wait_ge(e_xT, t + 2)
                    pe.transpose(bank[:, 3, 0:P], xs[:, par, :], I).then_inc(e_tr, 1)
                if ok(t - 1):
                    pe.wait_ge(e_Dn, t)
                    for c in range(EC_N):
                        ins = MM(bank[:, 4 + c // 4, P * (c % 4):P * (c % 4) + P], slots[:, 1 - par, P * c:P * c + P], tile(X, t - 1),
                                 start=(num(t) and t == 1 and c % 4 == 0), stop=(num(t) and t == NT), skip_group_check=True)
                        if num(t) and t == NT and c % 4 == 3:
                            ins.then_inc(y_xt, 1)
                    if not (num(t) and t == NT):
                        ins.then_inc(e_xt, 1)
                if ok(t + 2):
                    pe.wait_ge(e_xT, t + 3)
                    for b in range(4):
                        if b > 1 or not (num(t) and t < -1):
                            pe.wait_ge(e_lgc, 4 * (t + 2) + b - 1)
                        MM(bank[:, 2 * (b % 2), :], xT[:, par, 0:P], phiT[:, 512 * b:512 * b + 512], start=True, stop=False)
                        MM(bank[:, 2 * (b % 2), :], onesb[:, :], phib[:, 512 * b:512 * b + 512], start=False, stop=True).then_inc(e_log, 1)
                if ok(t):
                    pe.wait_ge(e_fold, t + 1)
                    if not (num(t) and t < 1):
                        pe.wait_ge(e_sumC, t)
                    MM(bank[:, 1, :], I, fold[:, 0:512], start=True, stop=False)
                    MM(bank[:, 1, :], I, fold[:, 512:1024], start=False, stop=True).then_inc(e_sum32, 1)
            pe.wait_ge(e_pb, 4)
            pe.wait_ge(a_qk, NT)
            pe.wait_ge(a_v, NT)
            pe.wait_ge(a_sub, 2 * NT)
            at(dispatch, -2)
            at(xa0, NT - 1)
            at(dispatch, -1)
            at(xa0, NT)
            pe.wait_ge(x_ready, LN_MOE)
            steps(pe, dispatch, first=0)

            pe.wait_ge(ld_eb, 16)
            for b in range(4):
                pe.wait_ge(y_clip, b + 1)
                MM(bank[:, 4 + b, :], sel4[0:4, :], phiT[0:4, 512 * b:512 * b + 512], start=True, stop=False, skip_group_check=True)
            pe.wait_ge(e_rC, NT)

            def experts(b):
                pe.wait_ge(y_trc, b + 1)
                pe.wait_ge(ld_ew[b], 16)
                for c in range(4 * b, 4 * b + 4):
                    for n in range(4):
                        ins = MM(bank[32 * n:32 * n + 32, 4 + b, P * (c % 4):P * (c % 4) + P], xtlT[:, c, 32 * n:32 * n + 32],
                                 ring[b % len(ring)][:, 4 * (c % 4) + n, :], start=False, stop=True, skip_group_check=True)
                ins.then_inc(y_mm, 1)

            for b in range(4):
                pe.wait_ge(y_tanh, b + 1)
                for i in range(4):
                    ins = pe.transpose(bank[:, b, P * i:P * i + P], xtl[:, 4 * b + i, :], I)
                ins.then_inc(y_tr, 1)
                if b > 0:
                    experts(b - 1)
            experts(3)

            pe.wait_ge(y_out, 4)

            def combine(j, par):
                t = 2 * j + par
                if ok(t + 1):
                    pe.wait_ge(c_np, t + 2)
                    pe.wait_ge(c_nv, t + 2)
                    for b in range(4):
                        if not (num(t) and t < 0):
                            if b < 2:
                                pe.wait_ge(c_ca, 2 * t + b + 1)
                            else:
                                pe.wait_ge(c_cv, 2 * t + b - 2 + 1)
                        for i in range(4):
                            src = EC[:, t + 1, :] if in_place(t + 1) else slots[:, 1 - par, :]
                            ins = pe.transpose(bank[:, b, P * i:P * i + P], src[:, P * (4 * b + i):P * (4 * b + i) + P], I)
                        ins.then_inc(c_tr, 1)
                if ok(t):
                    if not (num(t) and t < 2):
                        pe.wait_ge(lny_s, LN_MOE + t - 1)
                    pe.wait_ge(c_ca, 2 * t + 2)
                    pe.wait_ge(c_cv, 2 * t + 2)
                    for c in range(EC_N):
                        ins = MM(bank[:, 4 + par, 0:D], slotsT[:, par, c, :], Yt[:, c, :], start=(c == 0), stop=(c == EC_N - 1))
                    ins.then_inc(c_y, 1)
            steps(pe, combine, last=NT - 2)

            pe.wait_ge(ld_ret, 16 * 5)
            pe.wait_ge(set_v, 2)

            def scores(t, par, hf):
                if hf == 0:
                    pe.wait_ge(r_qe, t + 1)
                if not (num(t) and t == 0):
                    pe.wait_ge(r_rd, 2 * (t - 1) + hf + 1)
                for b in (2 * hf, 2 * hf + 1):
                    ins = MM(bank[:, 2 + b, :], qkT[:, par, P:2 * P], qexp[:, par, 4 * b:4 * b + 4, :], start=True, stop=True)
                ins.then_inc(r_s, 1)

            def retention(j, par):
                t = 2 * j + par
                if ok(t + 2):
                    pe.wait_ge(r_xs, t + 3)
                    if not (num(t) and t < -1):
                        pe.wait_ge(r_xT, t + 2)
                    pe.transpose(bank[:, 1, 0:P], xs[:, par, :], I).then_inc(r_tr, 1)
                if ok(t - 1):
                    pe.wait_ge(r_po, t)
                    if not (num(t) and t < 2):
                        pe.wait_ge(r_ve, t - 1)
                    for r in range(4):
                        ins = MM(bank[:, 7, 32 * r:32 * r + 32], rpo[:, 1 - par, r, :], sel8[:, :], start=True, stop=True)
                    ins.then_inc(r_sel, 1)
                if ok(t + 1):
                    pe.wait_ge(r_qk, t + 2)
                    pe.wait_ge(r_v, t + 2)
                    MM(bank[:, 0, 3 * P:4 * P], qkT[:, 1 - par, 0:P], kvbd, start=True, stop=True).then_inc(r_cr, 1)
                    scores(t + 1, 1 - par, 0)
                if ok(t + 2):
                    pe.wait_ge(r_xT, t + 3)
                    if not (num(t) and t < -1):
                        pe.wait_ge(r_crc, t + 2)
                    MM(bank[:, 0, 0:P], wqkv[:, 0:D], xT[:, par, 0:P], start=True, stop=True)
                    MM(bank[:, 0, P:2 * P], wqkv[:, D:2 * D], xT[:, par, 0:P], start=True, stop=True)
                    MM(bank[:, 0, 2 * P:3 * P], xT[:, par, 0:P], wqkv[:, 2 * D:3 * D], start=True, stop=True).then_inc(r_qkv, 1)
                if ok(t - 1):
                    pe.wait_ge(r_mv, t)
                    MM(bank[:, 7, P:P + 1], mean_w[:, :], gmv[:, 1 - par, 0:1], start=True, stop=True).then_inc(r_m1, 1)
                if ok(t + 1):
                    scores(t + 1, 1 - par, 1)
                if ok(t):
                    pe.wait_ge(r_v, t + 1)
                    pe.wait_ge(r_rd, 2 * t + 2)
                    if not (num(t) and t == 0):
                        pe.wait_ge(r_po, t)
                    for r in range(4):
                        for i in range(4):
                            ins = MM(bank[32 * i:32 * i + 32, 6, P * r:P * r + P], vpad[:, par, 4 * r + i, :], rd[:, par, 4 * r + i, :],
                                     start=True, stop=True, skip_group_check=True)
                    ins.then_inc(r_pv, 1)
                if ok(t - 1):
                    pe.wait_ge(r_v2, t)
                    MM(bank[:, 7, P + 1:P + 2], mean_w[:, :], gmv[:, 1 - par, 0:1], start=True, stop=True).then_inc(r_m2, 1)
            pe.wait_ge(c_ca, 2 * NT)
            pe.wait_ge(c_cv, 2 * NT)
            at(retention, -2)
            at(combine, NT - 1)
            pe.wait_ge(lny_s, LN_RET)
            at(retention, -1)
            at(combine, NT)
            steps(pe, retention, first=0, last=NT - 2)

            xa1 = attention(1, LN_XA1)
            pe.wait_ge(r_xT, NT)
            pe.wait_ge(r_qk, NT)
            pe.wait_ge(r_v, NT)
            at(xa1, -2)
            at(retention, NT - 1)
            at(xa1, -1)
            at(retention, NT)
            pe.wait_ge(r_ve, NT)
            at(xa1, 0)
            at(xa1, 1)
            pe.wait_ge(a_po, NT + 2)
            pe.wait_ge(f_wp, 13)
            for c in range(FC):
                ins = MM(bank[0:R, 6, P * c:P * c + P], bfc[:, c, :], I, start=True, stop=True)
            ins.then_inc(f_wt, 1)
            MM(bank[0:R, 7, 0:D], bpj, I, start=True, stop=True).then_inc(f_wt, 1)
            pe.wait_ge(f_wc, 2)
            for c in range(FC):
                MM(bank[:, 6, P * c:P * c + P], wf1[:, c, :], I, start=True, stop=False)
                ins = MM(bank[:, 6, P * c:P * c + P], afc[0:R, :], bT[0:R, P * c:P * c + P], start=False, stop=True)
            ins.then_inc(f_wt, 1)
            for c in range(FC):
                MM(bank[:, 7, P * c:P * c + P], wf2[:, P * c:P * c + P], I, start=True, stop=False)
                ins = MM(bank[:, 7, P * c:P * c + P], apj[0:R, P * c:P * c + P], bT[0:R, FF:FF + D], start=False, stop=True)
            ins.then_inc(f_wt, 1)
            pe.wait_ge(f_wc, 4)
            steps(pe, xa1, first=2, last=NT - 2)

            def up(g, par):
                pe.wait_ge(f_xs, 2 * g + 1)
                if not (num(g) and g == 0):
                    pe.wait_ge(f_xT, g)
                for j in range(GT):
                    ins = pe.transpose(bank[:, 0, P * j:P * j + P], fs4[:, par, j, :], I)
                ins.then_inc(f_tr, 1)
                pe.wait_ge(f_xT, g + 1)
                for c in range(FC):
                    if not (num(g) and g == 0):
                        pe.wait_ge(f_g, 4 * (g - 1) + c + 1)
                    MM(bank[:, 2 + c, :], w1T[:, P * c:P * c + P], fxT[:, par, :], start=True, stop=True).then_inc(f_h, 1)

            def down(g, par):
                pe.wait_ge(f_g, 4 * g + 4)
                if not (num(g) and g < 2):
                    pe.wait_ge(lny_s, LN_FFN + g - 1)
                for j in range(GT):
                    for c in range(FC):
                        ins = MM(bank[:, 6 + par, P * j:P * j + P], hT[:, par, c, P * j:P * j + P], w2T[:, c, :], start=(c == 0), stop=(c == FC - 1))
                ins.then_inc(f_o, 1)
            pe.wait_ge(a_qk, 2 * NT)
            pe.wait_ge(a_v, 2 * NT)
            pe.wait_ge(a_sub, 4 * NT)
            up(0, 0)
            at(xa1, NT - 1)
            up(1, 1)
            at(xa1, NT)
            pe.wait_ge(a_ptc, 8 * NT)
            for g in range(G):
                down(g, g % 2)
                if g + 2 < G:
                    up(g + 2, g % 2)


def shape_constants():
    p = np.arange(P)
    gamma = 1.0 - 2.0 ** (-5.0 - np.arange(NH, dtype=np.float64))
    diff = p[None, :] - p[:, None]
    decay = np.where(diff[:, None, :] >= 0, gamma[None, :, None] ** np.maximum(diff, 0)[:, None, :], 0.0)
    part = p[:, None]
    return {
        "c_ident": np.eye(P, dtype=np.float32),
        "c_hmask": (part // HD == np.arange(NH)[None, :]).astype(np.float32),
        "c_selcol": ((part >= 32) & (part % 32 == np.arange(NS)[None, :])).astype(np.float32),
        "c_sel9": ((p % 32 < HD + 1)[:, None] & ((HD + 1) * (p // 32) + p % 32)[:, None].__eq__(np.arange(4 * (HD + 1))[None, :])).astype(np.float32),
        "c_sel8": ((p % 32 < HD)[:, None] & (HD * (p // 32) + p % 32)[:, None].__eq__(np.arange(4 * HD)[None, :])).astype(np.float32),
        "c_sel4": (np.arange(P)[None, :] // PS == np.arange(4)[:, None]).astype(np.float32),
        "c_decay": decay.astype(np.float32),
    }


def kernel(**inputs):
    import numpy as _np
    import concourse.bacc as _bacc
    from concourse import mybir as _mybir
    from concourse.bass_utils import run_bass_kernel_spmd as _run

    nc = _bacc.Bacc("TRN2", target_bir_lowering=False, num_devices=1)
    arrays, aps = {}, {}
    for name, value in {**inputs, **shape_constants()}.items():
        v = _np.ascontiguousarray(value)
        arrays[f"in_{name}"] = v
        aps[name] = nc.dram_tensor(f"in_{name}", v.shape, _mybir.dt.from_np(v.dtype), kind="ExternalInput").ap()
    out = nc.dram_tensor("out_0", (NT, P, D), F32, kind="ExternalOutput").ap()
    build(nc, aps, out)
    r = _run(nc, [arrays], core_ids=[0])
    return r.results[0]["out_0"]
```
